# Optimizing a Trainium2 kernel written in Bass

```python
import numpy as np
import jax
import jax.numpy as jnp

def _softmax(x, axis=-1):
    return jax.nn.softmax(x, axis=axis)

def _gelu(x):
    return jax.nn.gelu(x, approximate=True)

def _silu(x):
    return jax.nn.silu(x)

def _sigmoid(x):
    return jax.nn.sigmoid(x)

def _layernorm(x, axis=-1, eps=1e-05):
    m = jnp.mean(x, axis=axis, keepdims=True)
    v = jnp.var(x, axis=axis, keepdims=True)
    return (x - m) / jnp.sqrt(v + eps)

def _scatter_add(tgt, idx, src, axis=0):
    return tgt.at[idx].add(src)

def _segment_sum(src, seg, n):
    return jax.ops.segment_sum(src, seg, n)
kernel_name = 'mk_conv_attn_hybrid_d2_conv_nhwc512_r4_d98976'

def setup_inputs(seed: int=0):
    np.random.seed(seed)
    _w = jnp.asarray

    def _rec_inputs():
        import jax
        import jax.numpy as jnp
        _gk = jax.random.key(seed)
        x = -0.000125 + 0.9999 * jax.random.normal(jax.random.fold_in(_gk, 1), (16, 32, 32, 128), jnp.float32)
        return x
    x = _rec_inputs()

    def _L0_conv_setup():
        import math
        import jax, jax.numpy as jnp
        import numpy as np
        WS = 8
        SS = 4
        NH = 16
        DIM = 128
        H = 32
        W = 32
        N = WS * WS
        LOGIT_MAX = math.log(100.0)

        def _make_consts():
            r = np.arange(-(WS - 1), WS, dtype=np.float32)
            table = np.stack(np.meshgrid(r, r, indexing='ij'), axis=-1)
            table = table / (WS - 1) * 8.0
            table = np.sign(table) * np.log2(np.abs(table) + 1.0) / np.log2(8.0)
            rel_table = table.reshape(-1, 2)
            coords = np.stack(np.meshgrid(np.arange(WS), np.arange(WS), indexing='ij')).reshape(2, -1)
            rel = (coords[:, :, None] - coords[:, None, :]).transpose(1, 2, 0)
            rel[..., 0] += WS - 1
            rel[..., 1] += WS - 1
            rel[..., 0] *= 2 * WS - 1
            rel_idx = rel.sum(-1).reshape(-1).astype(np.int32)
            img_mask = np.zeros((H, W), dtype=np.float32)
            cnt = 0
            for hs in (slice(0, -WS), slice(-WS, -SS), slice(-SS, None)):
                for ws_ in (slice(0, -WS), slice(-WS, -SS), slice(-SS, None)):
                    img_mask[hs, ws_] = cnt
                    cnt += 1
            mw = img_mask.reshape(H // WS, WS, W // WS, WS).transpose(0, 2, 1, 3).reshape(-1, N)
            am = mw[:, None, :] - mw[:, :, None]
            attn_mask = np.where(am != 0, -100.0, 0.0).astype(np.float32)
            return (jnp.asarray(rel_table), jnp.asarray(rel_idx), jnp.asarray(attn_mask))
        REL_TABLE, REL_IDX, ATTN_MASK = _make_consts()

        def _ln(x, g, b, eps=1e-05):
            mu = x.mean(-1, keepdims=True)
            var = ((x - mu) ** 2).mean(-1, keepdims=True)
            return (x - mu) * jax.lax.rsqrt(var + eps) * g + b

        def _l2n(x):
            return x / jnp.maximum(jnp.linalg.norm(x, axis=-1, keepdims=True), 1e-12)

        def _forward(x, qkv_w, q_bias, v_bias, logit_scale, cpb_w1, cpb_b1, cpb_w2, proj_w, proj_b, norm1_g, norm1_b, fc1_w, fc1_b, fc2_w, fc2_b, norm2_g, norm2_b):
            B, H_, W_, C = x.shape
            hd = C // NH
            shifted = jnp.roll(x, (-SS, -SS), axis=(1, 2))
            win = shifted.reshape(B, H_ // WS, WS, W_ // WS, WS, C).transpose(0, 1, 3, 2, 4, 5).reshape(-1, N, C)
            qkv_bias = jnp.concatenate([q_bias, jnp.zeros_like(q_bias), v_bias])
            qkv = (win @ qkv_w.T + qkv_bias).reshape(-1, N, 3, NH, hd).transpose(2, 0, 3, 1, 4)
            q, k, v = (qkv[0], qkv[1], qkv[2])
            scale = jnp.exp(jnp.minimum(logit_scale, LOGIT_MAX)).reshape(1, NH, 1, 1)
            attn = jnp.einsum('bhnd,bhmd->bhnm', _l2n(q), _l2n(k)) * scale
            tbl = jax.nn.relu(REL_TABLE @ cpb_w1.T + cpb_b1) @ cpb_w2.T
            rpb = 16.0 * jax.nn.sigmoid(tbl[REL_IDX].reshape(N, N, NH).transpose(2, 0, 1))
            attn = attn + rpb[None]
            nW = ATTN_MASK.shape[0]
            attn = attn.reshape(-1, nW, NH, N, N) + ATTN_MASK[None, :, None]
            attn = jax.nn.softmax(attn.reshape(-1, NH, N, N), axis=-1)
            out = jnp.einsum('bhnm,bhmd->bhnd', attn, v).transpose(0, 2, 1, 3).reshape(-1, N, C)
            out = out @ proj_w.T + proj_b
            out = out.reshape(B, H_ // WS, W_ // WS, WS, WS, C).transpose(0, 1, 3, 2, 4, 5).reshape(B, H_, W_, C)
            out = jnp.roll(out, (SS, SS), axis=(1, 2))
            x = x + _ln(out, norm1_g, norm1_b)
            h = jax.nn.gelu(x @ fc1_w.T + fc1_b, approximate=False)
            m = h @ fc2_w.T + fc2_b
            return x + _ln(m, norm2_g, norm2_b)
        key = jax.random.key(seed)
        ks = jax.random.split(key, 8)
        B = 16
        s = lambda i, shape, sc=0.02: jax.random.normal(ks[i], shape, jnp.float32) * sc
        return {'x': jax.random.normal(ks[0], (B, H, W, DIM), jnp.float32), 'qkv_w': s(1, (3 * DIM, DIM)), 'q_bias': jnp.zeros((DIM,), jnp.float32), 'v_bias': jnp.zeros((DIM,), jnp.float32), 'logit_scale': jnp.full((NH, 1, 1), math.log(10.0), jnp.float32), 'cpb_w1': s(2, (128, 2), 0.1), 'cpb_b1': jnp.zeros((128,), jnp.float32), 'cpb_w2': s(3, (NH, 128), 0.1), 'proj_w': s(4, (DIM, DIM)), 'proj_b': jnp.zeros((DIM,), jnp.float32), 'norm1_g': jnp.ones((DIM,), jnp.float32), 'norm1_b': jnp.zeros((DIM,), jnp.float32), 'fc1_w': s(5, (4 * DIM, DIM)), 'fc1_b': jnp.zeros((4 * DIM,), jnp.float32), 'fc2_w': s(6, (DIM, 4 * DIM)), 'fc2_b': jnp.zeros((DIM,), jnp.float32), 'norm2_g': jnp.ones((DIM,), jnp.float32), 'norm2_b': jnp.zeros((DIM,), jnp.float32)}
    _L0_conv_all = _L0_conv_setup()
    _L0_conv_in = {k: v for k, v in _L0_conv_all.items() if k in ('qkv_w', 'q_bias', 'v_bias', 'logit_scale', 'cpb_w1', 'cpb_b1', 'cpb_w2', 'proj_w', 'proj_b', 'norm1_g', 'norm1_b', 'fc1_w', 'fc1_b', 'fc2_w', 'fc2_b', 'norm2_g', 'norm2_b')}
    del _L0_conv_all

    def _L1_attn_setup():
        import jax, jax.numpy as jnp
        import numpy as np
        HEADS = 8
        DIM_HEAD = 16
        LANDMARKS = 64
        PINV_ITERS = 6
        SCALE = DIM_HEAD ** (-0.5)
        KSIZE = 33

        def _pinv(x, iters=PINV_ITERS):
            abs_x = jnp.abs(x)
            scale = abs_x.sum(-1).max() * abs_x.sum(-2).max()
            z = jnp.swapaxes(x, -1, -2) / scale
            I = jnp.eye(x.shape[-1], dtype=x.dtype)
            for _ in range(iters):
                xz = x @ z
                z = 0.25 * z @ (13.0 * I - xz @ (15.0 * I - xz @ (7.0 * I - xz)))
            return z
        key = jax.random.key(seed)
        ks = jax.random.split(key, 5)
        b, n, dim = (2, 2048, 128)
        inner = HEADS * DIM_HEAD
        inputs = jax.random.normal(ks[0], (b, n, dim), jnp.float32)
        Wqkv = jax.random.normal(ks[1], (dim, 3 * inner), jnp.float32) * 0.02
        Wout = jax.random.normal(ks[2], (inner, dim), jnp.float32) * 0.02
        bout = jnp.zeros((dim,), jnp.float32)
        conv_w = jax.random.normal(ks[3], (KSIZE, 1, DIM_HEAD // HEADS, DIM_HEAD), jnp.float32) * 0.02
        return {'inputs': inputs, 'Wqkv': Wqkv, 'Wout': Wout, 'bout': bout, 'conv_w': conv_w}
    _L1_attn_all = _L1_attn_setup()
    _L1_attn_in = {k: v for k, v in _L1_attn_all.items() if k in ('Wqkv', 'Wout', 'bout', 'conv_w')}
    del _L1_attn_all

    def _L1_ffn_setup():
        import jax, jax.numpy as jnp
        import numpy as np
        B, S, D, F, E, NS, K = (2, 512, 128, 512, 8, 2, 2)
        key = jax.random.key(seed)
        ks = jax.random.split(key, 6)
        scale = 0.02

        def p(k, shape):
            return jax.random.normal(k, shape, jnp.float32) * scale
        return {'x': jax.random.normal(ks[0], (B, S, D), jnp.float32), 'gate_w': p(ks[1], (E, D)), 'gate_b': jnp.zeros((E,), jnp.float32), 'sw1': p(ks[2], (NS, F, D)), 'sb1': jnp.zeros((NS, F), jnp.float32), 'sw2': p(ks[3], (NS, D, F)), 'sb2': jnp.zeros((NS, D), jnp.float32), 'rw1': p(ks[4], (E, F, D)), 'rb1': jnp.zeros((E, F), jnp.float32), 'rw2': p(ks[5], (E, D, F)), 'rb2': jnp.zeros((E, D), jnp.float32)}
    _L1_ffn_all = _L1_ffn_setup()
    _L1_ffn_in = {k: v for k, v in _L1_ffn_all.items() if k in ('gate_w', 'gate_b', 'sw1', 'sb1', 'sw2', 'sb2', 'rw1', 'rb1', 'rw2', 'rb2')}
    del _L1_ffn_all
    return {'x': x, 'L0_conv_qkv_w': _L0_conv_in['qkv_w'], 'L0_conv_q_bias': _L0_conv_in['q_bias'], 'L0_conv_v_bias': _L0_conv_in['v_bias'], 'L0_conv_logit_scale': _L0_conv_in['logit_scale'], 'L0_conv_cpb_w1': _L0_conv_in['cpb_w1'], 'L0_conv_cpb_b1': _L0_conv_in['cpb_b1'], 'L0_conv_cpb_w2': _L0_conv_in['cpb_w2'], 'L0_conv_proj_w': _L0_conv_in['proj_w'], 'L0_conv_proj_b': _L0_conv_in['proj_b'], 'L0_conv_norm1_g': _L0_conv_in['norm1_g'], 'L0_conv_norm1_b': _L0_conv_in['norm1_b'], 'L0_conv_fc1_w': _L0_conv_in['fc1_w'], 'L0_conv_fc1_b': _L0_conv_in['fc1_b'], 'L0_conv_fc2_w': _L0_conv_in['fc2_w'], 'L0_conv_fc2_b': _L0_conv_in['fc2_b'], 'L0_conv_norm2_g': _L0_conv_in['norm2_g'], 'L0_conv_norm2_b': _L0_conv_in['norm2_b'], 'L1_attn_Wqkv': _L1_attn_in['Wqkv'], 'L1_attn_Wout': _L1_attn_in['Wout'], 'L1_attn_bout': _L1_attn_in['bout'], 'L1_attn_conv_w': _L1_attn_in['conv_w'], 'L1_ffn_gate_w': _L1_ffn_in['gate_w'], 'L1_ffn_gate_b': _L1_ffn_in['gate_b'], 'L1_ffn_sw1': _L1_ffn_in['sw1'], 'L1_ffn_sb1': _L1_ffn_in['sb1'], 'L1_ffn_sw2': _L1_ffn_in['sw2'], 'L1_ffn_sb2': _L1_ffn_in['sb2'], 'L1_ffn_rw1': _L1_ffn_in['rw1'], 'L1_ffn_rb1': _L1_ffn_in['rb1'], 'L1_ffn_rw2': _L1_ffn_in['rw2'], 'L1_ffn_rb2': _L1_ffn_in['rb2']}

def reference(x, L0_conv_qkv_w, L0_conv_q_bias, L0_conv_v_bias, L0_conv_logit_scale, L0_conv_cpb_w1, L0_conv_cpb_b1, L0_conv_cpb_w2, L0_conv_proj_w, L0_conv_proj_b, L0_conv_norm1_g, L0_conv_norm1_b, L0_conv_fc1_w, L0_conv_fc1_b, L0_conv_fc2_w, L0_conv_fc2_b, L0_conv_norm2_g, L0_conv_norm2_b, L1_attn_Wqkv, L1_attn_Wout, L1_attn_bout, L1_attn_conv_w, L1_ffn_gate_w, L1_ffn_gate_b, L1_ffn_sw1, L1_ffn_sb1, L1_ffn_sw2, L1_ffn_sb2, L1_ffn_rw1, L1_ffn_rb1, L1_ffn_rw2, L1_ffn_rb2):
    import jax
    import jax.numpy as jnp

    def _L0_conv_ref(x, qkv_w, q_bias, v_bias, logit_scale, cpb_w1, cpb_b1, cpb_w2, proj_w, proj_b, norm1_g, norm1_b, fc1_w, fc1_b, fc2_w, fc2_b, norm2_g, norm2_b):
        import math
        import jax, jax.numpy as jnp
        import numpy as np
        WS = 8
        SS = 4
        NH = 16
        DIM = 128
        H = 32
        W = 32
        N = WS * WS
        LOGIT_MAX = math.log(100.0)

        def _make_consts():
            r = np.arange(-(WS - 1), WS, dtype=np.float32)
            table = np.stack(np.meshgrid(r, r, indexing='ij'), axis=-1)
            table = table / (WS - 1) * 8.0
            table = np.sign(table) * np.log2(np.abs(table) + 1.0) / np.log2(8.0)
            rel_table = table.reshape(-1, 2)
            coords = np.stack(np.meshgrid(np.arange(WS), np.arange(WS), indexing='ij')).reshape(2, -1)
            rel = (coords[:, :, None] - coords[:, None, :]).transpose(1, 2, 0)
            rel[..., 0] += WS - 1
            rel[..., 1] += WS - 1
            rel[..., 0] *= 2 * WS - 1
            rel_idx = rel.sum(-1).reshape(-1).astype(np.int32)
            img_mask = np.zeros((H, W), dtype=np.float32)
            cnt = 0
            for hs in (slice(0, -WS), slice(-WS, -SS), slice(-SS, None)):
                for ws_ in (slice(0, -WS), slice(-WS, -SS), slice(-SS, None)):
                    img_mask[hs, ws_] = cnt
                    cnt += 1
            mw = img_mask.reshape(H // WS, WS, W // WS, WS).transpose(0, 2, 1, 3).reshape(-1, N)
            am = mw[:, None, :] - mw[:, :, None]
            attn_mask = np.where(am != 0, -100.0, 0.0).astype(np.float32)
            return (jnp.asarray(rel_table), jnp.asarray(rel_idx), jnp.asarray(attn_mask))
        REL_TABLE, REL_IDX, ATTN_MASK = _make_consts()

        def _ln(x, g, b, eps=1e-05):
            mu = x.mean(-1, keepdims=True)
            var = ((x - mu) ** 2).mean(-1, keepdims=True)
            return (x - mu) * jax.lax.rsqrt(var + eps) * g + b

        def _l2n(x):
            return x / jnp.maximum(jnp.linalg.norm(x, axis=-1, keepdims=True), 1e-12)

        def _forward(x, qkv_w, q_bias, v_bias, logit_scale, cpb_w1, cpb_b1, cpb_w2, proj_w, proj_b, norm1_g, norm1_b, fc1_w, fc1_b, fc2_w, fc2_b, norm2_g, norm2_b):
            B, H_, W_, C = x.shape
            hd = C // NH
            shifted = jnp.roll(x, (-SS, -SS), axis=(1, 2))
            win = shifted.reshape(B, H_ // WS, WS, W_ // WS, WS, C).transpose(0, 1, 3, 2, 4, 5).reshape(-1, N, C)
            qkv_bias = jnp.concatenate([q_bias, jnp.zeros_like(q_bias), v_bias])
            qkv = (win @ qkv_w.T + qkv_bias).reshape(-1, N, 3, NH, hd).transpose(2, 0, 3, 1, 4)
            q, k, v = (qkv[0], qkv[1], qkv[2])
            scale = jnp.exp(jnp.minimum(logit_scale, LOGIT_MAX)).reshape(1, NH, 1, 1)
            attn = jnp.einsum('bhnd,bhmd->bhnm', _l2n(q), _l2n(k)) * scale
            tbl = jax.nn.relu(REL_TABLE @ cpb_w1.T + cpb_b1) @ cpb_w2.T
            rpb = 16.0 * jax.nn.sigmoid(tbl[REL_IDX].reshape(N, N, NH).transpose(2, 0, 1))
            attn = attn + rpb[None]
            nW = ATTN_MASK.shape[0]
            attn = attn.reshape(-1, nW, NH, N, N) + ATTN_MASK[None, :, None]
            attn = jax.nn.softmax(attn.reshape(-1, NH, N, N), axis=-1)
            out = jnp.einsum('bhnm,bhmd->bhnd', attn, v).transpose(0, 2, 1, 3).reshape(-1, N, C)
            out = out @ proj_w.T + proj_b
            out = out.reshape(B, H_ // WS, W_ // WS, WS, WS, C).transpose(0, 1, 3, 2, 4, 5).reshape(B, H_, W_, C)
            out = jnp.roll(out, (SS, SS), axis=(1, 2))
            x = x + _ln(out, norm1_g, norm1_b)
            h = jax.nn.gelu(x @ fc1_w.T + fc1_b, approximate=False)
            m = h @ fc2_w.T + fc2_b
            return x + _ln(m, norm2_g, norm2_b)
        return _forward(x, qkv_w, q_bias, v_bias, logit_scale, cpb_w1, cpb_b1, cpb_w2, proj_w, proj_b, norm1_g, norm1_b, fc1_w, fc1_b, fc2_w, fc2_b, norm2_g, norm2_b)

    def _L1_attn_ref(inputs, Wqkv, Wout, bout, conv_w):
        import jax, jax.numpy as jnp
        import numpy as np
        HEADS = 8
        DIM_HEAD = 16
        LANDMARKS = 64
        PINV_ITERS = 6
        SCALE = DIM_HEAD ** (-0.5)
        KSIZE = 33

        def _pinv(x, iters=PINV_ITERS):
            abs_x = jnp.abs(x)
            scale = abs_x.sum(-1).max() * abs_x.sum(-2).max()
            z = jnp.swapaxes(x, -1, -2) / scale
            I = jnp.eye(x.shape[-1], dtype=x.dtype)
            for _ in range(iters):
                xz = x @ z
                z = 0.25 * z @ (13.0 * I - xz @ (15.0 * I - xz @ (7.0 * I - xz)))
            return z
        b, n, dim = inputs.shape
        h, m, d = (HEADS, LANDMARKS, DIM_HEAD)
        qkv = inputs @ Wqkv
        q, k, v = jnp.split(qkv, 3, axis=-1)
        to_heads = lambda t: jnp.transpose(t.reshape(b, n, h, d), (0, 2, 1, 3))
        q, k, v = map(to_heads, (q, k, v))
        q = q * SCALE
        seg = n // m
        q_l = q.reshape(b, h, m, seg, d).mean(axis=3)
        k_l = k.reshape(b, h, m, seg, d).mean(axis=3)
        attn1 = jax.nn.softmax(jnp.einsum('bhnd,bhmd->bhnm', q, k_l), axis=-1)
        attn2 = jax.nn.softmax(jnp.einsum('bhid,bhjd->bhij', q_l, k_l), axis=-1)
        attn3 = jax.nn.softmax(jnp.einsum('bhmd,bhnd->bhmn', q_l, k), axis=-1)
        attn2_inv = _pinv(attn2)
        out = attn1 @ (attn2_inv @ (attn3 @ v))
        res = jax.lax.conv_general_dilated(v, conv_w, window_strides=(1, 1), padding='SAME', dimension_numbers=('NHWC', 'HWIO', 'NHWC'), feature_group_count=HEADS)
        out = out + res
        out = jnp.transpose(out, (0, 2, 1, 3)).reshape(b, n, h * d)
        return out @ Wout + bout

    def _L1_ffn_ref(x, gate_w, gate_b, sw1, sb1, sw2, sb2, rw1, rb1, rw2, rb2):
        import jax, jax.numpy as jnp
        import numpy as np
        B, S, D, F, E, NS, K = (2, 512, 128, 512, 8, 2, 2)
        b, s, d = x.shape
        t = x.reshape(-1, d)
        T = t.shape[0]
        hs = jax.nn.gelu(jnp.einsum('td,nfd->ntf', t, sw1) + sb1[:, None, :], approximate=False)
        shared = jnp.einsum('ntf,ndf->td', hs, sw2) + sb2.sum(axis=0)
        logits = t @ gate_w.T + gate_b
        probs = jax.nn.softmax(logits, axis=-1)
        top_v, top_i = jax.lax.top_k(probs, K)
        cw = jnp.zeros_like(probs).at[jnp.arange(T)[:, None], top_i].add(top_v)
        hr = jax.nn.gelu(jnp.einsum('td,efd->etf', t, rw1) + rb1[:, None, :], approximate=False)
        oe = jnp.einsum('etf,edf->etd', hr, rw2) + rb2[:, None, :]
        routed = jnp.einsum('etd,te->td', oe, cw)
        return (shared + routed).reshape(b, s, d)

    def _gn(v, G=32, eps=1e-05):
        B_, H_, W_, C_ = v.shape
        g = v.reshape(B_, H_, W_, G, C_ // G)
        m = jnp.mean(g, axis=(1, 2, 4), keepdims=True)
        s = jnp.var(g, axis=(1, 2, 4), keepdims=True)
        return ((g - m) / jnp.sqrt(s + eps)).reshape(v.shape)

    def _ln_c(v, eps=1e-06):
        m = jnp.mean(v, axis=-1, keepdims=True)
        s = jnp.var(v, axis=-1, keepdims=True)
        return (v - m) / jnp.sqrt(s + eps)

    def _ln_t(v, eps=1e-05):
        m = jnp.mean(v, axis=-1, keepdims=True)
        s = jnp.var(v, axis=-1, keepdims=True)
        return (v - m) / jnp.sqrt(s + eps)

    def _to_tokens(v):
        B_, H_, W_, C_ = v.shape
        return v.reshape(B_, H_ * W_, C_)

    def _from_tokens(t, like):
        return t.reshape(like.shape)
    x = _L0_conv_ref(x, L0_conv_qkv_w, L0_conv_q_bias, L0_conv_v_bias, L0_conv_logit_scale, L0_conv_cpb_w1, L0_conv_cpb_b1, L0_conv_cpb_w2, L0_conv_proj_w, L0_conv_proj_b, L0_conv_norm1_g, L0_conv_norm1_b, L0_conv_fc1_w, L0_conv_fc1_b, L0_conv_fc2_w, L0_conv_fc2_b, L0_conv_norm2_g, L0_conv_norm2_b)
    t = _to_tokens(x)
    t = t + _L1_attn_ref(_ln_t(t), L1_attn_Wqkv, L1_attn_Wout, L1_attn_bout, L1_attn_conv_w)
    t = t + _L1_ffn_ref(_ln_t(t), L1_ffn_gate_w, L1_ffn_gate_b, L1_ffn_sw1, L1_ffn_sb1, L1_ffn_sw2, L1_ffn_sb2, L1_ffn_rw1, L1_ffn_rb1, L1_ffn_rw2, L1_ffn_rb2)
    x = _from_tokens(t, x)
    return x

_drawn_inputs = setup_inputs


def setup_inputs(seed=0):
    import zlib

    import numpy as np

    out = dict(_drawn_inputs(seed))
    spreads = {'L0_conv_q_bias': (0.0, 0.1),
     'L0_conv_v_bias': (0.0, 0.1),
     'L0_conv_logit_scale': (2.3025851249694824, 0.2),
     'L0_conv_cpb_b1': (0.0, 0.8),
     'L0_conv_proj_b': (0.0, 0.1),
     'L0_conv_norm1_g': (1.0, 0.2),
     'L0_conv_norm1_b': (0.0, 0.1),
     'L0_conv_fc1_b': (0.0, 0.1),
     'L0_conv_fc2_b': (0.0, 0.1),
     'L0_conv_norm2_g': (1.0, 0.2),
     'L0_conv_norm2_b': (0.0, 0.1),
     'L1_attn_bout': (0.0, 0.1),
     'L1_ffn_gate_b': (0.0, 0.8),
     'L1_ffn_sb1': (0.0, 0.454),
     'L1_ffn_sb2': (0.0, 0.1),
     'L1_ffn_rb1': (0.0, 0.8),
     'L1_ffn_rb2': (0.0, 0.628)}
    factors = {'L0_conv_cpb_w1': 3.072,
     'L0_conv_cpb_w2': 3.707,
     'L1_attn_Wout': 2.807,
     'L1_attn_conv_w': 8.0,
     'L1_ffn_gate_w': 4.417,
     'L1_ffn_rw1': 7.644,
     'L1_ffn_rw2': 6.827}
    for name, (base, spread) in spreads.items():
        noise = np.random.default_rng([zlib.crc32(name.encode()), seed]).standard_normal(out[name].shape)
        drawn = base * np.exp(spread * noise) if base else spread * noise
        out[name] = jnp.asarray(drawn.astype(out[name].dtype))
    for name, factor in factors.items():
        out[name] = (out[name] * factor).astype(out[name].dtype)
    return out
```

```python
from contextlib import ExitStack
import math

import numpy as np

import concourse.bass as bass
from concourse import mybir

F32 = mybir.dt.float32
F16 = mybir.dt.float16
ALU = mybir.AluOpType
ACT = mybir.ActivationFunctionType
X = mybir.AxisListType.X

C = 128
P = 128
HW = 32
WS, SS = 8, 4
N = WS * WS
T = HW * HW
NP = T // P
NH, HD = 16, 8
AH, AD = 8, 16
LM = 64
SEG = T // LM
F = 512
NE = 8
NX = 10
FC = F // P
WSCALE = 64.0
ITERS = 6
LOADED = 16 * 34


class Signal:

    def __init__(self, sem, per, by=1):
        self.sem, self.per, self.by = sem, per, by

    def at(self, turn, n):
        return turn * (self.per * self.by) + n * self.by


def window_constants():
    r = np.arange(-(WS - 1), WS, dtype=np.float32)
    tab = np.stack(np.meshgrid(r, r, indexing="ij"), axis=-1) / (WS - 1) * 8.0
    tab = (np.sign(tab) * np.log2(np.abs(tab) + 1.0) / np.log2(8.0)).astype(np.float32)
    rel = np.ascontiguousarray(tab.reshape(-1, 2).T)
    ch, rr, cc = np.meshgrid(np.arange(2), np.arange(WS), np.arange(4), indexing="ij")
    y, x = rr.reshape(-1), (4 * ch + cc).reshape(-1)
    img = np.zeros((HW, HW), np.float32)
    cnt = 0
    for hs in (slice(0, -WS), slice(-WS, -SS), slice(-SS, None)):
        for ws in (slice(0, -WS), slice(-WS, -SS), slice(-SS, None)):
            img[hs, ws] = cnt
            cnt += 1
    mask = np.zeros((P, 4, N), np.float32)
    for kind in range(4):
        wy, half = (3 if kind >= 2 else 0), kind % 2
        for w in range(2):
            m = img[8 * wy + y, 8 * (2 * half + w) + x]
            mask[64 * w:64 * w + 64, kind] = np.where(m[None, :] != m[:, None], -100.0, 0.0)
    sel = np.zeros((NH, NH, N), np.float16)
    for i in range(NH):
        sel[i, i] = 1.0
    return rel, mask, sel.reshape(NH, NH * N), y, x


def build(nc, NB, A, out):
    _, _, _, KY, KX = window_constants()
    with ExitStack() as ctx:
        def sb(name, shape, dt=F32):
            return ctx.enter_context(nc.sbuf_tensor(name, shape, dt))

        def sem(name):
            return ctx.enter_context(nc.semaphore(name))

        def signal(name, per, by=1):
            return Signal(sem(name), per, by)

        mid = nc.dram_tensor("mid_dram", [NB, T, C], F32).ap()
        res = nc.dram_tensor("res_dram", [NB, T, C], F32).ap()
        psum = ctx.enter_context(nc.psum_tensor("psum", [P, 8 * 512], F32))

        def apart(eng):
            eng.sem_inc(s_apart, 1)

        def banks(i, n):
            return psum[:, 512 * i:512 * (i + n)]

        def bank(i):
            return banks(i, 1)

        ident = sb("ident", [P, P])
        ident16 = sb("ident16", [P, P], F16)
        w1hi = sb("w1hi", [P, NX, F], F16)
        w1lo = sb("w1lo", [P, NX, F], F16)
        w2hi = sb("w2hi", [P, NX, FC, C], F16)
        w2lo = sb("w2lo", [P, NX, FC, C], F16)
        b1 = sb("b1", [P, NX, FC])
        cw = sb("cw", [P, NB, NP * NE])
        wqkv2 = sb("wqkv2", [P, 3 * C])
        wvc = sb("wvc", [P, C])
        wout = sb("wout", [P, C])
        bout = sb("bout", [P, C])
        gw = sb("gw", [P, NE])
        gb = sb("gb", [P, NE])
        b2r = sb("b2r", [NE, C])
        b2s = sb("b2s", [P, 2, C])
        headmask = sb("headmask", [P, AH])
        nhalf = sb("nhalf", [P, NP * 32])
        ones1 = sb("ones1", [1, P])

        s_load = sem("s_load")
        s_apart = sem("s_apart")
        s_set = sem("s_set")
        s_out = sem("s_out")

        def phase_windows():
            with ExitStack() as c1:
                def sb(name, shape, dt=F32):
                    return c1.enter_context(nc.sbuf_tensor(name, shape, dt))

                wqkT = sb("wqkT", [P, 3 * C])
                qb = sb("qb", [P, 2 * C])
                projT = sb("projT", [P, C])
                projb = sb("projb", [P, C])
                vbcol = sb("vbcol", [P, P])
                g1, be1, g2, be2 = (sb(n, [P, C]) for n in ("g1", "be1", "g2", "be2"))
                f1T = sb("f1T", [P, F])
                f1b = sb("f1b", [P, FC])
                f2T = sb("f2T", [P, FC, C])
                f2b = sb("f2b", [P, C])
                sc = sb("sc", [P, NH])
                cpw1 = sb("cpw1", [2, P])
                cpb1 = sb("cpb1", [P, 1])
                cpw2 = sb("cpw2", [P, NH])
                rel = sb("rel", [2, 225])
                relh = sb("relh", [P, 15, 15])
                relx = sb("relx", [P, 12, 15, 4])
                sig = sb("sig", [P, N, NH])
                mask = sb("mask", [P, 4, N])
                sel = sb("sel", [NH, NH * N], F16)
                bth = sb("bth", [P, 4, 4, 4, N], F16)
                btl = sb("btl", [P, 4, 4, 4, N], F16)
                btmp = sb("btmp", [P, 2, 4, N])

                xw = sb("xw", [P, NP, C])
                xT = sb("xT", [P, NP, P])
                qk = sb("qk", [P, NP, 2, NH, HD])
                sq = sb("sq", [P, 2, 2 * C])
                nrm = sb("nrm", [P, NP, 2, NH])
                split = sb("split", [P, 2, 2, NH, 4, HD], F16)
                qkT = sb("qkT", [P, NP, 2, 4, P], F16)
                vd = sb("vd", [P, NP, 2, NH, HD + 1])
                mx = sb("mx", [P, NH])
                mT = sb("mT", [NH, P], F16)
                pr = sb("pr", [P, 16, N])
                prT = sb("prT", [P, 8, P])
                rs = sb("rs", [P, NH])
                on = sb("on", [P, NP, C])
                onT = sb("onT", [P, NP, P])
                y = sb("y", [P, NP, C])
                xg = sb("xg", [P, NP, C])
                st = sb("st", [P, NP, 6])
                mv = sb("mv", [P, NP, 2])
                rstd = sb("rstd", [P, NP])
                x1 = sb("x1", [P, NP, C])
                x1T = sb("x1T", [P, 2, 4 * P])
                gl = sb("gl", [P, FC, 4 * P])

                loads = [(ident, "ident"), (ident16, "ident16"), (wqkv2, "wqkv2"), (wout, "wout"), (bout, "bout"),
                         (gw, "gw"), (gb, "gb"), (b2r, "b2r"), (b2s, "b2s"), (headmask, "headmask"), (b1, "b1"),
                         (wqkT, "wqkT"), (qb, "qb"), (projT, "projT"), (projb, "projb"), (vbcol, "vbcol"),
                         (g1, "g1"), (be1, "be1"), (g2, "g2"), (be2, "be2"), (f1T, "f1T"), (f1b, "f1b"),
                         (f2T, "f2T"), (f2b, "f2b"), (sc, "ls"), (cpw1, "cpw1"), (cpb1, "cpb1"), (cpw2, "cpw2"),
                         (rel, "rel"), (mask, "mask"), (sel, "sel")]
                stage = sb("stage", [P, NX * F])
                cm = xw
                assert LOADED == 16 * (len(loads) + 3)

                s_w = sem("s_w")
                s_wdone = sem("s_wdone")
                s_pe = sem("s_pe")
                s_ac = sem("s_ac")
                s_ve = sem("s_ve")
                s_po = sem("s_po")
                s_rel = sem("s_rel")
                x_in = signal("x_in", 40, 16)
                xT_ps = signal("xT_ps", NP)
                xT_ok = signal("xT_ok", NP)
                qkv_ps = signal("qkv_ps", NP)
                qk_ok = signal("qk_ok", NP)
                v_ok = signal("v_ok", NP * 2)
                sq_ok = signal("sq_ok", NP)
                ss_ok = signal("ss_ok", NP)
                ss_max = signal("ss_max", 1)
                nrm_ok = signal("nrm_ok", 1)
                qsc_ok = signal("qsc_ok", 1)
                qn_ok = signal("qn_ok", NP)
                hi_ok = signal("hi_ok", NP * 2)
                lo_ok = signal("lo_ok", NP * 2)
                qkT_ps = signal("qkT_ps", NP)
                qkT_ok = signal("qkT_ok", NP)
                s_ps = signal("s_ps", NP)
                mx_ok = signal("mx_ok", NP)
                mT_ps = signal("mT_ps", NP)
                mT_ok = signal("mT_ok", NP)
                sm_ps = signal("sm_ps", NP)
                pr_ok = signal("pr_ok", NP)
                prT_ps = signal("prT_ps", NP * 2)
                prT_a = signal("prT_a", NP)
                prT_v = signal("prT_v", NP)
                o_ps = signal("o_ps", NP)
                rs_ok = signal("rs_ok", NP)
                on_ok = signal("on_ok", NP)
                onT_ps = signal("onT_ps", NP)
                onT_ok = signal("onT_ok", NP)
                pj_ps = signal("pj_ps", NP)
                y_ok = signal("y_ok", 2 * NP)
                st_ok = signal("st_ok", 2 * NP)
                mv_ok = signal("mv_ok", 2)
                ve_ok = signal("ve_ok", 2)
                rstd_ok = signal("rstd_ok", 2)
                yn_ok = signal("yn_ok", 2 * NP)
                yg_ok = signal("yg_ok", 2 * NP)
                xb_ok = signal("xb_ok", 2)
                x1_ok = signal("x1_ok", 2 * NP)
                x1T_ps = signal("x1T_ps", 2)
                x1T_ok = signal("x1T_ok", 2)
                h_ps = signal("h_ps", 2 * FC)
                gl_ok = signal("gl_ok", 2 * FC)
                m_ps = signal("m_ps", 2)
                mid_out = signal("mid_out", 40, 16)
                turn_done = sem("turn_done")

                def pieces(b, dram):
                    img = dram[b].rearrange("(y x) c -> y x c", y=HW)
                    for p in range(NP):
                        wy = p // 2
                        for w in range(2):
                            for ch in range(2):
                                x0 = (WS * (2 * (p % 2) + w) + 4 * ch + SS) % HW
                                q0 = 64 * w + 32 * ch
                                if wy < 3:
                                    yield p, q0, 32, img[8 * wy + SS:8 * wy + SS + 8, x0:x0 + 4, :]
                                else:
                                    yield p, q0, 16, img[28:32, x0:x0 + 4, :]
                                    yield p, q0 + 16, 16, img[0:4, x0:x0 + 4, :]

                with nc.Block() as block:
                    @block.sync
                    def _(sp):
                        for dst, name in loads:
                            sp.dma_start(dst[:], A[name]).then_inc(s_load, 16)
                        sp.dma_start(cm[:, 0, :], A["convT"]).then_inc(s_load, 16)
                        sp.dma_start(cm[:, 1, :], A["convmask"]).then_inc(s_load, 16)
                        sp.dma_start(cm[:, 2, :], A["wvT"]).then_inc(s_load, 16)
                        sp.dma_start(stage[:], A["w1"]).then_inc(s_w, 16)
                        sp.wait_ge(s_wdone, 2)
                        sp.dma_start(stage[:], A["w2"]).then_inc(s_w, 16)
                        sp.wait_ge(s_pe, 5)
                        with sp.Fori(0, NB) as b:
                            sp.wait_ge(turn_done, b * 4)
                            apart(sp)
                            for p, q0, n, src in pieces(b, A["x"]):
                                sp.dma_start(xw[q0:q0 + n, p, :], src).then_inc(x_in.sem, 16)
                            k = 0
                            for p, q0, n, dst in pieces(b, mid):
                                if k % 4 == 0 and q0 == 0:
                                    sp.wait_ge(x1_ok.sem, x1_ok.at(b, NP + p + 1))
                                    apart(sp)
                                sp.dma_start(dst, x1[q0:q0 + n, p, :]).then_inc(mid_out.sem, 16)
                            sp.wait_ge(mid_out.sem, mid_out.at(b, 40))
                            apart(sp)

                    @block.gpsimd
                    def _(gp):
                        gp.memset(nhalf[:], -0.5).then_inc(s_po, 1)
                        gp.memset(ones1[:], 1.0).then_inc(s_po, 1)
                        gp.memset(vd[:], 0.0).then_inc(s_po, 1)
                        gp.memset(split[:], 0.0).then_inc(s_po, 1)
                        k = 4
                        for p in range(NP):
                            for w in range(2):
                                v = vd[:, p, w].rearrange("q (t k j) d -> q t k j d", t=2, k=2)
                                for t in range(2):
                                    for half in range(2):
                                        gp.wait_ge(s_po, k)
                                        gp.memset(v[64 * half:64 * half + 64, t, half, :, HD:HD + 1], 1.0)\
                                            .then_inc(s_po, 1)
                                        k += 1
                        gp.wait_ge(s_po, k)
                        gp.wait_ge(s_ac, 2)
                        for i in range(12):
                            gp.tensor_copy(relx[:, i], relh[:, :, i:i + 4]).then_inc(s_rel, 1)
                        gp.wait_ge(s_load, LOADED)
                        with gp.Fori(0, NB) as b:
                            for p in range(NP):
                                gp.wait_ge(qk_ok.sem, qk_ok.at(b, p + 1))
                                if p >= 2:
                                    gp.wait_ge(ss_ok.sem, ss_ok.at(b, p - 1))
                                q2 = qk[:, p].rearrange("q a h d -> q (a h d)")
                                gp.tensor_tensor(sq[:, p % 2, :], q2, q2, ALU.mult).then_inc(sq_ok.sem, 1)
                            gp.wait_ge(ss_max.sem, ss_max.at(b, 1))
                            n2 = nrm[:].rearrange("q p a h -> q (p a h)")
                            gp.tensor_tensor(n2, n2, nhalf[:], ALU.pow).then_inc(nrm_ok.sem, 1)
                            gp.wait_ge(x_in.sem, x_in.at(b, 40))
                            gp.tensor_tensor(xg[:], xw[:], be1[:].unsqueeze(1).to_broadcast([P, NP, C]),
                                             ALU.add).then_inc(xb_ok.sem, 1)
                            for ln in range(2):
                                gp.wait_ge(ve_ok.sem, ve_ok.at(b, ln + 1))
                                gp.tensor_tensor(rstd[:], rstd[:], nhalf[:, 0:NP], ALU.pow).then_inc(rstd_ok.sem, 1)
                                for p in range(NP):
                                    gp.wait_ge(yn_ok.sem, yn_ok.at(b, ln * NP + p + 1))
                                    gp.tensor_tensor(y[:, p, :], y[:, p, :], (g1, g2)[ln][:], ALU.mult)\
                                        .then_inc(yg_ok.sem, 1)
                                if ln == 0:
                                    gp.wait_ge(x1_ok.sem, x1_ok.at(b, NP))
                                    gp.tensor_tensor(xg[:], x1[:], be2[:].unsqueeze(1).to_broadcast([P, NP, C]),
                                                     ALU.add).then_inc(xb_ok.sem, 1)
                            gp.wait_ge(x1_ok.sem, x1_ok.at(b, 2 * NP))
                            gp.sem_inc(turn_done, 1)

                    @block.scalar
                    def _(ac):
                        ac.wait_ge(s_ve, 1)
                        ac.activation(sc[:], sc[:], ACT.Exp).then_inc(s_ac, 1)
                        ac.wait_ge(s_pe, 1)
                        ac.activation(relh[:].rearrange("q a b -> q (a b)"), bank(0)[:, 0:225], ACT.Relu,
                                      bias=cpb1[:, 0:1]).then_inc(s_ac, 1)
                        ac.wait_ge(s_pe, 2)
                        for i in range(2):
                            ac.activation(sig[:, 32 * i:32 * i + 32, :].rearrange("q m h -> q (m h)"), bank(1 + i)[:, :],
                                          ACT.Sigmoid).then_inc(s_ac, 1)
                        ac.wait_ge(s_pe, 5)
                        ac.activation(wvc[:], bank(3)[:, 0:C], ACT.Copy).then_inc(s_ac, 1)
                        ac.wait_ge(s_load, LOADED)
                        ac.wait_ge(s_po, 4 + 4 * 2 * NP)
                        with ac.Fori(0, NB) as b:
                            for p in range(NP):
                                ac.wait_ge(xT_ps.sem, xT_ps.at(b, p + 1))
                                ac.activation(xT[:, p, :], bank(p % 2)[:, 0:P], ACT.Copy).then_inc(xT_ok.sem, 1)
                                ac.wait_ge(qkv_ps.sem, qkv_ps.at(b, p + 1))
                                for k in range(2):
                                    src = bank(4 + p % 2)[64 * k:64 * k + 64, 0:2 * C].rearrange(
                                        "q (w t k j d) -> q w t k (j d)", w=2, t=2, k=2, j=4)
                                    dst = vd[64 * k:64 * k + 64, p].rearrange("q w (t k j) d -> q w t k j d", t=2, k=2)
                                    for w in range(2):
                                        i = ac.activation(dst[:, w, :, k, :, 0:HD],
                                                          src[:, w, :, k, :].rearrange("q t (j d) -> q t j d", j=4),
                                                          ACT.Copy)
                                    i.then_inc(v_ok.sem, 1)
                            for p in range(NP):
                                ac.wait_ge(qn_ok.sem, qn_ok.at(b, p + 1))
                                if p >= 2:
                                    ac.wait_ge(qkT_ps.sem, qkT_ps.at(b, p - 1))
                                for a in range(2):
                                    for s in ((0, 1), (0, 2))[a]:
                                        i = ac.activation(split[:, p % 2, a, :, s, :], qk[:, p, a, :, :], ACT.Copy)
                                    i.then_inc(hi_ok.sem, 1)
                                if p >= 1:
                                    ac.wait_ge(qkT_ps.sem, qkT_ps.at(b, p))
                                    ac.activation(qkT[:, p - 1].rearrange("q a g t -> q (a g t)"),
                                                  bank(6 + (p - 1) % 2)[:].bitcast(F16), ACT.Copy)\
                                        .then_inc(qkT_ok.sem, 1)
                            ac.wait_ge(qkT_ps.sem, qkT_ps.at(b, NP))
                            ac.activation(qkT[:, NP - 1].rearrange("q a g t -> q (a g t)"),
                                          bank(6 + (NP - 1) % 2)[:].bitcast(F16), ACT.Copy).then_inc(qkT_ok.sem, 1)
                            for p in range(NP):
                                ac.wait_ge(mT_ps.sem, mT_ps.at(b, p + 1))
                                ac.activation(mT[:], bank(7)[0:NH, 0:P], ACT.Copy, scale=-1.0).then_inc(mT_ok.sem, 1)
                                ac.wait_ge(sm_ps.sem, sm_ps.at(b, p + 1))
                                if p >= 1:
                                    ac.wait_ge(prT_ps.sem, prT_ps.at(b, 2 * p))
                                for j in range(4):
                                    i = ac.activation(pr[:, 4 * j:4 * j + 4, :].rearrange("q g m -> q (g m)"),
                                                      bank(j)[:, 0:256], ACT.Exp)
                                i.then_inc(pr_ok.sem, 1)
                                ac.wait_ge(prT_ps.sem, prT_ps.at(b, 2 * p + 1))
                                if p >= 1:
                                    ac.wait_ge(o_ps.sem, o_ps.at(b, p))
                                ac.activation(prT[:, 0:4, :].rearrange("q k t -> q (k t)"), bank(4)[:, :], ACT.Copy)\
                                    .then_inc(prT_a.sem, 1)
                            for p in range(NP):
                                ac.wait_ge(onT_ps.sem, onT_ps.at(b, p + 1))
                                ac.activation(onT[:, p, :], bank(p % 2)[:, 0:P], ACT.Copy).then_inc(onT_ok.sem, 1)
                            for u in range(2):
                                ac.wait_ge(x1T_ps.sem, x1T_ps.at(b, u + 1))
                                ac.activation(x1T[:, u, :], bank(4 + u)[:, :], ACT.Copy).then_inc(x1T_ok.sem, 1)
                                for f in range(FC):
                                    ac.wait_ge(h_ps.sem, h_ps.at(b, u * FC + f + 1))
                                    if u == 1 and f == 0:
                                        ac.wait_ge(m_ps.sem, m_ps.at(b, 1))
                                    ac.activation(gl[:, f, :], bank(f % 2)[:, :], ACT.Gelu, bias=f1b[:, f:f + 1])\
                                        .then_inc(gl_ok.sem, 1)
                            ac.wait_ge(gl_ok.sem, gl_ok.at(b, 2 * FC))
                            ac.sem_inc(turn_done, 1)

                    @block.vector
                    def _(ve):
                        ve.wait_ge(s_load, LOADED)
                        ve.tensor_scalar(sc[:], sc[:], math.log(100.0), None, ALU.min).then_inc(s_ve, 1)
                        ve.tensor_tensor(cm[:, 0, :], cm[:, 0, :], cm[:, 1, :], ALU.mult).then_inc(s_ve, 1)
                        ve.tensor_tensor(b2s[:, 0, :], b2s[:, 0, :], b2s[:, 1, :], ALU.add).then_inc(s_ve, 1)
                        ve.wait_ge(s_pe, 4)
                        ve.tensor_copy(cm[:, 3, :], bank(4)[:, 0:C]).then_inc(s_ve, 1)
                        ve.tensor_tensor(projb[:], projb[:], bank(5)[:, 0:C], ALU.add).then_inc(s_ve, 1)
                        n = 5
                        ve.wait_ge(s_ac, 4)
                        k = 0
                        for kind in range(4):
                            for j in range(4):
                                t = btmp[:, k % 2]
                                src = sig[:].rearrange("q m (g j) -> q g m j", j=4)[:, :, :, j]
                                ve.scalar_tensor_tensor(out=t, in0=src, scalar=16.0,
                                                        in1=mask[:, kind, :].unsqueeze(1).to_broadcast([P, 4, N]),
                                                        op0=ALU.mult, op1=ALU.add).then_inc(s_ve, 1)
                                n += 1
                                ve.wait_ge(s_ve, n)
                                ve.tensor_copy(bth[:, kind, j], t).then_inc(s_ve, 1)
                                n += 1
                                ve.wait_ge(s_ve, n)
                                ve.tensor_tensor(btl[:, kind, j], t, bth[:, kind, j], ALU.subtract).then_inc(s_ve, 1)
                                n += 1
                                k += 1
                                ve.wait_ge(s_ve, n)
                        wd = 0
                        for which, (hi, lo) in enumerate(((w1hi, w1lo), (w2hi, w2lo))):
                            ve.wait_ge(s_w, 16 * which + 16)
                            src = stage[:]
                            hi2 = hi[:].rearrange("p a b -> p (a b)") if not which else hi[:].rearrange("p a b c -> p (a b c)")
                            lo2 = lo[:].rearrange("p a b -> p (a b)") if not which else lo[:].rearrange("p a b c -> p (a b c)")
                            ve.tensor_scalar(hi2, src, WSCALE, None, ALU.mult).then_inc(s_wdone, 1)
                            wd += 1
                            ve.wait_ge(s_wdone, wd)
                            ve.scalar_tensor_tensor(out=lo2, in0=src, scalar=WSCALE, in1=hi2, op0=ALU.mult,
                                                    op1=ALU.subtract).then_inc(s_wdone, 1)
                            wd += 1
                        ve.wait_ge(s_po, 4 + 4 * 2 * NP)
                        with ve.Fori(0, NB) as b:
                            for p in range(NP):
                                ve.wait_ge(qkv_ps.sem, qkv_ps.at(b, p + 1))
                                q2 = qk[:, p].rearrange("q a h d -> q (a h d)")
                                ve.tensor_tensor(q2, bank(2 + p % 2)[:, 0:2 * C], qb[:], ALU.add).then_inc(qk_ok.sem, 1)
                                ve.wait_ge(sq_ok.sem, sq_ok.at(b, p + 1))
                                ve.tensor_reduce(nrm[:, p].rearrange("q a h -> q (a h)"),
                                                 sq[:, p % 2].rearrange("q (h d) -> q h d", d=HD), X, ALU.add)\
                                    .then_inc(ss_ok.sem, 1)
                            ve.wait_ge(ss_ok.sem, ss_ok.at(b, NP))
                            n2 = nrm[:].rearrange("q p a h -> q (p a h)")
                            ve.tensor_scalar(n2, n2, 1e-24, None, ALU.max).then_inc(ss_max.sem, 1)
                            ve.wait_ge(nrm_ok.sem, nrm_ok.at(b, 1))
                            ve.tensor_tensor(nrm[:, :, 0, :], nrm[:, :, 0, :],
                                             sc[:].unsqueeze(1).to_broadcast([P, NP, NH]), ALU.mult)\
                                .then_inc(qsc_ok.sem, 1)
                            ve.wait_ge(qsc_ok.sem, qsc_ok.at(b, 1))

                            def lo_parts(p):
                                ve.wait_ge(hi_ok.sem, hi_ok.at(b, 2 * p + 2))
                                for a in range(2):
                                    ve.tensor_tensor(split[:, p % 2, a, :, 2 - a, :], qk[:, p, a], split[:, p % 2, a, :, 0, :],
                                                     ALU.subtract).then_inc(lo_ok.sem, 1)

                            for p in range(NP):
                                q3 = qk[:, p].rearrange("q a h d -> q (a h) d")
                                ve.tensor_tensor(q3, q3, nrm[:, p].rearrange("q a h -> q (a h)").unsqueeze(2)
                                                 .to_broadcast([P, 2 * NH, HD]), ALU.mult).then_inc(qn_ok.sem, 1)
                                if p >= 1:
                                    lo_parts(p - 1)
                            lo_parts(NP - 1)
                            for p in range(NP):
                                ve.wait_ge(s_ps.sem, s_ps.at(b, p + 1))
                                if p >= 1:
                                    ve.wait_ge(mT_ps.sem, mT_ps.at(b, p))
                                for j in range(4):
                                    i = ve.tensor_reduce(mx[:, 4 * j:4 * j + 4],
                                                         bank(j)[:, 0:256].rearrange("q (g m) -> q g m", g=4), X, ALU.max)
                                i.then_inc(mx_ok.sem, 1)
                                ve.wait_ge(prT_ps.sem, prT_ps.at(b, 2 * p + 2))
                                if p >= 1:
                                    ve.wait_ge(o_ps.sem, o_ps.at(b, p))
                                ve.tensor_copy(prT[:, 4:8, :].rearrange("q k t -> q (k t)"), bank(5)[:, :])\
                                    .then_inc(prT_v.sem, 1)
                                ve.wait_ge(o_ps.sem, o_ps.at(b, p + 1))
                                o = bank(6)[:, 0:NH * (HD + 1)].rearrange("q (h d) -> q h d", d=HD + 1)
                                ve.reciprocal(rs[:], o[:, :, HD]).then_inc(rs_ok.sem, 1)
                                ve.wait_ge(rs_ok.sem, rs_ok.at(b, p + 1))
                                ve.tensor_tensor(on[:, p, :].rearrange("q (h d) -> q h d", d=HD), o[:, :, 0:HD],
                                                 rs[:].unsqueeze(2).to_broadcast([P, NH, HD]), ALU.mult)\
                                    .then_inc(on_ok.sem, 1)

                            def norm_steps(ln):
                                for p in range(NP):
                                    ve.wait_ge(y_ok.sem, y_ok.at(b, ln * NP + p + 1))
                                    ve.bn_stats(st[:, p, :], y[:, p, :]).then_inc(st_ok.sem, 1)
                                ve.wait_ge(st_ok.sem, st_ok.at(b, (ln + 1) * NP))
                                apart(ve)
                                for p in range(NP):
                                    i = ve.bn_aggr(mv[:, p, :], st[:, p, :])
                                i.then_inc(mv_ok.sem, 1)
                                ve.wait_ge(mv_ok.sem, mv_ok.at(b, ln + 1))
                                ve.tensor_scalar(rstd[:], mv[:, :, 1], 1e-5, None, ALU.add).then_inc(ve_ok.sem, 1)
                                ve.wait_ge(rstd_ok.sem, rstd_ok.at(b, ln + 1))
                                for p in range(NP):
                                    ve.tensor_scalar(y[:, p, :], y[:, p, :], mv[:, p, 0:1], rstd[:, p:p + 1],
                                                     ALU.subtract, ALU.mult).then_inc(yn_ok.sem, 1)
                                ve.wait_ge(xb_ok.sem, xb_ok.at(b, ln + 1))
                                for p in range(NP):
                                    ve.wait_ge(yg_ok.sem, yg_ok.at(b, ln * NP + p + 1))
                                    if ln and p == 0:
                                        ve.wait_ge(x1T_ps.sem, x1T_ps.at(b, 2))
                                    ve.tensor_tensor(x1[:, p, :], y[:, p, :], xg[:, p, :], ALU.add)\
                                        .then_inc(x1_ok.sem, 1)

                            for p in range(NP):
                                ve.wait_ge(pj_ps.sem, pj_ps.at(b, p + 1))
                                ve.tensor_tensor(y[:, p, :], bank(2 + p % 2)[:, 0:C], projb[:], ALU.add)\
                                    .then_inc(y_ok.sem, 1)
                            norm_steps(0)
                            for u in range(2):
                                ve.wait_ge(m_ps.sem, m_ps.at(b, u + 1))
                                for p in range(4):
                                    ve.tensor_tensor(y[:, 4 * u + p, :], bank(6 + u)[:, C * p:C * p + C], f2b[:], ALU.add)\
                                        .then_inc(y_ok.sem, 1)
                            norm_steps(1)
                            ve.wait_ge(x1_ok.sem, x1_ok.at(b, 2 * NP))
                            ve.sem_inc(turn_done, 1)

                    @block.tensor
                    def _(pe):
                        pe.wait_ge(s_load, LOADED)
                        pe.matmul(bank(0)[:, 0:225], cpw1[:], rel[:], start=True, stop=True).then_inc(s_pe, 1)
                        pe.wait_ge(s_rel, 12)
                        for m in range(N):
                            ky, kx = int(KY[m]), int(KX[m])
                            for half in range(2):
                                for c in range(2):
                                    w = relx[:, 7 - kx + 4 * c, 7 - ky:15 - ky, :].rearrange("q a b -> q (a b)")
                                    i = pe.matmul(bank(1 + m // 32)[64 * half + 32 * c:64 * half + 32 * c + 32,
                                                                    (m % 32) * NH:(m % 32 + 1) * NH],
                                                  w, cpw2[:], start=True, stop=True)
                        i.then_inc(s_pe, 1)
                        pe.wait_ge(s_ve, 3)
                        pe.matmul(bank(4)[:, 0:C], cm[:, 0, :], wout[:], start=True, stop=True)
                        pe.matmul(bank(5)[:, 0:C], vbcol[:], projT[:], start=True, stop=True).then_inc(s_pe, 2)
                        pe.wait_ge(s_ve, 5)
                        pe.matmul(bank(3)[:, 0:C], cm[:, 2, :], cm[:, 3, :], start=True, stop=True).then_inc(s_pe, 1)
                        pe.wait_ge(s_ac, 5)
                        pe.wait_ge(s_ve, 5)
                        with pe.Fori(0, NB) as b:
                            pe.wait_ge(turn_done, b * 4)
                            pe.wait_ge(x_in.sem, x_in.at(b, 40))

                            def to_channels(p):
                                pe.transpose(bank(p % 2)[:, 0:P], xw[:, p, :], ident[:]).then_inc(xT_ps.sem, 1)

                            to_channels(0)
                            for p in range(NP):
                                if p + 1 < NP:
                                    to_channels(p + 1)
                                pe.wait_ge(xT_ok.sem, xT_ok.at(b, p + 1))
                                if p >= 2:
                                    pe.wait_ge(qk_ok.sem, qk_ok.at(b, p - 1))
                                    pe.wait_ge(v_ok.sem, v_ok.at(b, 2 * p - 2))
                                pe.matmul(bank(2 + p % 2)[:, 0:2 * C], xT[:, p, :], wqkT[:, 0:2 * C], start=True, stop=True)
                                for w in range(2):
                                    for k in range(2):
                                        i = pe.matmul(bank(4 + p % 2)[64 * k:64 * k + 64, C * w:C * w + C],
                                                      xT[:, p, 64 * w:64 * w + 64], wqkT[:, 2 * C:3 * C],
                                                      start=True, stop=True)
                                i.then_inc(qkv_ps.sem, 1)
                            for p in range(NP):
                                pe.wait_ge(hi_ok.sem, hi_ok.at(b, 2 * p + 2))
                                pe.wait_ge(lo_ok.sem, lo_ok.at(b, 2 * p + 2))
                                if p >= 2:
                                    pe.wait_ge(qkT_ok.sem, qkT_ok.at(b, p - 1))
                                dst = bank(6 + p % 2)[:].bitcast(F16)
                                for a in range(2):
                                    for g in range(4):
                                        i = pe.transpose(dst[:, (4 * a + g) * P:(4 * a + g + 1) * P],
                                                         split[:, p % 2, a, 4 * g:4 * g + 4].rearrange("q h s d -> q (h s d)"),
                                                         ident16[:])
                                i.then_inc(qkT_ps.sem, 1)

                            def scores(p):
                                kind = (2 if p >= 6 else 0) + p % 2
                                pe.wait_ge(qkT_ok.sem, qkT_ok.at(b, p + 1))
                                if p == 0:
                                    pe.wait_ge(v_ok.sem, v_ok.at(b, 2 * NP))
                                    pe.wait_ge(qk_ok.sem, qk_ok.at(b, NP))
                                    pe.wait_ge(qkT_ok.sem, qkT_ok.at(b, NP))
                                for j in range(4):
                                    for k, bt in enumerate((bth, btl)):
                                        pe.matmul(bank(j)[:, 0:256], ident16[:], bt[:, kind, j].rearrange("q g m -> q (g m)"),
                                                  start=(k == 0), stop=False, skip_group_check=True)
                                for g in range(4):
                                    for w in range(2):
                                        for j in range(4):
                                            i = pe.matmul(bank(j)[64 * w:64 * w + 64, 64 * g:64 * g + 64],
                                                          qkT[32 * j:32 * j + 32, p, 0, g, 64 * w:64 * w + 64],
                                                          qkT[32 * j:32 * j + 32, p, 1, g, 64 * w:64 * w + 64],
                                                          start=False, stop=False, skip_group_check=True)
                                i.then_inc(s_ps.sem, 1)

                            def outputs(p):
                                pe.wait_ge(pr_ok.sem, pr_ok.at(b, p + 1))
                                if p >= 1:
                                    pe.wait_ge(prT_a.sem, prT_a.at(b, p))
                                    pe.wait_ge(prT_v.sem, prT_v.at(b, p))
                                for k in range(8):
                                    i = pe.transpose(bank(4 + k // 4)[:, (k % 4) * P:(k % 4 + 1) * P],
                                                     pr[:, 2 * k:2 * k + 2, :].rearrange("q h m -> q (h m)"), ident[:])
                                    if k % 4 == 3:
                                        i.then_inc(prT_ps.sem, 1)

                            def values(p):
                                pe.wait_ge(prT_a.sem, prT_a.at(b, p + 1))
                                pe.wait_ge(prT_v.sem, prT_v.at(b, p + 1))
                                if p >= 1:
                                    pe.wait_ge(on_ok.sem, on_ok.at(b, p))
                                for k in range(8):
                                    j, t = k // 2, k % 2
                                    for w in range(2):
                                        o = bank(6)[64 * w:64 * w + 64, 0:NH * (HD + 1)]\
                                            .rearrange("q (t k j d) -> q t k j d", t=2, k=2, j=4)
                                        v = vd[:, p, w].rearrange("q (t k j) d -> q t k j d", t=2, k=2)
                                        i = pe.matmul(o[:, t, :, j, :], prT[:, k, 64 * w:64 * w + 64], v[:, t, :, j, :],
                                                      start=True, stop=True)
                                i.then_inc(o_ps.sem, 1)

                            scores(0)
                            for p in range(NP):
                                pe.wait_ge(mx_ok.sem, mx_ok.at(b, p + 1))
                                if p >= 1:
                                    pe.wait_ge(mT_ok.sem, mT_ok.at(b, p))
                                pe.transpose(bank(7)[0:NH, 0:P], mx[:], ident[:]).then_inc(mT_ps.sem, 1)
                                pe.wait_ge(mT_ok.sem, mT_ok.at(b, p + 1))
                                for j in range(4):
                                    i = pe.matmul(bank(j)[:, 0:256], mT[:], sel[:, 256 * j:256 * j + 256],
                                                  start=False, stop=True, skip_group_check=True)
                                i.then_inc(sm_ps.sem, 1)
                                outputs(p)
                                if p + 1 < NP:
                                    scores(p + 1)
                                values(p)
                            def merge_heads(p):
                                pe.wait_ge(on_ok.sem, on_ok.at(b, p + 1))
                                if p >= 2:
                                    pe.wait_ge(onT_ok.sem, onT_ok.at(b, p - 1))
                                pe.transpose(bank(p % 2)[:, 0:P], on[:, p, :], ident[:]).then_inc(onT_ps.sem, 1)

                            merge_heads(0)
                            for p in range(NP):
                                if p + 1 < NP:
                                    merge_heads(p + 1)
                                pe.wait_ge(onT_ok.sem, onT_ok.at(b, p + 1))
                                if p >= 2:
                                    pe.wait_ge(y_ok.sem, y_ok.at(b, p - 1))
                                pe.matmul(bank(2 + p % 2)[:, 0:C], onT[:, p, :], projT[:], start=True, stop=True)\
                                    .then_inc(pj_ps.sem, 1)
                            for u in range(2):
                                for p in range(4):
                                    pe.wait_ge(x1_ok.sem, x1_ok.at(b, 4 * u + p + 1))
                                    i = pe.transpose(bank(4 + u)[:, p * P:(p + 1) * P], x1[:, 4 * u + p, :], ident[:])
                                i.then_inc(x1T_ps.sem, 1)
                            for u in range(2):
                                pe.wait_ge(x1T_ok.sem, x1T_ok.at(b, u + 1))
                                for f in range(FC):
                                    if u * FC + f >= 2:
                                        pe.wait_ge(gl_ok.sem, gl_ok.at(b, u * FC + f - 1))
                                    pe.matmul(bank(f % 2)[:, :], f1T[:, f * P:(f + 1) * P], x1T[:, u, :], start=True, stop=True)\
                                        .then_inc(h_ps.sem, 1)
                                pe.wait_ge(gl_ok.sem, gl_ok.at(b, (u + 1) * FC))
                                for p in range(4):
                                    for f in range(FC):
                                        i = pe.matmul(bank(6 + u)[:, C * p:C * p + C], gl[:, f, p * P:(p + 1) * P],
                                                      f2T[:, f, :], start=(f == 0), stop=(f == FC - 1))
                                i.then_inc(m_ps.sem, 1)
                            pe.sem_inc(turn_done, 1)

        def phase_landmarks(lnT, klA, xA, xTA, yA, stR, stC):
            with ExitStack() as c1:
                def sb(name, shape, dt=F32):
                    return c1.enter_context(nc.sbuf_tensor(name, shape, dt))

                t_in = sb("l_t", [P, NP, C])
                st = sb("l_st", [P, NP, 6])
                mv = sb("l_mv", [P, NP, 2])
                rstd = sb("l_rstd", [P, NP])
                lt = sb("l_lt", [P, T])
                lbar = sb("l_bar", [P, LM])
                kl = sb("l_kl", [P, LM])
                qlm = sb("l_qlm", [P, AH, LM])
                kT = sb("l_kT", [P, T])
                v = sb("l_v", [P, NP, C])
                e2 = sb("l_e2", [P, 4, LM])
                m2 = sb("l_m2", [P, 4])
                r2 = sb("l_r2", [P, 4])
                xTs = sb("l_xTs", [LM, 4 * P])
                m3 = sb("l_m3", [P, 4])
                n3 = sb("l_n3", [P, 4])
                sum3 = sb("l_sum3", [P, 4])
                r3 = sb("l_r3", [P, 4])
                p3 = sb("l_p3", [P, 2, T])
                p3T = lt[:].rearrange("p (t l) -> p t l", t=NP)

                t_land = signal("l_t_land", 1, 16)
                st_ok = signal("l_st_ok", NP)
                mv_ok = signal("l_mv_ok", NP)
                var_ok = signal("l_var_ok", 1)
                rstd_ok = signal("l_rstd_ok", 1)
                xn_ok = signal("l_xn_ok", NP)
                lt_ps = signal("l_lt_ps", 2)
                lt_ok = signal("l_lt_ok", 2)
                lnT_ok = signal("l_lnT_ok", 1)
                bar_ok = signal("l_bar_ok", 2)
                kl_ps = signal("l_kl_ps", 1)
                kl_ok = signal("l_kl_ok", 3)
                kT_ps = signal("l_kT_ps", 2)
                kT_ok = signal("l_kT_ok", 2)
                v_ps = signal("l_v_ps", 2)
                v_ok = signal("l_v_ok", 2)
                s2_ps = signal("l_s2_ps", 1)
                m2_ok = signal("l_m2_ok", 1)
                d2_ok = signal("l_d2_ok", 1)
                e2_ok = signal("l_e2_ok", 1)
                r2_ok = signal("l_r2_ok", 2)
                x_ok = signal("l_x_ok", 1)
                xT_ps = signal("l_xT_ps", 1)
                xT_ok = signal("l_xT_ok", 1)
                keep_ok = signal("l_keep_ok", 2)
                s3_ps = signal("l_s3_ps", 4)
                n3_ok = signal("l_n3_ok", 8)
                p3_ok = signal("l_p3_ok", 4)
                p3T_ps = signal("l_p3T_ps", 8)
                p3T_a = signal("l_p3T_a", 4)
                p3T_v = signal("l_p3T_v", 4)
                y_ps = signal("l_y_ps", 4)
                r3_ok = signal("l_r3_ok", 4)
                y_ok = signal("l_y_ok", 8)
                turn_done = sem("l_turn_done")

                with nc.Block() as block:
                    @block.sync
                    def _(sp):
                        with sp.Fori(0, NB) as b:
                            sp.wait_ge(lt_ps.sem, lt_ps.at(b, 0))
                            apart(sp)
                            sp.dma_start(t_in[:], mid[b].rearrange("(t p) c -> p t c", p=P)).then_inc(t_land.sem, 16)

                    @block.gpsimd
                    def _(gp):
                        with gp.Fori(0, NB) as b:
                            gp.wait_ge(var_ok.sem, var_ok.at(b, 1))
                            gp.tensor_tensor(rstd[:], rstd[:], nhalf[:, 0:NP], ALU.pow).then_inc(rstd_ok.sem, 1)
                            gp.wait_ge(lt_ok.sem, lt_ok.at(b, 2))
                            gp.tensor_copy(lnT[:, b, :], lt[:]).then_inc(lnT_ok.sem, 1)
                            gp.wait_ge(x_ok.sem, x_ok.at(b, 1))
                            gp.tensor_copy(xA[:, b, :], e2[:].rearrange("p h j -> p (h j)")).then_inc(keep_ok.sem, 1)
                            gp.wait_ge(keep_ok.sem, keep_ok.at(b, 1))
                            gp.wait_ge(xT_ok.sem, xT_ok.at(b, 1))
                            gp.tensor_copy(xTA[:, b, :], xTs[:]).then_inc(keep_ok.sem, 1)

                    @block.scalar
                    def _(ac):
                        with ac.Fori(0, NB) as b:
                            ac.wait_ge(turn_done, b * 3)
                            for u in range(2):
                                ac.wait_ge(lt_ps.sem, lt_ps.at(b, u + 1))
                                if u == 0:
                                    ac.wait_ge(lnT_ok.sem, lnT_ok.at(b, 0))
                                ac.activation(lt[:, 512 * u:512 * u + 512], bank(u), ACT.Copy).then_inc(lt_ok.sem, 1)
                            for u in range(2):
                                ac.wait_ge(kT_ps.sem, kT_ps.at(b, u + 1))
                                ac.activation(kT[:, 512 * u:512 * u + 512], bank(3 + u), ACT.Copy).then_inc(kT_ok.sem, 1)
                            ac.wait_ge(d2_ok.sem, d2_ok.at(b, 1))
                            ac.activation(e2[:], e2[:], ACT.Exp).then_inc(e2_ok.sem, 1)
                            ac.wait_ge(xT_ps.sem, xT_ps.at(b, 1))
                            ac.wait_ge(keep_ok.sem, keep_ok.at(b, 0))
                            ac.activation(xTs[:], bank(7)[0:LM, :], ACT.Copy).then_inc(xT_ok.sem, 1)
                            for h in range(4):
                                ac.wait_ge(n3_ok.sem, n3_ok.at(b, 2 * h + 2))
                                if h >= 2:
                                    ac.wait_ge(p3T_ps.sem, p3T_ps.at(b, 2 * h - 2))
                                ac.activation(p3[:, h % 2, :], banks(2 * (h % 2), 2), ACT.Exp, bias=n3[:, h:h + 1],
                                              accum_out=sum3[:, h:h + 1]).then_inc(p3_ok.sem, 1)
                                ac.wait_ge(p3T_ps.sem, p3T_ps.at(b, 2 * h + 1))
                                if h == 0:
                                    ac.wait_ge(lnT_ok.sem, lnT_ok.at(b, 1))
                                else:
                                    ac.wait_ge(y_ps.sem, y_ps.at(b, h))
                                ac.activation(p3T[:, 0:4, :].rearrange("p a c -> p (a c)"), bank(4), ACT.Copy)\
                                    .then_inc(p3T_a.sem, 1)
                            ac.wait_ge(p3T_a.sem, p3T_a.at(b, 4))
                            ac.sem_inc(turn_done, 1)

                    @block.vector
                    def _(ve):
                        with ve.Fori(0, NB) as b:
                            ve.wait_ge(turn_done, b * 3)
                            ve.wait_ge(t_land.sem, t_land.at(b, 1))
                            for t in range(NP):
                                ve.bn_stats(st[:, t, :], t_in[:, t, :]).then_inc(st_ok.sem, 1)
                            for t in range(NP):
                                ve.wait_ge(st_ok.sem, st_ok.at(b, t + 1))
                                apart(ve)
                                ve.bn_aggr(mv[:, t, :], st[:, t, :]).then_inc(mv_ok.sem, 1)
                            ve.wait_ge(mv_ok.sem, mv_ok.at(b, NP))
                            ve.tensor_scalar(rstd[:], mv[:, :, 1], 1e-5, None, ALU.add).then_inc(var_ok.sem, 1)
                            ve.wait_ge(rstd_ok.sem, rstd_ok.at(b, 1))
                            for t in range(NP):
                                ve.tensor_scalar(t_in[:, t, :], t_in[:, t, :], mv[:, t, 0:1], rstd[:, t:t + 1],
                                                 ALU.subtract, ALU.mult).then_inc(xn_ok.sem, 1)
                            ve.wait_ge(lt_ok.sem, lt_ok.at(b, 2))
                            ve.tensor_reduce(lbar[:], lt[:].rearrange("p (l s) -> p l s", s=SEG), X, ALU.add)\
                                .then_inc(bar_ok.sem, 1)
                            ve.wait_ge(bar_ok.sem, bar_ok.at(b, 1))
                            ve.tensor_scalar(lbar[:], lbar[:], 1.0 / SEG, None, ALU.mult).then_inc(bar_ok.sem, 1)
                            ve.wait_ge(kl_ps.sem, kl_ps.at(b, 1))
                            ve.tensor_copy(kl[:], bank(2)[:, 0:LM]).then_inc(kl_ok.sem, 1)
                            ve.tensor_copy(klA[:, b, :], bank(2)[:, 0:LM]).then_inc(kl_ok.sem, 1)
                            ve.tensor_tensor(qlm[:], bank(2)[:, LM:2 * LM].unsqueeze(1).to_broadcast([P, AH, LM]),
                                             headmask[:].unsqueeze(2).to_broadcast([P, AH, LM]), ALU.mult)\
                                .then_inc(kl_ok.sem, 1)
                            for u in range(2):
                                ve.wait_ge(v_ps.sem, v_ps.at(b, u + 1))
                                ve.tensor_copy(v[:, 4 * u:4 * u + 4, :].rearrange("p t c -> p (t c)"), bank(5 + u))\
                                    .then_inc(v_ok.sem, 1)
                            ve.wait_ge(s2_ps.sem, s2_ps.at(b, 1))
                            ve.wait_ge(keep_ok.sem, keep_ok.at(b, 0))
                            s2 = bank(7)[:, 0:4 * LM].rearrange("p (h j) -> p h j", h=4)
                            ve.tensor_reduce(m2[:], s2, X, ALU.max).then_inc(m2_ok.sem, 1)
                            ve.wait_ge(m2_ok.sem, m2_ok.at(b, 1))
                            ve.tensor_tensor(e2[:], s2, m2[:].unsqueeze(2).to_broadcast([P, 4, LM]), ALU.subtract)\
                                .then_inc(d2_ok.sem, 1)
                            ve.wait_ge(e2_ok.sem, e2_ok.at(b, 1))
                            ve.tensor_reduce(r2[:], e2[:], X, ALU.add).then_inc(r2_ok.sem, 1)
                            ve.wait_ge(r2_ok.sem, r2_ok.at(b, 1))
                            ve.reciprocal(r2[:], r2[:]).then_inc(r2_ok.sem, 1)
                            ve.wait_ge(r2_ok.sem, r2_ok.at(b, 2))
                            ve.tensor_tensor(e2[:], e2[:], r2[:].unsqueeze(2).to_broadcast([P, 4, LM]), ALU.mult)\
                                .then_inc(x_ok.sem, 1)
                            ve.wait_ge(x_ok.sem, x_ok.at(b, 1))
                            ve.tensor_reduce(stR[:, b, :], e2[:], X, ALU.add)
                            ve.wait_ge(xT_ok.sem, xT_ok.at(b, 1))
                            ve.tensor_reduce(stC[:, b, :], xTs[:].rearrange("p (h i) -> p h i", h=AH), X, ALU.add)
                            for h in range(4):
                                ve.wait_ge(s3_ps.sem, s3_ps.at(b, h + 1))
                                ve.tensor_reduce(m3[:, h:h + 1], banks(2 * (h % 2), 2), X, ALU.max).then_inc(n3_ok.sem, 1)
                                ve.wait_ge(n3_ok.sem, n3_ok.at(b, 2 * h + 1))
                                ve.tensor_scalar(n3[:, h:h + 1], m3[:, h:h + 1], -1.0, None, ALU.mult)\
                                    .then_inc(n3_ok.sem, 1)
                                ve.wait_ge(p3T_ps.sem, p3T_ps.at(b, 2 * h + 2))
                                if h == 0:
                                    ve.wait_ge(lnT_ok.sem, lnT_ok.at(b, 1))
                                else:
                                    ve.wait_ge(y_ps.sem, y_ps.at(b, h))
                                ve.tensor_copy(p3T[:, 4:8, :].rearrange("p a c -> p (a c)"), bank(5))\
                                    .then_inc(p3T_v.sem, 1)
                                ve.wait_ge(p3_ok.sem, p3_ok.at(b, h + 1))
                                ve.reciprocal(r3[:, h:h + 1], sum3[:, h:h + 1]).then_inc(r3_ok.sem, 1)
                                ve.wait_ge(r3_ok.sem, r3_ok.at(b, h + 1))
                                ve.wait_ge(y_ps.sem, y_ps.at(b, h + 1))
                                for k in range(2):
                                    q = slice(64 * k, 64 * k + 64)
                                    ve.tensor_scalar(yA[q, b, AD * h:AD * h + AD], bank(6)[q, 32 * h + AD * k:32 * h + AD * k + AD],
                                                     r3[q, h:h + 1], None, ALU.mult).then_inc(y_ok.sem, 1)
                            ve.wait_ge(y_ok.sem, y_ok.at(b, 8))
                            ve.sem_inc(turn_done, 1)

                    @block.tensor
                    def _(pe):
                        with pe.Fori(0, NB) as b:
                            pe.wait_ge(turn_done, b * 3)
                            for t in range(NP):
                                pe.wait_ge(xn_ok.sem, xn_ok.at(b, t + 1))
                                i = pe.transpose(bank(t // 4)[:, (t % 4) * P:(t % 4 + 1) * P], t_in[:, t, :], ident[:])
                                if t % 4 == 3:
                                    i.then_inc(lt_ps.sem, 1)
                            pe.wait_ge(lt_ok.sem, lt_ok.at(b, 2))
                            for u in range(2):
                                pe.matmul(bank(3 + u), wqkv2[:, C:2 * C], lt[:, 512 * u:512 * u + 512], start=True, stop=True)\
                                    .then_inc(kT_ps.sem, 1)
                            for t in range(NP):
                                i = pe.matmul(bank(5 + t // 4)[:, (t % 4) * C:(t % 4 + 1) * C], lt[:, t * P:(t + 1) * P],
                                              wqkv2[:, 2 * C:3 * C], start=True, stop=True)
                                if t % 4 == 3:
                                    i.then_inc(v_ps.sem, 1)
                            pe.wait_ge(bar_ok.sem, bar_ok.at(b, 2))
                            pe.matmul(bank(2)[:, 0:LM], wqkv2[:, C:2 * C], lbar[:], start=True, stop=True)
                            pe.matmul(bank(2)[:, LM:2 * LM], wqkv2[:, 0:C], lbar[:], start=True, stop=True)\
                                .then_inc(kl_ps.sem, 1)
                            pe.wait_ge(kl_ok.sem, kl_ok.at(b, 3))
                            for h in range(4):
                                i = pe.matmul(bank(7)[:, h * LM:(h + 1) * LM], qlm[:, 2 * h:2 * h + 2, :]
                                              .rearrange("p a l -> p (a l)"), kl[:], start=True, stop=True)
                            i.then_inc(s2_ps.sem, 1)

                            def scores(h):
                                if h == 0:
                                    pe.wait_ge(kT_ok.sem, kT_ok.at(b, 2))
                                if h >= 2:
                                    pe.wait_ge(p3_ok.sem, p3_ok.at(b, h - 1))
                                for u in range(2):
                                    i = pe.matmul(bank(2 * (h % 2) + u), qlm[:, 2 * h:2 * h + 2, :].rearrange("p a l -> p (a l)"),
                                                  kT[:, 512 * u:512 * u + 512], start=True, stop=True)
                                i.then_inc(s3_ps.sem, 1)

                            scores(0)
                            scores(1)
                            pe.wait_ge(x_ok.sem, x_ok.at(b, 1))
                            apart(pe)
                            for h in range(4):
                                i = pe.transpose(bank(7)[0:LM, h * P:(h + 1) * P], e2[:, h, :], ident[:])
                            i.then_inc(xT_ps.sem, 1)
                            for h in range(4):
                                pe.wait_ge(p3_ok.sem, p3_ok.at(b, h + 1))
                                if h == 0:
                                    pe.wait_ge(v_ok.sem, v_ok.at(b, 2))
                                else:
                                    pe.wait_ge(p3T_a.sem, p3T_a.at(b, h))
                                    pe.wait_ge(p3T_v.sem, p3T_v.at(b, h))
                                for t in range(NP):
                                    i = pe.transpose(bank(4 + t // 4)[:, (t % 4) * P:(t % 4 + 1) * P],
                                                     p3[:, h % 2, t * P:(t + 1) * P], ident[:])
                                    if t % 4 == 3:
                                        i.then_inc(p3T_ps.sem, 1)
                                if h + 2 < 4:
                                    scores(h + 2)
                                pe.wait_ge(p3T_a.sem, p3T_a.at(b, h + 1))
                                pe.wait_ge(p3T_v.sem, p3T_v.at(b, h + 1))
                                if h:
                                    pe.wait_ge(y_ok.sem, y_ok.at(b, 2 * h))
                                for t in range(NP):
                                    i = pe.matmul(bank(6)[:, 32 * h:32 * h + 32], p3T[:, t, :], v[:, t, 32 * h:32 * h + 32],
                                                  start=(t == 0), stop=(t == NP - 1))
                                i.then_inc(y_ps.sem, 1)
                            pe.sem_inc(turn_done, 1)

        def phase_pinv(xA, xTA, yA, zA, stR, stC):
            G = min(4, NB)
            with ExitStack() as c1:
                def sb(name, shape, dt=F32):
                    return c1.enter_context(nc.sbuf_tensor(name, shape, dt))

                i64 = sb("p_i64", [P, 3, LM])
                mxs = sb("p_mx", [P, 2])
                mrow = sb("p_mrow", [1, 4])
                cc = sb("p_c", [P, 1])
                xts = sb("p_xts", [LM, G, 4 * P])
                xs = sb("p_xs", [P, G, 4 * LM])
                ay = sb("p_ay", [P, G, 4, LM + AD])
                tm = sb("p_t", [P, G, 4, LM])

                s_i = sem("p_s_i")
                s_ik = sem("p_s_ik")
                s_m = sem("p_s_m")
                s_mt = sem("p_s_mt")
                s_row = sem("p_s_row")
                s_cb = sem("p_s_cb")
                s_c = sem("p_s_c")
                got = signal("p_got", 3 * G)
                prod = signal("p_prod", G * (3 * ITERS + 2))
                a_ok = signal("p_a_ok", G * (ITERS + 1))
                t_ok = signal("p_t_ok", G * 3 * ITERS)
                z_ok = signal("p_z_ok", G)

                def slot(n, i):
                    return (n % 2) * 4 + i

                with nc.Block() as block:
                    @block.sync
                    def _(sp):
                        sp.dma_start(i64[:, 0, :], A["i64"]).then_inc(s_i, 16)

                    @block.gpsimd
                    def _(gp):
                        with gp.Fori(0, NB // G) as g:
                            gp.wait_ge(prod.sem, prod.at(g, 0))
                            gp.wait_ge(z_ok.sem, z_ok.at(g, 0))
                            for i in range(G):
                                if i:
                                    gp.wait_ge(got.sem, got.at(g, 3 * i))
                                gp.tensor_copy(xts[:, i, :], xTA[:, g * G + i, :]).then_inc(got.sem, 1)
                                gp.wait_ge(got.sem, got.at(g, 3 * i + 1))
                                gp.tensor_copy(xs[:, i, :], xA[:, g * G + i, :]).then_inc(got.sem, 1)
                                gp.tensor_copy(ay[:, i, :, LM:LM + AD],
                                               yA[:, g * G + i, :].rearrange("p (h d) -> p h d", h=4)).then_inc(got.sem, 1)

                    @block.vector
                    def _(ve):
                        ve.wait_ge(s_i, 16)
                        ve.tensor_scalar(i64[:, 1, :], i64[:, 0, :], 15.0, None, ALU.mult).then_inc(s_ik, 1)
                        ve.tensor_scalar(i64[:, 2, :], i64[:, 0, :], 3.25, None, ALU.mult).then_inc(s_ik, 1)
                        ve.wait_ge(s_ik, 2)
                        ve.tensor_scalar(i64[:, 0, :], i64[:, 0, :], 7.0, None, ALU.mult).then_inc(s_ik, 1)
                        ve.tensor_reduce(mxs[:, 0:1], stR[:].rearrange("p b h -> p (b h)"), X, ALU.max).then_inc(s_m, 1)
                        ve.tensor_reduce(mxs[0:LM, 1:2], stC[:].rearrange("p b h -> p (b h)"), X, ALU.max).then_inc(s_m, 1)
                        ve.wait_ge(s_mt, 1)
                        ve.tensor_reduce(mrow[:, 0:1], bank(0)[0:1, 0:P], X, ALU.max).then_inc(s_row, 1)
                        ve.tensor_reduce(mrow[:, 1:2], bank(0)[0:1, P:P + LM], X, ALU.max).then_inc(s_row, 1)
                        ve.wait_ge(s_row, 2)
                        ve.tensor_tensor(mrow[:, 2:3], mrow[:, 0:1], mrow[:, 1:2], ALU.mult).then_inc(s_row, 1)
                        ve.wait_ge(s_row, 3)
                        ve.reciprocal(mrow[:, 3:4], mrow[:, 2:3]).then_inc(s_row, 1)
                        ve.wait_ge(s_cb, 1)
                        ve.tensor_copy(cc[:], bank(1)[:, 0:1]).then_inc(s_c, 1)
                        ve.wait_ge(s_c, 1)
                        ve.wait_ge(s_ik, 3)
                        with ve.Fori(0, NB // G) as g:
                            def ident_minus(i, k, n):
                                ps = bank(slot(n, i))[:, 0:4 * (LM + AD)].rearrange("p (h j) -> p h j", h=4)[:, :, 0:LM]
                                eye = i64[:, k, :].unsqueeze(1).to_broadcast([P, 4, LM])
                                if k == 2:
                                    ve.scalar_tensor_tensor(out=tm[:, i], in0=ps, scalar=-0.25, in1=eye, op0=ALU.mult,
                                                            op1=ALU.add).then_inc(t_ok.sem, 1)
                                else:
                                    ve.tensor_tensor(tm[:, i], eye, ps, ALU.subtract).then_inc(t_ok.sem, 1)

                            for i in range(G):
                                ve.wait_ge(prod.sem, prod.at(g, i + 1))
                                ps = bank(slot(0, i))[:, 0:4 * (LM + AD)].rearrange("p (h j) -> p h j", h=4)[:, :, 0:LM]
                                ve.tensor_scalar(ay[:, i, :, 0:LM], ps, cc[:, 0:1], None, ALU.mult).then_inc(a_ok.sem, 1)
                            for i in range(G):
                                ve.wait_ge(a_ok.sem, a_ok.at(g, i + 1))
                                ve.tensor_tensor(tm[:, i], i64[:, 0, :].unsqueeze(1).to_broadcast([P, 4, LM]),
                                                 ay[:, i, :, 0:LM], ALU.subtract).then_inc(t_ok.sem, 1)
                            n = 1
                            for it in range(ITERS):
                                for k in (1, 2, 0):
                                    for i in range(G):
                                        ve.wait_ge(prod.sem, prod.at(g, G * n + i + 1))
                                        if k:
                                            ident_minus(i, k, n)
                                        else:
                                            ve.tensor_copy(ay[:, i], bank(slot(n, i))[:, 0:4 * (LM + AD)]
                                                           .rearrange("p (h j) -> p h j", h=4)).then_inc(a_ok.sem, 1)
                                            if it < ITERS - 1:
                                                ident_minus(i, 0, n)
                                    n += 1
                            for i in range(G):
                                ve.wait_ge(prod.sem, prod.at(g, G * n + i + 1))
                                ve.tensor_scalar(zA[:, g * G + i, :], bank(slot(n, i))[:, 0:4 * AD], cc[:, 0:1], None,
                                                 ALU.mult).then_inc(z_ok.sem, 1)

                    @block.tensor
                    def _(pe):
                        pe.wait_ge(s_m, 2)
                        pe.transpose(bank(0)[0:1, 0:P], mxs[:, 0:1], ident[:])
                        pe.transpose(bank(0)[0:1, P:P + LM], mxs[0:LM, 1:2], ident[0:LM, 0:LM]).then_inc(s_mt, 1)
                        pe.wait_ge(s_row, 4)
                        pe.matmul(bank(1)[:, 0:1], ones1[:], mrow[:, 3:4], start=True, stop=True).then_inc(s_cb, 1)
                        pe.wait_ge(s_c, 1)
                        with pe.Fori(0, NB // G) as g:
                            def each(n, i, width, left, right, stride=LM + AD):
                                for h in range(4):
                                    for k in range(2):
                                        j = pe.matmul(bank(slot(n, i))[64 * k:64 * k + 64, stride * h:stride * h + width],
                                                      left(h, k), right(h, k), start=True, stop=True)
                                j.then_inc(prod.sem, 1)

                            half = lambda k: slice(64 * k, 64 * k + 64)
                            pe.wait_ge(z_ok.sem, z_ok.at(g, 0))
                            for i in range(G):
                                pe.wait_ge(got.sem, got.at(g, 3 * i + 3))
                                apart(pe)
                                xt = lambda h, k: xts[:, i, P * h + 64 * k:P * h + 64 * k + 64]
                                each(0, i, LM, xt, xt)
                            n = 1
                            for it in range(ITERS):
                                for k in range(3):
                                    for i in range(G):
                                        if it == 0 and k == 0:
                                            pe.wait_ge(a_ok.sem, a_ok.at(g, i + 1))
                                        pe.wait_ge(t_ok.sem, t_ok.at(g, G * (n - 1) + i + 1))
                                        apart(pe)
                                        a = lambda h, q: ay[half(q), i, h, 0:LM]
                                        t = lambda h, q: tm[half(q), i, h, :]
                                        if k < 2:
                                            each(n, i, LM, a, t)
                                        else:
                                            each(n, i, LM + AD, t, lambda h, q: ay[half(q), i, h, :])
                                    n += 1
                            for i in range(G):
                                pe.wait_ge(a_ok.sem, a_ok.at(g, G * ITERS + i + 1))
                                apart(pe)
                                each(n, i, AD, lambda h, q: xs[half(q), i, LM * h:LM * h + LM],
                                     lambda h, q: ay[half(q), i, h, LM:LM + AD], stride=AD)

        def phase_mix(lnT, klA, zA):
            with ExitStack() as c1:
                def sb(name, shape, dt=F32):
                    return c1.enter_context(nc.sbuf_tensor(name, shape, dt))

                t_in = sb("m_t", [P, NP, C])
                lt = sb("m_lt", [P, T])
                kl = sb("m_kl", [P, LM])
                klm = sb("m_klm", [P, AH, LM])
                zd = sb("m_zd", [P, 4, 2, AD + 1])
                qT = sb("m_qT", [P, T])
                m1 = sb("m_m1", [P, 2, AH])
                e1 = sb("m_e1", [P, 2, AH, LM])
                p1T = sb("m_p1T", [P, 2, 4, P])
                r1 = sb("m_r1", [P, 2, AH])
                on = sb("m_on", [P, 2, C])
                onT = sb("m_onT", [P, 2, P])
                t2 = sb("m_t2", [P, NP, C])
                xn = sb("m_xn", [P, NP, C])
                st = sb("m_st", [P, NP, 6])
                mv = sb("m_mv", [P, NP, 2])
                rstd = sb("m_rstd", [P, NP])
                xf = sb("m_xf", [P, T])
                xh = sb("m_xh", [P, T], F16)
                lg = sb("m_lg", [P, NP, NE])
                lm = sb("m_lm", [P, NP])
                gt = sb("m_gt", [P, NP, NE, NE])
                eq = sb("m_eq", [P, NP, NE, NE])
                tri = sb("m_tri", [P, NE, NE])
                rank = sb("m_rank", [P, NP, NE])
                cwl = sb("m_cwl", [P, NP, NE])
                cwT = sb("m_cwT", [NE, T])
                x16 = lnT[:].bitcast(F16)

                tri_in = sem("m_tri_in")
                zd_set = sem("m_zd_set")
                t_land = signal("m_t_land", 1, 16)
                lt_in = signal("m_lt_in", 1)
                klz_in = signal("m_klz_in", 3)
                klm_ok = signal("m_klm_ok", 1)
                tb_ok = signal("m_tb_ok", 1)
                qT_ps = signal("m_qT_ps", 2)
                qT_ok = signal("m_qT_ok", 2)
                s_ps = signal("m_s_ps", NP)
                mx_ok = signal("m_mx_ok", NP)
                d_ok = signal("m_d_ok", NP)
                e_ok = signal("m_e_ok", NP)
                eT_ps = signal("m_eT_ps", NP)
                eT_ok = signal("m_eT_ok", NP)
                o_ps = signal("m_o_ps", NP)
                r_ok = signal("m_r_ok", NP)
                on_ok = signal("m_on_ok", NP)
                onT_ps = signal("m_onT_ps", NP)
                onT_ok = signal("m_onT_ok", NP)
                w_ps = signal("m_w_ps", NP)
                t2_ok = signal("m_t2_ok", NP)
                st_ok = signal("m_st_ok", NP)
                mv_ok = signal("m_mv_ok", NP)
                var_ok = signal("m_var_ok", 1)
                rstd_ok = signal("m_rstd_ok", 1)
                xn_ok = signal("m_xn_ok", NP)
                xf_ps = signal("m_xf_ps", 2)
                xf_ok = signal("m_xf_ok", 2)
                hi_ok = signal("m_hi_ok", 2)
                keep_ok = signal("m_keep_ok", 1)
                lo_ok = signal("m_lo_ok", 1)
                lg_ps = signal("m_lg_ps", 1)
                gate = signal("m_gate", 13)
                ex_ok = signal("m_ex_ok", 1)
                cwT_ps = signal("m_cwT_ps", 1)
                cwT_ok = signal("m_cwT_ok", 1)
                b_ps = signal("m_b_ps", 1)
                b_ok = signal("m_b_ok", 1)
                r_out = signal("m_r_out", 1)
                stored = signal("m_stored", 1, 16)
                turn_done = sem("m_turn_done")

                def onT_copy(ac, b, t):
                    ac.wait_ge(onT_ps.sem, onT_ps.at(b, t + 1))
                    if t >= 2:
                        ac.wait_ge(w_ps.sem, w_ps.at(b, t - 1))
                    ac.activation(onT[:, t % 2, :], bank(t % 2)[:, 0:P], ACT.Copy).then_inc(onT_ok.sem, 1)

                with nc.Block() as block:
                    @block.sync
                    def _(sp):
                        sp.dma_start(tri[:], A["tri"]).then_inc(tri_in, 16)
                        with sp.Fori(0, NB) as b:
                            sp.wait_ge(r_out.sem, r_out.at(b, 0))
                            apart(sp)
                            sp.dma_start(t_in[:], mid[b].rearrange("(t p) c -> p t c", p=P)).then_inc(t_land.sem, 16)
                            sp.wait_ge(r_out.sem, r_out.at(b, 1))
                            apart(sp)
                            sp.dma_start(res[b].rearrange("(t p) c -> p t c", p=P), xn[:]).then_inc(stored.sem, 16)
                            sp.wait_ge(stored.sem, stored.at(b, 1))
                            apart(sp)

                    @block.gpsimd
                    def _(gp):
                        gp.memset(zd[:], 0.0).then_inc(zd_set, 1)
                        for k in range(2):
                            gp.wait_ge(zd_set, k + 1)
                            gp.memset(zd[64 * k:64 * k + 64, :, k, AD:AD + 1], 1.0).then_inc(zd_set, 1)
                        gp.wait_ge(zd_set, 3)
                        with gp.Fori(0, NB) as b:
                            gp.wait_ge(turn_done, b * 4)
                            gp.tensor_copy(lt[:], lnT[:, b, :]).then_inc(lt_in.sem, 1)
                            gp.tensor_copy(kl[:], klA[:, b, :]).then_inc(klz_in.sem, 1)
                            for k in range(2):
                                q = slice(64 * k, 64 * k + 64)
                                gp.wait_ge(klz_in.sem, klz_in.at(b, k + 1))
                                gp.tensor_copy(zd[q, :, k, 0:AD], zA[q, b, :].rearrange("p (h d) -> p h d", h=4))\
                                    .then_inc(klz_in.sem, 1)
                            gp.wait_ge(klz_in.sem, klz_in.at(b, 3))
                            gp.wait_ge(t_land.sem, t_land.at(b, 1))
                            gp.tensor_tensor(t_in[:], t_in[:], bout[:].unsqueeze(1).to_broadcast([P, NP, C]), ALU.add)\
                                .then_inc(tb_ok.sem, 1)
                            gp.wait_ge(var_ok.sem, var_ok.at(b, 1))
                            gp.tensor_tensor(rstd[:], rstd[:], nhalf[:, 0:NP], ALU.pow).then_inc(rstd_ok.sem, 1)
                            gp.wait_ge(hi_ok.sem, hi_ok.at(b, 2))
                            gp.tensor_copy(x16[:, b, 0:T], xh[:]).then_inc(keep_ok.sem, 1)
                            gp.wait_ge(b_ok.sem, b_ok.at(b, 1))
                            gp.tensor_tensor(xn[:], xn[:], b2s[:, 0, :].unsqueeze(1).to_broadcast([P, NP, C]), ALU.add)\
                                .then_inc(r_out.sem, 1)
                            gp.wait_ge(r_out.sem, r_out.at(b, 1))
                            gp.wait_ge(keep_ok.sem, keep_ok.at(b, 1))
                            gp.sem_inc(turn_done, 1)

                    @block.scalar
                    def _(ac):
                        with ac.Fori(0, NB) as b:
                            ac.wait_ge(turn_done, b * 4)
                            for u in range(2):
                                ac.wait_ge(qT_ps.sem, qT_ps.at(b, u + 1))
                                ac.activation(qT[:, 512 * u:512 * u + 512], bank(u), ACT.Copy).then_inc(qT_ok.sem, 1)
                            for t in range(NP):
                                ac.wait_ge(d_ok.sem, d_ok.at(b, t + 1))
                                ac.activation(e1[:, t % 2], e1[:, t % 2], ACT.Exp).then_inc(e_ok.sem, 1)
                                ac.wait_ge(eT_ps.sem, eT_ps.at(b, t + 1))
                                if t >= 2:
                                    ac.wait_ge(o_ps.sem, o_ps.at(b, t - 1))
                                ac.activation(p1T[:, t % 2].rearrange("p a c -> p (a c)"), bank(4 + t % 2), ACT.Copy)\
                                    .then_inc(eT_ok.sem, 1)
                                if t >= 1:
                                    onT_copy(ac, b, t - 1)
                            onT_copy(ac, b, NP - 1)
                            for u in range(2):
                                ac.wait_ge(xf_ps.sem, xf_ps.at(b, u + 1))
                                s = slice(512 * u, 512 * u + 512)
                                ac.activation(xf[:, s], bank(2 + u), ACT.Copy).then_inc(xf_ok.sem, 1)
                                ac.activation(xh[:, s], bank(2 + u), ACT.Copy).then_inc(hi_ok.sem, 1)
                            ac.wait_ge(gate.sem, gate.at(b, 3))
                            ac.activation(lg[:], lg[:], ACT.Exp).then_inc(ex_ok.sem, 1)
                            ac.wait_ge(cwT_ps.sem, cwT_ps.at(b, 1))
                            ac.activation(cwT[:], banks(5, 2)[0:NE, :], ACT.Copy).then_inc(cwT_ok.sem, 1)
                            ac.wait_ge(cwT_ok.sem, cwT_ok.at(b, 1))
                            ac.sem_inc(turn_done, 1)

                    @block.vector
                    def _(ve):
                        ve.wait_ge(tri_in, 16)
                        with ve.Fori(0, NB) as b:
                            ve.wait_ge(turn_done, b * 4)
                            ve.wait_ge(klz_in.sem, klz_in.at(b, 1))
                            ve.tensor_tensor(klm[:], kl[:].unsqueeze(1).to_broadcast([P, AH, LM]),
                                             headmask[:].unsqueeze(2).to_broadcast([P, AH, LM]), ALU.mult)\
                                .then_inc(klm_ok.sem, 1)

                            def soft(t):
                                ve.wait_ge(s_ps.sem, s_ps.at(b, t + 1))
                                if t >= 2:
                                    ve.wait_ge(eT_ps.sem, eT_ps.at(b, t - 1))
                                s = bank(2 + t % 2).rearrange("p (h l) -> p h l", h=AH)
                                ve.tensor_reduce(m1[:, t % 2, :], s, X, ALU.max).then_inc(mx_ok.sem, 1)
                                ve.wait_ge(mx_ok.sem, mx_ok.at(b, t + 1))
                                ve.tensor_tensor(e1[:, t % 2], s, m1[:, t % 2, :].unsqueeze(2).to_broadcast([P, AH, LM]),
                                                 ALU.subtract).then_inc(d_ok.sem, 1)

                            def normed(t):
                                ve.wait_ge(o_ps.sem, o_ps.at(b, t + 1))
                                if t >= 2:
                                    ve.wait_ge(onT_ps.sem, onT_ps.at(b, t - 1))
                                o = bank(6 + t % 2)[:, 0:AH * (AD + 1)].rearrange("p (h d) -> p h d", h=AH)
                                ve.reciprocal(r1[:, t % 2, :], o[:, :, AD]).then_inc(r_ok.sem, 1)
                                ve.wait_ge(r_ok.sem, r_ok.at(b, t + 1))
                                ve.tensor_tensor(on[:, t % 2, :].rearrange("p (h d) -> p h d", h=AH), o[:, :, 0:AD],
                                                 r1[:, t % 2, :].unsqueeze(2).to_broadcast([P, AH, AD]), ALU.mult)\
                                    .then_inc(on_ok.sem, 1)

                            def add_out(t):
                                ve.wait_ge(w_ps.sem, w_ps.at(b, t + 1))
                                if t == 0:
                                    ve.wait_ge(tb_ok.sem, tb_ok.at(b, 1))
                                ve.tensor_tensor(t2[:, t, :], bank(t % 2)[:, C:2 * C], t_in[:, t, :], ALU.add)\
                                    .then_inc(t2_ok.sem, 1)
                                ve.wait_ge(t2_ok.sem, t2_ok.at(b, t + 1))
                                ve.bn_stats(st[:, t, :], t2[:, t, :]).then_inc(st_ok.sem, 1)

                            soft(0)
                            for t in range(NP):
                                if t + 1 < NP:
                                    soft(t + 1)
                                normed(t)
                                if t >= 1:
                                    add_out(t - 1)
                            add_out(NP - 1)
                            for t in range(NP):
                                ve.wait_ge(st_ok.sem, st_ok.at(b, t + 1))
                                apart(ve)
                                ve.bn_aggr(mv[:, t, :], st[:, t, :]).then_inc(mv_ok.sem, 1)
                            ve.wait_ge(mv_ok.sem, mv_ok.at(b, NP))
                            ve.tensor_scalar(rstd[:], mv[:, :, 1], 1e-5, None, ALU.add).then_inc(var_ok.sem, 1)
                            ve.wait_ge(rstd_ok.sem, rstd_ok.at(b, 1))
                            ve.wait_ge(stored.sem, stored.at(b, 0))
                            for t in range(NP):
                                ve.tensor_scalar(xn[:, t, :], t2[:, t, :], mv[:, t, 0:1], rstd[:, t:t + 1],
                                                 ALU.subtract, ALU.mult).then_inc(xn_ok.sem, 1)
                            g = lambda n: gate.at(b, n)
                            ve.wait_ge(lg_ps.sem, lg_ps.at(b, 1))
                            ve.tensor_tensor(lg[:], bank(4)[:, 0:NP * NE].rearrange("p (t e) -> p t e", e=NE),
                                             gb[:].unsqueeze(1).to_broadcast([P, NP, NE]), ALU.add).then_inc(gate.sem, 1)
                            ve.wait_ge(gate.sem, g(1))
                            ve.tensor_reduce(lm[:], lg[:], X, ALU.max).then_inc(gate.sem, 1)
                            ve.wait_ge(gate.sem, g(2))
                            ve.tensor_tensor(lg[:], lg[:], lm[:].unsqueeze(2).to_broadcast([P, NP, NE]), ALU.subtract)\
                                .then_inc(gate.sem, 1)
                            ve.wait_ge(ex_ok.sem, ex_ok.at(b, 1))
                            ve.tensor_reduce(lm[:], lg[:], X, ALU.add).then_inc(gate.sem, 1)
                            ve.wait_ge(gate.sem, g(4))
                            ve.reciprocal(lm[:], lm[:]).then_inc(gate.sem, 1)
                            ve.wait_ge(gate.sem, g(5))
                            ve.tensor_tensor(lg[:], lg[:], lm[:].unsqueeze(2).to_broadcast([P, NP, NE]), ALU.mult)\
                                .then_inc(gate.sem, 1)
                            ve.wait_ge(gate.sem, g(6))
                            for t in range(NP):
                                other = lg[:, t, :].unsqueeze(1).to_broadcast([P, NE, NE])
                                own = lg[:, t, :].unsqueeze(2).to_broadcast([P, NE, NE])
                                i1 = ve.tensor_tensor(eq[:, t], other, own, ALU.is_equal)
                                i2 = ve.tensor_tensor(gt[:, t], other, own, ALU.is_gt)
                            i1.then_inc(gate.sem, 1)
                            i2.then_inc(gate.sem, 1)
                            ve.wait_ge(gate.sem, g(8))
                            ve.tensor_tensor(eq[:].rearrange("p t a b -> p t (a b)"), eq[:].rearrange("p t a b -> p t (a b)"),
                                             tri[:].rearrange("p a b -> p (a b)").unsqueeze(1).to_broadcast([P, NP, NE * NE]),
                                             ALU.mult).then_inc(gate.sem, 1)
                            ve.wait_ge(gate.sem, g(9))
                            flat = lambda a: a[:].rearrange("p t a b -> p (t a b)")
                            ve.tensor_tensor(flat(gt), flat(gt), flat(eq), ALU.add).then_inc(gate.sem, 1)
                            ve.wait_ge(gate.sem, g(10))
                            ve.tensor_reduce(rank[:].rearrange("p t e -> p (t e)"), gt[:].rearrange("p t a b -> p (t a) b"),
                                             X, ALU.add).then_inc(gate.sem, 1)
                            ve.wait_ge(gate.sem, g(11))
                            ve.tensor_scalar(rank[:], rank[:], 2.0, None, ALU.is_lt).then_inc(gate.sem, 1)
                            ve.wait_ge(gate.sem, g(12))
                            ve.tensor_tensor(cwl[:], rank[:], lg[:], ALU.mult).then_inc(gate.sem, 1)
                            ve.wait_ge(gate.sem, g(13))
                            ve.tensor_scalar(cw[:, b, :], cwl[:].rearrange("p t e -> p (t e)"), 1.0 / WSCALE, None, ALU.mult)
                            ve.wait_ge(xf_ok.sem, xf_ok.at(b, 2))
                            ve.wait_ge(hi_ok.sem, hi_ok.at(b, 2))
                            ve.tensor_tensor(x16[:, b, T:2 * T], xf[:], xh[:], ALU.subtract).then_inc(lo_ok.sem, 1)
                            ve.wait_ge(b_ps.sem, b_ps.at(b, 1))
                            ve.tensor_tensor(xn[:].rearrange("p t c -> p (t c)"), banks(0, 2),
                                             t2[:].rearrange("p t c -> p (t c)"), ALU.add).then_inc(b_ok.sem, 1)
                            ve.wait_ge(b_ok.sem, b_ok.at(b, 1))
                            ve.wait_ge(lo_ok.sem, lo_ok.at(b, 1))
                            ve.sem_inc(turn_done, 1)

                    @block.tensor
                    def _(pe):
                        with pe.Fori(0, NB) as b:
                            pe.wait_ge(turn_done, b * 4)
                            pe.wait_ge(lt_in.sem, lt_in.at(b, 1))
                            for u in range(2):
                                pe.matmul(bank(u), wqkv2[:, 0:C], lt[:, 512 * u:512 * u + 512], start=True, stop=True)\
                                    .then_inc(qT_ps.sem, 1)
                            pe.wait_ge(klm_ok.sem, klm_ok.at(b, 1))
                            pe.wait_ge(klz_in.sem, klz_in.at(b, 3))

                            def scores(t):
                                if t % 4 == 0:
                                    pe.wait_ge(qT_ok.sem, qT_ok.at(b, t // 4 + 1))
                                if t >= 2:
                                    pe.wait_ge(d_ok.sem, d_ok.at(b, t - 1))
                                pe.matmul(bank(2 + t % 2), qT[:, t * P:(t + 1) * P], klm[:].rearrange("p h l -> p (h l)"),
                                          start=True, stop=True).then_inc(s_ps.sem, 1)

                            def turned(t):
                                pe.wait_ge(e_ok.sem, e_ok.at(b, t + 1))
                                if t >= 2:
                                    pe.wait_ge(eT_ok.sem, eT_ok.at(b, t - 1))
                                for h in range(4):
                                    i = pe.transpose(bank(4 + t % 2)[:, h * P:(h + 1) * P],
                                                     e1[:, t % 2, 2 * h:2 * h + 2, :].rearrange("p a l -> p (a l)"), ident[:])
                                i.then_inc(eT_ps.sem, 1)

                            def values(t):
                                pe.wait_ge(eT_ok.sem, eT_ok.at(b, t + 1))
                                if t >= 2:
                                    pe.wait_ge(on_ok.sem, on_ok.at(b, t - 1))
                                for h in range(4):
                                    w = 2 * (AD + 1)
                                    i = pe.matmul(bank(6 + t % 2)[:, w * h:w * h + w], p1T[:, t % 2, h, :],
                                                  zd[:, h].rearrange("p a d -> p (a d)"), start=True, stop=True)
                                i.then_inc(o_ps.sem, 1)

                            def merge(t):
                                pe.wait_ge(on_ok.sem, on_ok.at(b, t + 1))
                                if t == 0:
                                    pe.wait_ge(qT_ok.sem, qT_ok.at(b, 2))
                                if t >= 2:
                                    pe.wait_ge(t2_ok.sem, t2_ok.at(b, t - 1))
                                pe.transpose(bank(t % 2)[:, 0:P], on[:, t % 2, :], ident[:]).then_inc(onT_ps.sem, 1)

                            def project(t):
                                pe.wait_ge(onT_ok.sem, onT_ok.at(b, t + 1))
                                pe.matmul(bank(t % 2)[:, C:2 * C], onT[:, t % 2, :], wout[:], start=True, stop=False)
                                pe.matmul(bank(t % 2)[:, C:2 * C], lt[:, t * P:(t + 1) * P], wvc[:], start=False, stop=True)\
                                    .then_inc(w_ps.sem, 1)

                            scores(0)
                            scores(1)
                            for t in range(NP):
                                turned(t)
                                if t + 2 < NP:
                                    scores(t + 2)
                                if t >= 1:
                                    merge(t - 1)
                                values(t)
                                if t >= 1:
                                    project(t - 1)
                            merge(NP - 1)
                            project(NP - 1)
                            pe.wait_ge(d_ok.sem, d_ok.at(b, NP))
                            for t in range(NP):
                                pe.wait_ge(xn_ok.sem, xn_ok.at(b, t + 1))
                                i = pe.transpose(bank(2 + t // 4)[:, (t % 4) * P:(t % 4 + 1) * P], xn[:, t, :], ident[:])
                                if t % 4 == 3:
                                    i.then_inc(xf_ps.sem, 1)
                            for t in range(NP):
                                pe.wait_ge(xf_ok.sem, xf_ok.at(b, t // 4 + 1))
                                i = pe.matmul(bank(4)[:, NE * t:NE * t + NE], xf[:, t * P:(t + 1) * P], gw[:],
                                              start=True, stop=True)
                            i.then_inc(lg_ps.sem, 1)
                            pe.wait_ge(gate.sem, gate.at(b, 13))
                            for t in range(NP):
                                i = pe.transpose(bank(5 + t // 4)[0:NE, (t % 4) * P:(t % 4 + 1) * P], cwl[:, t, :], ident[:])
                            i.then_inc(cwT_ps.sem, 1)
                            pe.wait_ge(cwT_ok.sem, cwT_ok.at(b, 1))
                            pe.wait_ge(t2_ok.sem, t2_ok.at(b, NP))
                            for t in range(NP):
                                i = pe.matmul(bank(t // 4)[:, (t % 4) * C:(t % 4 + 1) * C], cwT[:, t * P:(t + 1) * P], b2r[:],
                                              start=True, stop=True)
                            i.then_inc(b_ps.sem, 1)
                            pe.sem_inc(turn_done, 1)

        def phase_experts(lnT):
            NC = 2 * NX * FC
            with ExitStack() as c1:
                def sb(name, shape, dt=F32):
                    return c1.enter_context(nc.sbuf_tensor(name, shape, dt))

                acc = sb("e_acc", [P, NP, C])
                g32 = sb("e_g32", [P, 4, 512])
                ghi = sb("e_ghi", [P, 4, 512], F16)
                glo = sb("e_glo", [P, 4, 512], F16)
                x16 = lnT[:].bitcast(F16)
                NG = 2 * (NE + 1)

                r_in = signal("e_r_in", 1, 16)
                h_ps = signal("e_h_ps", NC)
                g_ok = signal("e_g_ok", NC)
                ghi_a = signal("e_ghi_a", NC // 2)
                ghi_v = signal("e_ghi_v", NC // 2)
                glo_ok = signal("e_glo_ok", NC)
                y_ps = signal("e_y_ps", NC)
                acc_ok = signal("e_acc_ok", NG)
                out_ok = signal("e_out_ok", 2, 16)

                def group(c):
                    u, e = c // (NX * FC), c // FC % NX
                    return u * (NE + 1) + max(e - 1, 0)

                with nc.Block() as block:
                    @block.sync
                    def _(sp):
                        with sp.Fori(0, NB) as b:
                            sp.wait_ge(out_ok.sem, out_ok.at(b, 0))
                            apart(sp)
                            sp.dma_start(acc[:], res[b].rearrange("(t p) c -> p t c", p=P)).then_inc(r_in.sem, 16)
                            for u in range(2):
                                sp.wait_ge(acc_ok.sem, acc_ok.at(b, (u + 1) * (NE + 1)))
                                apart(sp)
                                sp.dma_start(out[b].rearrange("(t p) c -> p t c", p=P)[:, 4 * u:4 * u + 4, :],
                                             acc[:, 4 * u:4 * u + 4, :]).then_inc(out_ok.sem, 16)
                        sp.wait_ge(out_ok.sem, out_ok.at(NB, 0))

                    @block.scalar
                    def _(ac):
                        with ac.Fori(0, NB) as b:
                            for c in range(NC):
                                e, f = c // FC % NX, c % FC
                                ac.wait_ge(h_ps.sem, h_ps.at(b, c + 1))
                                ac.wait_ge(glo_ok.sem, glo_ok.at(b, c - 3) if c >= 4 else glo_ok.at(b, 0))
                                ac.activation(g32[:, c % 4, :], bank(c % 3), ACT.Gelu, bias=b1[:, e, f:f + 1],
                                              scale=1.0 / WSCALE).then_inc(g_ok.sem, 1)
                                if f < 2:
                                    ac.wait_ge(y_ps.sem, y_ps.at(b, c - 3) if c >= 4 else y_ps.at(b, 0))
                                    ac.activation(ghi[:, c % 4, :], bank(c % 3), ACT.Gelu, bias=b1[:, e, f:f + 1],
                                                  scale=1.0 / WSCALE).then_inc(ghi_a.sem, 1)

                    @block.vector
                    def _(ve):
                        with ve.Fori(0, NB) as b:
                            def add_up(n):
                                u, e = n // (NE + 1), n % (NE + 1)
                                last = (u * NX + e + 1) * FC + FC
                                ve.wait_ge(y_ps.sem, y_ps.at(b, last))
                                bk = bank(4 + n % 2)
                                if e == 0:
                                    if u == 0:
                                        ve.wait_ge(r_in.sem, r_in.at(b, 1))
                                    a = acc[:, 4 * u:4 * u + 4, :].rearrange("p t c -> p (t c)")
                                    ve.scalar_tensor_tensor(out=a, in0=bk, scalar=1.0 / WSCALE, in1=a, op0=ALU.mult,
                                                            op1=ALU.add).then_inc(acc_ok.sem, 1)
                                    return
                                ve.wait_ge(acc_ok.sem, acc_ok.at(b, n))
                                for t in range(4):
                                    tt = 4 * u + t
                                    i = ve.scalar_tensor_tensor(out=acc[:, tt, :], in0=bk[:, C * t:C * t + C],
                                                                scalar=cw[:, b, tt * NE + e - 1:tt * NE + e],
                                                                in1=acc[:, tt, :], op0=ALU.mult, op1=ALU.add)
                                i.then_inc(acc_ok.sem, 1)

                            for c in range(NC):
                                f = c % FC
                                ve.wait_ge(g_ok.sem, g_ok.at(b, c + 1))
                                ve.wait_ge(y_ps.sem, y_ps.at(b, c - 3) if c >= 4 else y_ps.at(b, 0))
                                if f >= 2:
                                    ve.tensor_copy(ghi[:, c % 4, :], g32[:, c % 4, :]).then_inc(ghi_v.sem, 1)
                                    ve.wait_ge(ghi_v.sem, ghi_v.at(b, 2 * (c // FC) + f - 1))
                                else:
                                    ve.wait_ge(ghi_a.sem, ghi_a.at(b, 2 * (c // FC) + f + 1))
                                ve.tensor_tensor(glo[:, c % 4, :], g32[:, c % 4, :], ghi[:, c % 4, :], ALU.subtract)\
                                    .then_inc(glo_ok.sem, 1)
                                if f == 3 and c // FC >= 1:
                                    done = c // FC - 1
                                    if done % NX != 0:
                                        add_up(done // NX * (NE + 1) + done % NX - 1)
                            add_up(NG - 1)

                    @block.tensor
                    def _(pe):
                        with pe.Fori(0, NB) as b:
                            def hidden(c):
                                u, e, f = c // (NX * FC), c // FC % NX, c % FC
                                if c >= 3:
                                    pe.wait_ge(g_ok.sem, g_ok.at(b, c - 2))
                                    k = c - 3
                                    if k % FC < 2:
                                        pe.wait_ge(ghi_a.sem, ghi_a.at(b, 2 * (k // FC) + k % FC + 1))
                                else:
                                    pe.wait_ge(g_ok.sem, g_ok.at(b, 0))
                                    pe.wait_ge(ghi_a.sem, ghi_a.at(b, 0))
                                w = slice(f * P, f * P + P)
                                xhi = x16[:, b, 512 * u:512 * u + 512]
                                xlo = x16[:, b, T + 512 * u:T + 512 * u + 512]
                                pe.matmul(bank(c % 3), w1hi[:, e, w], xhi, start=True, stop=False)
                                pe.matmul(bank(c % 3), w1hi[:, e, w], xlo, start=False, stop=False)
                                pe.matmul(bank(c % 3), w1lo[:, e, w], xhi, start=False, stop=True).then_inc(h_ps.sem, 1)

                            def output(c):
                                e, f = c // FC % NX, c % FC
                                n = group(c)
                                first = f == 0 and e != 1
                                if first:
                                    pe.wait_ge(acc_ok.sem, acc_ok.at(b, n - 1) if n >= 2 else acc_ok.at(b, 0))
                                pe.wait_ge(glo_ok.sem, glo_ok.at(b, c + 1))
                                for t in range(4):
                                    o = bank(4 + n % 2)[:, C * t:C * t + C]
                                    s = slice(t * P, t * P + P)
                                    pe.matmul(o, ghi[:, c % 4, s], w2hi[:, e, f, :], start=first and t == 0, stop=False,
                                              skip_group_check=True)
                                    pe.matmul(o, ghi[:, c % 4, s], w2lo[:, e, f, :], start=False, stop=False,
                                              skip_group_check=True)
                                    i = pe.matmul(o, glo[:, c % 4, s], w2hi[:, e, f, :], start=False,
                                                  stop=True, skip_group_check=True)
                                i.then_inc(y_ps.sem, 1)

                            hidden(0)
                            hidden(1)
                            for c in range(NC):
                                if c + 2 < NC:
                                    hidden(c + 2)
                                output(c)

        phase_windows()
        lnT = sb("lnT", [P, NB, T])
        with ExitStack() as c2:
            def sb2(name, shape):
                return c2.enter_context(nc.sbuf_tensor(name, shape, F32))

            klA = sb2("klA", [P, NB, LM])
            zA = sb2("zA", [P, NB, 4 * AD])
            with ExitStack() as c3:
                def sb3(name, shape):
                    return c3.enter_context(nc.sbuf_tensor(name, shape, F32))

                xA = sb3("xA", [P, NB, 4 * LM])
                xTA = sb3("xTA", [LM, NB, 4 * P])
                yA = sb3("yA", [P, NB, 4 * AD])
                stR = sb3("stR", [P, NB, 4])
                stC = sb3("stC", [LM, NB, AH])
                phase_landmarks(lnT, klA, xA, xTA, yA, stR, stC)
                phase_pinv(xA, xTA, yA, zA, stR, stC)
            phase_mix(lnT, klA, zA)
        phase_experts(lnT)


def host_arrays(inp):
    rel, mask, sel, _, _ = window_constants()
    f = lambda a: np.ascontiguousarray(a)
    rows = lambda a, *s: f(np.broadcast_to(np.reshape(a, (1, *s)), (P, *s)))
    I = {k: np.asarray(v) for k, v in inp.items()}
    L0 = lambda k: I["L0_conv_" + k]
    w1 = np.concatenate([I["L1_ffn_sw1"], I["L1_ffn_rw1"]])
    w2 = np.concatenate([I["L1_ffn_sw2"], I["L1_ffn_rw2"]])
    bb = np.concatenate([I["L1_ffn_sb1"], I["L1_ffn_rb1"]])
    kernel_w = I["L1_attn_conv_w"][:, 0]
    hh, cc = np.meshgrid(np.arange(AH), np.arange(AD), indexing="ij")
    hh, cc = hh.reshape(-1), cc.reshape(-1)
    convT = kernel_w[hh[None, :] - hh[:, None] + 16, cc[None, :] % 2, cc[:, None]]
    convmask = (cc[None, :] // 2 == cc[:, None] // 2).astype(np.float32)
    headmask = np.zeros((P, AH), np.float32)
    headmask[np.arange(P), hh] = 0.25
    i64 = np.concatenate([np.eye(LM, dtype=np.float32)] * 2)
    wqkv2 = I["L1_attn_Wqkv"]
    return {
        "x": f(I["x"]).reshape(-1, T, C),
        "ident": np.eye(P, dtype=np.float32), "ident16": np.eye(P, dtype=np.float16),
        "i64": i64, "tri": rows(np.tril(np.ones((NE, NE), np.float32), -1), NE, NE), "wqkv2": f(wqkv2), "wvT": f(wqkv2[:, 2 * C:].T), "wout": f(I["L1_attn_Wout"]),
        "bout": rows(I["L1_attn_bout"], C), "gw": f(I["L1_ffn_gate_w"].T), "gb": rows(I["L1_ffn_gate_b"], NE),
        "b2r": f(I["L1_ffn_rb2"]), "b2s": rows(I["L1_ffn_sb2"], 2, C), "headmask": headmask,
        "b1": f(bb.reshape(NX, FC, P).transpose(2, 0, 1)), "convT": f(convT), "convmask": convmask,
        "w1": f(w1.transpose(2, 0, 1)).reshape(P, NX * F),
        "w2": f(w2.reshape(NX, C, FC, P).transpose(3, 0, 2, 1)).reshape(P, NX * F),
        "wqkT": f(L0("qkv_w").T), "qb": rows(np.concatenate([L0("q_bias"), np.zeros_like(L0("q_bias"))]), 2 * C),
        "projT": f(L0("proj_w").T), "projb": rows(L0("proj_b"), C),
        "vbcol": f(np.broadcast_to(L0("v_bias")[:, None], (C, P))),
        "g1": rows(L0("norm1_g"), C), "be1": rows(L0("norm1_b"), C),
        "g2": rows(L0("norm2_g"), C), "be2": rows(L0("norm2_b"), C),
        "f1T": f(L0("fc1_w").T), "f1b": f(L0("fc1_b").reshape(FC, P).T),
        "f2T": f(L0("fc2_w").T.reshape(FC, P, C).transpose(1, 0, 2)), "f2b": rows(L0("fc2_b"), C),
        "ls": rows(L0("logit_scale").reshape(NH), NH), "cpw1": f(L0("cpb_w1").T), "cpb1": f(L0("cpb_b1")[:, None]),
        "cpw2": f(L0("cpb_w2").T), "rel": rel, "mask": mask, "sel": sel,
    }


def kernel(**inputs):
    import concourse.bacc as bacc
    from concourse.bass_utils import run_bass_kernel_spmd

    nc = bacc.Bacc("TRN2", target_bir_lowering=False, num_devices=1)
    arrays = {f"in_{k}": a for k, a in host_arrays(inputs).items()}
    A = {k[3:]: nc.dram_tensor(k, a.shape, mybir.dt.from_np(a.dtype), kind="ExternalInput").ap()
         for k, a in arrays.items()}
    NB = arrays["in_x"].shape[0]
    out = nc.dram_tensor("out_dram", (NB, T, C), F32, kind="ExternalOutput").ap()
    build(nc, NB, A, out)
    r = run_bass_kernel_spmd(nc, [arrays], core_ids=[0])
    return r.results[0]["out_dram"].reshape(NB, HW, HW, C)
```

```python
from contextlib import ExitStack
import math

import numpy as np

import concourse.bass as bass
from concourse import mybir

F32 = mybir.dt.float32
F16 = mybir.dt.float16
ALU = mybir.AluOpType
ACT = mybir.ActivationFunctionType
X = mybir.AxisListType.X

C = 128
P = 128
HW = 32
WS, SS = 8, 4
N = WS * WS
T = HW * HW
NP = T // P
NH, HD = 16, 8
AH, AD = 8, 16
LM = 64
SEG = T // LM
F = 512
NE = 8
NX = 10
FC = F // P
WSCALE = 64.0
ITERS = 6
LOADED = 16 * 34


class Signal:

    def __init__(self, sem, per, by=1):
        self.sem, self.per, self.by = sem, per, by

    def at(self, turn, n):
        return turn * (self.per * self.by) + n * self.by


def window_constants():
    r = np.arange(-(WS - 1), WS, dtype=np.float32)
    tab = np.stack(np.meshgrid(r, r, indexing="ij"), axis=-1) / (WS - 1) * 8.0
    tab = (np.sign(tab) * np.log2(np.abs(tab) + 1.0) / np.log2(8.0)).astype(np.float32)
    rel = np.ascontiguousarray(tab.reshape(-1, 2).T)
    ch, rr, cc = np.meshgrid(np.arange(2), np.arange(WS), np.arange(4), indexing="ij")
    y, x = rr.reshape(-1), (4 * ch + cc).reshape(-1)
    img = np.zeros((HW, HW), np.float32)
    cnt = 0
    for hs in (slice(0, -WS), slice(-WS, -SS), slice(-SS, None)):
        for ws in (slice(0, -WS), slice(-WS, -SS), slice(-SS, None)):
            img[hs, ws] = cnt
            cnt += 1
    mask = np.zeros((P, 4, N), np.float32)
    for kind in range(4):
        wy, half = (3 if kind >= 2 else 0), kind % 2
        for w in range(2):
            m = img[8 * wy + y, 8 * (2 * half + w) + x]
            mask[64 * w:64 * w + 64, kind] = np.where(m[None, :] != m[:, None], -100.0, 0.0)
    sel = np.zeros((NH, NH, N), np.float16)
    for i in range(NH):
        sel[i, i] = 1.0
    return rel, mask, sel.reshape(NH, NH * N), y, x


def build(nc, NB, A, out):
    _, _, _, KY, KX = window_constants()
    with ExitStack() as ctx:
        def sb(name, shape, dt=F32):
            return ctx.enter_context(nc.sbuf_tensor(name, shape, dt))

        phase_sems = []

        def sem(name):
            phase_sems.append(nc.alloc_semaphore(name))
            return phase_sems[-1]

        def phase_ends():
            nc.clear_and_free_semaphores(phase_sems)
            phase_sems.clear()
            nc.all_engine_barrier()

        def signal(name, per, by=1):
            return Signal(sem(name), per, by)

        mid = nc.dram_tensor("mid_dram", [NB, T, C], F32).ap()
        res = nc.dram_tensor("res_dram", [NB, T, C], F32).ap()
        psum = ctx.enter_context(nc.psum_tensor("psum", [P, 8 * 512], F32))

        def apart(eng):
            eng.sem_inc(s_apart, 1)

        def banks(i, n):
            return psum[:, 512 * i:512 * (i + n)]

        def bank(i):
            return banks(i, 1)

        ident = sb("ident", [P, P])
        ident16 = sb("ident16", [P, P], F16)
        w1hi = sb("w1hi", [P, NX, F], F16)
        w1lo = sb("w1lo", [P, NX, F], F16)
        w2hi = sb("w2hi", [P, NX, FC, C], F16)
        w2lo = sb("w2lo", [P, NX, FC, C], F16)
        b1 = sb("b1", [P, NX, FC])
        cw = sb("cw", [P, NB, NP * NE])
        wqkv2 = sb("wqkv2", [P, 3 * C])
        wvc = sb("wvc", [P, C])
        wout = sb("wout", [P, C])
        bout = sb("bout", [P, C])
        gw = sb("gw", [P, NE])
        gb = sb("gb", [P, NE])
        b2r = sb("b2r", [NE, C])
        b2s = sb("b2s", [P, 2, C])
        headmask = sb("headmask", [P, AH])
        nhalf = sb("nhalf", [P, NP * 32])
        ones1 = sb("ones1", [1, P])

        s_load = sem("s_load")
        s_apart = sem("s_apart")
        phase_sems.clear()

        def phase_setup(c1, W):
            with ExitStack() as c2:
                def sb(name, shape, dt=F32):
                    return c2.enter_context(nc.sbuf_tensor(name, shape, dt))

                def keep(name, shape, dt=F32):
                    W[name] = c1.enter_context(nc.sbuf_tensor(name, shape, dt))
                    return W[name]

                wqkT = keep("wqkT", [P, 3 * C])
                qb = keep("qb", [P, 2 * C])
                projT = keep("projT", [P, C])
                projb = keep("projb", [P, C])
                g1, be1, g2, be2 = (keep(n, [P, C]) for n in ("g1", "be1", "g2", "be2"))
                f1T = keep("f1T", [P, F])
                f1b = keep("f1b", [P, FC])
                f2T = keep("f2T", [P, FC, C])
                f2b = keep("f2b", [P, C])
                sc = keep("sc", [P, NH])
                sel = keep("sel", [NH, NH * N], F16)
                bth = keep("bth", [P, 4, 4, 4, N], F16)
                btl = keep("btl", [P, 4, 4, 4, N], F16)
                vbcol = sb("vbcol", [P, P])
                cpw1 = sb("cpw1", [2, P])
                cpb1 = sb("cpb1", [P, 1])
                cpw2 = sb("cpw2", [P, NH])
                rel = sb("rel", [2, 225])
                relh = sb("relh", [P, 15, 15])
                relx = sb("relx", [P, 12, 15, 4])
                sig = sb("sig", [P, N, NH])
                mask = sb("mask", [P, 4, N])
                btmp = sb("btmp", [P, 2, 4, N])
                cm = sb("cm", [P, 4, C])

                loads = [(ident, "ident"), (ident16, "ident16"), (wqkv2, "wqkv2"), (wout, "wout"), (bout, "bout"),
                         (gw, "gw"), (gb, "gb"), (b2r, "b2r"), (b2s, "b2s"), (headmask, "headmask"), (b1, "b1"),
                         (wqkT, "wqkT"), (qb, "qb"), (projT, "projT"), (projb, "projb"), (vbcol, "vbcol"),
                         (g1, "g1"), (be1, "be1"), (g2, "g2"), (be2, "be2"), (f1T, "f1T"), (f1b, "f1b"),
                         (f2T, "f2T"), (f2b, "f2b"), (sc, "ls"), (cpw1, "cpw1"), (cpb1, "cpb1"), (cpw2, "cpw2"),
                         (rel, "rel"), (mask, "mask"), (sel, "sel")]
                stage = sb("stage", [P, NX * F])
                assert LOADED == 16 * (len(loads) + 3)

                s_w = sem("s_w")
                s_wdone = sem("s_wdone")
                s_pe = sem("s_pe")
                s_ac = sem("s_ac")
                s_ve = sem("s_ve")
                s_po = sem("s_po")
                s_rel = sem("s_rel")
                with nc.Block() as block:
                    @block.sync
                    def _(sp):
                        for dst, name in loads:
                            sp.dma_start(dst[:], A[name]).then_inc(s_load, 16)
                        sp.dma_start(cm[:, 0, :], A["convT"]).then_inc(s_load, 16)
                        sp.dma_start(cm[:, 1, :], A["convmask"]).then_inc(s_load, 16)
                        sp.dma_start(cm[:, 2, :], A["wvT"]).then_inc(s_load, 16)
                        sp.dma_start(stage[:], A["w1"]).then_inc(s_w, 16)
                        sp.wait_ge(s_wdone, 2)
                        sp.dma_start(stage[:], A["w2"]).then_inc(s_w, 16)

                    @block.gpsimd
                    def _(gp):
                        gp.memset(nhalf[:], -0.5).then_inc(s_po, 1)
                        gp.memset(ones1[:], 1.0).then_inc(s_po, 1)
                        gp.wait_ge(s_ac, 2)
                        for i in range(12):
                            gp.tensor_copy(relx[:, i], relh[:, :, i:i + 4]).then_inc(s_rel, 1)

                    @block.scalar
                    def _(ac):
                        ac.wait_ge(s_ve, 1)
                        ac.activation(sc[:], sc[:], ACT.Exp).then_inc(s_ac, 1)
                        ac.wait_ge(s_pe, 1)
                        ac.activation(relh[:].rearrange("q a b -> q (a b)"), bank(0)[:, 0:225], ACT.Relu,
                                      bias=cpb1[:, 0:1]).then_inc(s_ac, 1)
                        ac.wait_ge(s_pe, 2)
                        for i in range(2):
                            ac.activation(sig[:, 32 * i:32 * i + 32, :].rearrange("q m h -> q (m h)"), bank(1 + i)[:, :],
                                          ACT.Sigmoid).then_inc(s_ac, 1)
                        ac.wait_ge(s_pe, 5)
                        ac.activation(wvc[:], bank(3)[:, 0:C], ACT.Copy).then_inc(s_ac, 1)

                    @block.vector
                    def _(ve):
                        ve.wait_ge(s_load, LOADED)
                        ve.tensor_scalar(sc[:], sc[:], math.log(100.0), None, ALU.min).then_inc(s_ve, 1)
                        ve.tensor_tensor(cm[:, 0, :], cm[:, 0, :], cm[:, 1, :], ALU.mult).then_inc(s_ve, 1)
                        ve.tensor_tensor(b2s[:, 0, :], b2s[:, 0, :], b2s[:, 1, :], ALU.add).then_inc(s_ve, 1)
                        ve.wait_ge(s_pe, 4)
                        ve.tensor_copy(cm[:, 3, :], bank(4)[:, 0:C]).then_inc(s_ve, 1)
                        ve.tensor_tensor(projb[:], projb[:], bank(5)[:, 0:C], ALU.add).then_inc(s_ve, 1)
                        n = 5
                        ve.wait_ge(s_ac, 4)
                        k = 0
                        for kind in range(4):
                            for j in range(4):
                                t = btmp[:, k % 2]
                                src = sig[:].rearrange("q m (g j) -> q g m j", j=4)[:, :, :, j]
                                ve.scalar_tensor_tensor(out=t, in0=src, scalar=16.0,
                                                        in1=mask[:, kind, :].unsqueeze(1).to_broadcast([P, 4, N]),
                                                        op0=ALU.mult, op1=ALU.add).then_inc(s_ve, 1)
                                n += 1
                                ve.wait_ge(s_ve, n)
                                ve.tensor_copy(bth[:, kind, j], t).then_inc(s_ve, 1)
                                n += 1
                                ve.wait_ge(s_ve, n)
                                ve.tensor_tensor(btl[:, kind, j], t, bth[:, kind, j], ALU.subtract).then_inc(s_ve, 1)
                                n += 1
                                k += 1
                                ve.wait_ge(s_ve, n)
                        wd = 0
                        for which, (hi, lo) in enumerate(((w1hi, w1lo), (w2hi, w2lo))):
                            ve.wait_ge(s_w, 16 * which + 16)
                            src = stage[:]
                            hi2 = hi[:].rearrange("p a b -> p (a b)") if not which else hi[:].rearrange("p a b c -> p (a b c)")
                            lo2 = lo[:].rearrange("p a b -> p (a b)") if not which else lo[:].rearrange("p a b c -> p (a b c)")
                            ve.tensor_scalar(hi2, src, WSCALE, None, ALU.mult).then_inc(s_wdone, 1)
                            wd += 1
                            ve.wait_ge(s_wdone, wd)
                            ve.scalar_tensor_tensor(out=lo2, in0=src, scalar=WSCALE, in1=hi2, op0=ALU.mult,
                                                    op1=ALU.subtract).then_inc(s_wdone, 1)
                            wd += 1

                    @block.tensor
                    def _(pe):
                        pe.wait_ge(s_load, LOADED)
                        pe.matmul(bank(0)[:, 0:225], cpw1[:], rel[:], start=True, stop=True).then_inc(s_pe, 1)
                        pe.wait_ge(s_rel, 12)
                        for m in range(N):
                            ky, kx = int(KY[m]), int(KX[m])
                            for half in range(2):
                                for c in range(2):
                                    w = relx[:, 7 - kx + 4 * c, 7 - ky:15 - ky, :].rearrange("q a b -> q (a b)")
                                    i = pe.matmul(bank(1 + m // 32)[64 * half + 32 * c:64 * half + 32 * c + 32,
                                                                    (m % 32) * NH:(m % 32 + 1) * NH],
                                                  w, cpw2[:], start=True, stop=True)
                        i.then_inc(s_pe, 1)
                        pe.wait_ge(s_ve, 3)
                        pe.matmul(bank(4)[:, 0:C], cm[:, 0, :], wout[:], start=True, stop=True)
                        pe.matmul(bank(5)[:, 0:C], vbcol[:], projT[:], start=True, stop=True).then_inc(s_pe, 2)
                        pe.wait_ge(s_ve, 5)
                        pe.matmul(bank(3)[:, 0:C], cm[:, 2, :], cm[:, 3, :], start=True, stop=True).then_inc(s_pe, 1)

        def phase_windows(c1, W):
            I32 = mybir.dt.int32

            def sb(name, shape, dt=F32):
                return c1.enter_context(nc.sbuf_tensor(name, shape, dt))

            wqkT, qb, projT, projb, g1, be1, g2, be2, f1T, f1b, f2T, f2b, sel, bth, btl, sc = (
                W[k] for k in "wqkT qb projT projb g1 be1 g2 be2 f1T f1b f2T f2b sel bth btl sc".split())
            xw = sb("xw", [P, NP, C])
            xT = sb("xT", [P, 2, P])
            qk = sb("qk", [P, 2, 2, NH, HD])
            sq = sb("sq", [P, 2, 2 * C])
            nrm = sb("nrm", [P, 2, 2, NH])
            rsq = sb("rsq", [P, 2, 2 * NH])
            split = sb("split", [P, 2, 2, NH, 4, HD], F16)
            qkT = sb("qkT", [P, 2, 2, 4, P], F16)
            vd = sb("vd", [P, 2, 2, NH, HD + 1])
            mx = sb("mx", [P, NH])
            mT = sb("mT", [NH, P], F16)
            pr = sb("pr", [P, 2, 16, N])
            prT = sb("prT", [P, 2, 8, P])
            rs = sb("rs", [P, NH])
            on = sb("on", [P, 2, C])
            onT = sb("onT", [P, 2, P])
            y = sb("y", [P, 4, C])
            st = sb("st", [P, 4, 6])
            mv = sb("mv", [P, 4, 2])
            rstd = sb("rstd", [P, 4])
            x1 = sb("x1", [P, NP, C])
            x1T = sb("x1T", [P, 2, 4 * P])
            gl = sb("gl", [P, FC, 4 * P])
            z = sb("z", [P, 4, C])
            zt = sb("zt", [P, 4, 6])
            zv = sb("zv", [P, 4, 2])
            zr = sb("zr", [P, 4])
            xo = sb("xo", [P, 4, C])

            beside = psum[:, 0:4 * 512].rearrange("q (j c) -> q j c", j=4)
            heads, turned = beside[:, :, 0:256], beside[:, :, 256:512]
            psig = lambda name, per=1, by=1: signal("w_" + name, per, by)
            x_in = [psig(f"x_in{p}", 1, 16) for p in range(NP)]
            stored = [psig(f"stored{p}", 1, 16) for p in range(4)]
            ready = sem("w_ready")
            (xT_ps, xT_ok, qk_ps, qk_ok, sq_ok, ss_ok, rsq_ok, v_ps, v_ok, qn_ok, qkT_ps, qkT_ok, s_ps, mx_ok,
             mT_ps, mT_ok, sm_ps, pr_ok, prT_ps, prT_a, prT_v, o_ps, rs_ok, on_ok, onT_ps, onT_ok, pj_ps, y_ok, st_ok,
             mv_ok, ve_ok, rstd_ok, yn_ok, yg_ok, x1_ok, x1T_ps, x1T_ok, m_ps, z_ok, zt_ok, zv_ok, ze_ok,
             zr_ok, zn_ok, zg_ok, xo_ok) = (psig(k) for k in (
                 "xT_ps xT_ok qk_ps qk_ok sq_ok ss_ok rsq_ok v_ps v_ok qn_ok qkT_ps qkT_ok s_ps mx_ok "
                 "mT_ps mT_ok sm_ps pr_ok prT_ps prT_a prT_v o_ps rs_ok on_ok onT_ps onT_ok pj_ps y_ok st_ok "
                 "mv_ok ve_ok rstd_ok yn_ok yg_ok x1_ok x1T_ps x1T_ok m_ps z_ok zt_ok zv_ok ze_ok "
                 "zr_ok zn_ok zg_ok xo_ok").split())
            hi_ok, lo_ok = psig("hi_ok", 2), psig("lo_ok", 2)
            newton = psig("newton", 11)
            be_ok, bf_ok = psig("be_ok"), psig("bf_ok")
            h_ps, gl_ok = psig("h_ps"), psig("gl_ok")

            class Pair:

                def __init__(self, b, p):
                    if isinstance(b, int):
                        b, p = b + p // NP, p % NP
                    else:
                        b, p = (b + p // NP if p // NP else b), p % NP
                    self.b, self.p = b, p

                def real(self):
                    return not isinstance(self.b, int) or 0 <= self.b < NB

                def __add__(self, d):
                    return Pair(self.b, self.p + d)

                def __sub__(self, d):
                    return self + -d

            def met(eng, s, q, n=1):
                if q.real():
                    eng.wait_ge(s.sem, (s.per * s.by) * NP * q.b + s.by * (s.per * q.p + n))

            def landed(eng, q):
                eng.wait_ge(x_in[q.p].sem, 16 * PIECES[q.p] * (q.b + 1))

            def written(eng, q):
                if q.real():
                    k = q.p % 4
                    eng.wait_ge(stored[k].sem, 16 * (PIECES[k] + PIECES[k + 4]) * q.b
                                + 16 * (PIECES[k] + (PIECES[k + 4] if q.p >= 4 else 0)))

            PIECES = [4] * 6 + [8] * 2

            def pieces(q, dram):
                img = dram[q.b].rearrange("(y x) c -> y x c", y=HW)
                wy = q.p // 2
                for w in range(2):
                    for ch in range(2):
                        x0 = (WS * (2 * (q.p % 2) + w) + 4 * ch + SS) % HW
                        q0 = 64 * w + 32 * ch
                        if wy < 3:
                            yield q0, 32, img[8 * wy + SS:8 * wy + SS + 8, x0:x0 + 4, :]
                        else:
                            yield q0, 16, img[28:32, x0:x0 + 4, :]
                            yield q0 + 16, 16, img[0:4, x0:x0 + 4, :]

            def outputs_of(s):
                g = {3: (s - 7, (0, 1)), 0: (s - 8, (2,)), 1: (s - 9, (3,))}.get(s.p % 4)
                return [g[0] + r for r in g[1]] if g else []

            def hidden_of(s):
                return s - 6 if s.p % 4 == 2 else None

            def slots(eng, body):
                for s in range(-2, NP * min(2, NB - 1)):
                    body(Pair(0, s))
                if NB > 3:
                    with eng.Fori(2, NB - 1) as b:
                        for s in range(NP):
                            body(Pair(b, s))
                for s in range(NP):
                    body(Pair(NB - 1, s))
                for s in range(NP + 3):
                    body(Pair(NB, s))

            with nc.Block() as block:
                @block.sync
                def _(sp):
                    def load(q):
                        if q.real():
                            met(sp, x1_ok, q - 8)
                            apart(sp)
                            for q0, n, src in pieces(q, A["x"]):
                                sp.dma_start(xw[q0:q0 + n, q.p, :], src).then_inc(x_in[q.p].sem, 16)

                    for p in range(3):
                        load(Pair(0, p))

                    def slot(s):
                        load(s + 5)
                        for q in outputs_of(s - 1):
                            if q.real():
                                met(sp, xo_ok, q)
                                apart(sp)
                                for q0, n, dst in pieces(q, mid):
                                    sp.dma_start(dst, xo[q0:q0 + n, q.p % 4, :]).then_inc(stored[q.p % 4].sem, 16)

                    slots(sp, slot)
                    for p in range(4, NP):
                        written(sp, Pair(NB - 1, p))

                @block.gpsimd
                def _(gp):
                    k = 2
                    gp.memset(vd[:], 0.0).then_inc(ready, 1)
                    gp.memset(split[:], 0.0).then_inc(ready, 1)
                    for p in range(2):
                        for w in range(2):
                            v = vd[:, p, w].rearrange("q (t k j) d -> q t k j d", t=2, k=2)
                            for t in range(2):
                                for half in range(2):
                                    gp.wait_ge(ready, k)
                                    gp.memset(v[64 * half:64 * half + 64, t, half, :, HD:HD + 1], 1.0).then_inc(ready, 1)
                                    k += 1
                    gp.wait_ge(ready, k)

                    def slot(s):
                        q = s - 2
                        if q.real():
                            met(gp, rstd_ok, q)
                            met(gp, yn_ok, q)
                            yp = y[:, q.p % 4, :]
                            gp.tensor_tensor(yp, yp, g1[:], ALU.mult).then_inc(yg_ok.sem, 1)
                            met(gp, yg_ok, q)
                            gp.tensor_tensor(yp, yp, be1[:], ALU.add).then_inc(be_ok.sem, 1)
                        q = s + 2
                        if q.real():
                            met(gp, qk_ok, q)
                            met(gp, ss_ok, q - 2)
                            q2 = qk[:, q.p % 2].rearrange("q a h d -> q (a h d)")
                            gp.tensor_tensor(sq[:, q.p % 2, :], q2, q2, ALU.mult).then_inc(sq_ok.sem, 1)
                        for q in outputs_of(s - 1):
                            if q.real():
                                met(gp, zn_ok, q)
                                zp = z[:, q.p % 4, :]
                                gp.tensor_tensor(zp, zp, g2[:], ALU.mult).then_inc(zg_ok.sem, 1)
                                met(gp, zg_ok, q)
                                gp.tensor_tensor(zp, zp, be2[:], ALU.add).then_inc(bf_ok.sem, 1)
                        for q in outputs_of(s):
                            if q.real():
                                met(gp, ze_ok, q)
                                r = zr[:, q.p % 4:q.p % 4 + 1]
                                gp.tensor_tensor(r, r, nhalf[:, 0:1], ALU.pow).then_inc(zr_ok.sem, 1)
                        q = s - 1
                        if q.real():
                            met(gp, ve_ok, q)
                            r = rstd[:, q.p % 4:q.p % 4 + 1]
                            gp.tensor_tensor(r, r, nhalf[:, 0:1], ALU.pow).then_inc(rstd_ok.sem, 1)

                    slots(gp, slot)

                @block.scalar
                def _(ac):
                    ac.wait_ge(ready, 18)

                    def hidden(s, f):
                        q0 = hidden_of(s)
                        if q0 is not None and q0.real():
                            if f == 0:
                                met(ac, m_ps, q0 - 1)
                            met(ac, h_ps, q0 + f)
                            ac.activation(gl[:, f, :], bank(7), ACT.Gelu, bias=f1b[:, f:f + 1]).then_inc(gl_ok.sem, 1)

                    def slot(s):
                        if s.real():
                            met(ac, mT_ps, s)
                            ac.activation(mT[:], bank(5)[0:NH, 384:512], ACT.Copy, scale=-1.0).then_inc(mT_ok.sem, 1)
                            met(ac, sm_ps, s)
                            met(ac, prT_ps, s - 2)
                            ac.activation(pr[:, s.p % 2].rearrange("q (j g) m -> q j (g m)", j=4), heads, ACT.Exp)\
                                .then_inc(pr_ok.sem, 1)
                        q = s + 2
                        if q.real():
                            met(ac, xT_ps, q)
                            met(ac, v_ps, q - 2)
                            ac.activation(xT[:, q.p % 2, :], bank(5)[:, 0:P], ACT.Copy).then_inc(xT_ok.sem, 1)
                        q = s + 1
                        if q.real():
                            met(ac, qn_ok, q)
                            met(ac, qkT_ps, q - 2)
                            for a in range(2):
                                dst = split[:, q.p % 2, a, :, 0:2 + a:1 + a, :]
                                ac.activation(dst, qk[:, q.p % 2, a].unsqueeze(2).to_broadcast([P, NH, 2, HD]), ACT.Copy)\
                                    .then_inc(hi_ok.sem, 1)
                            met(ac, v_ps, q)
                            met(ac, o_ps, q - 2)
                            for k in range(2):
                                src = bank(6)[64 * k:64 * k + 64, 0:2 * C].rearrange("q (u k j d) -> q u k j d", u=4, k=2, j=4)
                                dst = vd[64 * k:64 * k + 64, q.p % 2].rearrange("q w (t k j) d -> q (w t) k j d", t=2, k=2)
                                i = ac.activation(dst[:, :, k, :, 0:HD], src[:, :, k], ACT.Copy)
                            i.then_inc(v_ok.sem, 1)
                        if s.real():
                            met(ac, prT_ps, s)
                            met(ac, o_ps, s - 2)
                            ac.activation(prT[:, s.p % 2, 0:4, :].rearrange("q (j k) t -> q j (k t)", j=2), turned[:, 0:2, :],
                                          ACT.Copy).then_inc(prT_a.sem, 1)
                        if q.real():
                            met(ac, qkT_ps, q)
                            met(ac, s_ps, q - 2)
                            ac.activation(qkT[:, q.p % 2].rearrange("q a g t -> q (a g t)"), bank(6).bitcast(F16), ACT.Copy)\
                                .then_inc(qkT_ok.sem, 1)
                        hidden(s, 0)
                        hidden(s, 1)
                        hidden(s, 2)
                        q = s - 1
                        if q.real():
                            met(ac, onT_ps, q)
                            met(ac, pj_ps, q - 2)
                            ac.activation(onT[:, q.p % 2, :], bank(5)[:, 384:512], ACT.Copy).then_inc(onT_ok.sem, 1)
                        q = s - 2
                        if q.real():
                            met(ac, x1T_ps, q)
                            if q.p % 4 == 0:
                                met(ac, h_ps, q - 5)
                            ac.activation(x1T[:, q.p // 4, (q.p % 4) * P:(q.p % 4 + 1) * P], bank(6)[:, 0:P], ACT.Copy)\
                                .then_inc(x1T_ok.sem, 1)
                        hidden(s, 3)

                    slots(ac, slot)

                @block.vector
                def _(ve):
                    def rsqrt(q):
                        k = [0]

                        def done(i):
                            i.then_inc(newton.sem, 1)
                            k[0] += 1
                            met(ve, newton, q, k[0])

                        v = nrm[:, q.p % 2].rearrange("q a h -> q (a h)")
                        g, t = rsq[:, 0, :], rsq[:, 1, :]
                        done(ve.tensor_scalar(v, v, 1e-24, None, ALU.max))
                        done(ve.tensor_scalar(g.bitcast(I32), v.bitcast(I32), -0.5, float(0x5F3759DF), ALU.mult, ALU.add))
                        for it in range(3):
                            done(ve.tensor_tensor(t, g, g, ALU.mult))
                            done(ve.scalar_tensor_tensor(out=t, in0=t, scalar=-0.5, in1=v, op0=ALU.mult, op1=ALU.mult))
                            i = ve.scalar_tensor_tensor(out=(g, g, v)[it], in0=t, scalar=1.5, in1=g, op0=ALU.add, op1=ALU.mult)
                            if it < 2:
                                done(i)
                        i.then_inc(rsq_ok.sem, 1)

                    def slot(s):
                        q = s
                        if q.real():
                            met(ve, s_ps, q)
                            met(ve, mT_ps, q - 1)
                            ve.tensor_reduce(mx[:].rearrange("q (j g) -> q j g", j=4),
                                             heads.rearrange("q j (g m) -> q j g m", g=4), X, ALU.max).then_inc(mx_ok.sem, 1)
                        q = s + 1
                        if q.real():
                            met(ve, rsq_ok, q)
                            nq = nrm[:, q.p % 2]
                            ve.tensor_tensor(nq[:, 0, :], nq[:, 0, :], sc[:], ALU.mult).then_inc(newton.sem, 1)
                            met(ve, newton, q, 11)
                            q3 = qk[:, q.p % 2].rearrange("q a h d -> q (a h) d")
                            ve.tensor_tensor(q3, q3, nq.rearrange("q a h -> q (a h)").unsqueeze(2)
                                             .to_broadcast([P, 2 * NH, HD]), ALU.mult).then_inc(qn_ok.sem, 1)
                        q = s - 2
                        if q.real():
                            met(ve, rstd_ok, q)
                            k = q.p % 4
                            ve.tensor_scalar(y[:, k, :], y[:, k, :], mv[:, k, 0:1], rstd[:, k:k + 1],
                                             ALU.subtract, ALU.mult).then_inc(yn_ok.sem, 1)
                        q = s + 2
                        if q.real():
                            met(ve, qk_ps, q)
                            q2 = qk[:, q.p % 2].rearrange("q a h d -> q (a h d)")
                            met(ve, lo_ok, q - 2, 2)
                            ve.tensor_tensor(q2, bank(5)[:, P:P + 2 * C], qb[:], ALU.add).then_inc(qk_ok.sem, 1)
                        q = s + 1
                        if q.real():
                            met(ve, hi_ok, q, 2)
                            for a in range(2):
                                ve.tensor_tensor(split[:, q.p % 2, a, :, 2 - a, :], qk[:, q.p % 2, a],
                                                 split[:, q.p % 2, a, :, 0, :], ALU.subtract).then_inc(lo_ok.sem, 1)
                        if s.real():
                            met(ve, prT_ps, s)
                            met(ve, o_ps, s - 2)
                            ve.tensor_copy(prT[:, s.p % 2, 4:8, :].rearrange("q (j k) t -> q j (k t)", j=2),
                                           turned[:, 2:4, :]).then_inc(prT_v.sem, 1)
                        q = s - 2
                        if q.real():
                            met(ve, be_ok, q)
                            ve.tensor_tensor(x1[:, q.p, :], y[:, q.p % 4, :], xw[:, q.p, :], ALU.add).then_inc(x1_ok.sem, 1)
                        q = s + 2
                        if q.real():
                            met(ve, sq_ok, q)
                            ve.tensor_reduce(nrm[:, q.p % 2].rearrange("q a h -> q (a h)"),
                                             sq[:, q.p % 2].rearrange("q (h d) -> q h d", d=HD), X, ALU.add)\
                                .then_inc(ss_ok.sem, 1)
                        for q in outputs_of(s - 1):
                            if q.real():
                                k = q.p % 4
                                met(ve, zr_ok, q)
                                ve.tensor_scalar(z[:, k, :], z[:, k, :], zv[:, k, 0:1], zr[:, k:k + 1],
                                                 ALU.subtract, ALU.mult).then_inc(zn_ok.sem, 1)
                        q = s + 2
                        if q.real():
                            met(ve, ss_ok, q)
                            rsqrt(q)
                        for q in outputs_of(s):
                            if q.real():
                                k = q.p % 4
                                met(ve, m_ps, outputs_of(s)[-1])
                                c = 0 if k in (0, 2, 3) else C
                                ve.tensor_tensor(z[:, k, :], bank(7)[:, c:c + C], f2b[:], ALU.add).then_inc(z_ok.sem, 1)
                                met(ve, z_ok, q)
                                ve.bn_stats(zt[:, k, :], z[:, k, :]).then_inc(zt_ok.sem, 1)
                                met(ve, zt_ok, q)
                                apart(ve)
                                ve.bn_aggr(zv[:, k, :], zt[:, k, :]).then_inc(zv_ok.sem, 1)
                                met(ve, zv_ok, q)
                                ve.tensor_scalar(zr[:, k:k + 1], zv[:, k, 1:2], 1e-5, None, ALU.add).then_inc(ze_ok.sem, 1)
                        for q in outputs_of(s - 1):
                            if q.real():
                                k = q.p % 4
                                met(ve, bf_ok, q)
                                written(ve, q - 4)
                                ve.tensor_tensor(xo[:, k, :], z[:, k, :], x1[:, q.p, :], ALU.add).then_inc(xo_ok.sem, 1)
                        if s.real():
                            met(ve, o_ps, s)
                            met(ve, onT_ps, s - 2)
                            o = bank(4)[:, 0:NH * (HD + 1)].rearrange("q (h d) -> q h d", d=HD + 1)
                            ve.reciprocal(rs[:], o[:, :, HD]).then_inc(rs_ok.sem, 1)
                            met(ve, rs_ok, s)
                            ve.tensor_tensor(on[:, s.p % 2, :].rearrange("q (h d) -> q h d", d=HD), o[:, :, 0:HD],
                                             rs[:].unsqueeze(2).to_broadcast([P, NH, HD]), ALU.mult).then_inc(on_ok.sem, 1)
                        q = s - 1
                        if q.real():
                            k = q.p % 4
                            met(ve, pj_ps, q)
                            ve.tensor_tensor(y[:, k, :], bank(5)[:, P:2 * P], projb[:], ALU.add).then_inc(y_ok.sem, 1)
                            met(ve, y_ok, q)
                            ve.bn_stats(st[:, k, :], y[:, k, :]).then_inc(st_ok.sem, 1)
                            met(ve, st_ok, q)
                            apart(ve)
                            ve.bn_aggr(mv[:, k, :], st[:, k, :]).then_inc(mv_ok.sem, 1)
                            met(ve, mv_ok, q)
                            ve.tensor_scalar(rstd[:, k:k + 1], mv[:, k, 1:2], 1e-5, None, ALU.add).then_inc(ve_ok.sem, 1)

                    slots(ve, slot)

                @block.tensor
                def _(pe):
                    def scores(q):
                        if not q.real():
                            return
                        kind = (2 if q.p >= 6 else 0) + q.p % 2
                        met(pe, pr_ok, q - 1)
                        met(pe, prT_a, q - 1)
                        met(pe, prT_v, q - 1)
                        met(pe, qkT_ok, q)
                        for j in range(4):
                            for k, bt in enumerate((bth, btl)):
                                pe.matmul(bank(j)[:, 0:256], ident16[:], bt[:, kind, j].rearrange("q g m -> q (g m)"),
                                          start=(k == 0), stop=False, skip_group_check=True)
                        for g in range(4):
                            for w in range(2):
                                for j in range(4):
                                    i = pe.matmul(bank(j)[64 * w:64 * w + 64, 64 * g:64 * g + 64],
                                                  qkT[32 * j:32 * j + 32, q.p % 2, 0, g, 64 * w:64 * w + 64],
                                                  qkT[32 * j:32 * j + 32, q.p % 2, 1, g, 64 * w:64 * w + 64],
                                                  start=False, stop=False, skip_group_check=True)
                        i.then_inc(s_ps.sem, 1)

                    def hidden(s, f):
                        q0 = hidden_of(s)
                        if q0 is None or not q0.real():
                            return
                        if f == 0:
                            met(pe, x1T_ok, q0 + 3)
                            met(pe, z_ok, q0 - 1)
                        met(pe, gl_ok, q0 + (f - 1))
                        pe.matmul(bank(7), f1T[:, f * P:(f + 1) * P], x1T[:, q0.p // 4, :], start=True, stop=True)\
                            .then_inc(h_ps.sem, 1)

                    def slot(s):
                        if s.real():
                            met(pe, mx_ok, s)
                            met(pe, qk_ok, s + 1)
                            met(pe, y_ok, s - 2)
                            pe.transpose(bank(5)[0:NH, 384:512], mx[:], ident[:]).then_inc(mT_ps.sem, 1)
                            met(pe, mT_ok, s)
                            for j in range(4):
                                i = pe.matmul(bank(j)[:, 0:256], mT[:], sel[:, 256 * j:256 * j + 256],
                                              start=False, stop=True, skip_group_check=True)
                            i.then_inc(sm_ps.sem, 1)
                        q = s + 2
                        if q.real():
                            landed(pe, q)
                            met(pe, qk_ok, q - 1)
                            met(pe, y_ok, q - 4)
                            pe.transpose(bank(5)[:, 0:P], xw[:, q.p, :], ident[:]).then_inc(xT_ps.sem, 1)
                        q = s + 1
                        if q.real():
                            met(pe, x1T_ok, q - 4)
                            met(pe, qkT_ok, q - 1)
                            for w in range(2):
                                for k in range(2):
                                    i = pe.matmul(bank(6)[64 * k:64 * k + 64, C * w:C * w + C],
                                                  xT[:, q.p % 2, 64 * w:64 * w + 64], wqkT[:, 2 * C:3 * C],
                                                  start=True, stop=True)
                            i.then_inc(v_ps.sem, 1)
                        q = s + 2
                        if q.real():
                            met(pe, xT_ok, q)
                            pe.matmul(bank(5)[:, P:P + 2 * C], xT[:, q.p % 2, :], wqkT[:, 0:2 * C], start=True, stop=True)\
                                .then_inc(qk_ps.sem, 1)
                        if s.real():
                            met(pe, pr_ok, s)
                            for k in range(8):
                                i = pe.transpose(bank(k // 2)[:, 256 + (k % 2) * P:256 + (k % 2 + 1) * P],
                                                 pr[:, s.p % 2, 2 * k:2 * k + 2, :].rearrange("q h m -> q (h m)"), ident[:])
                            i.then_inc(prT_ps.sem, 1)
                        q = s + 1
                        if q.real():
                            met(pe, hi_ok, q, 2)
                            met(pe, lo_ok, q, 2)
                            met(pe, v_ok, q)
                            dst = bank(6).bitcast(F16)
                            for a in range(2):
                                for g in range(4):
                                    i = pe.transpose(dst[:, (4 * a + g) * P:(4 * a + g + 1) * P],
                                                     split[:, q.p % 2, a, 4 * g:4 * g + 4].rearrange("q h s d -> q (h s d)"),
                                                     ident16[:])
                            i.then_inc(qkT_ps.sem, 1)
                        hidden(s, 0)
                        todo = [q for q in outputs_of(s) if q.real()]
                        for n, q in enumerate(todo):
                            k = q.p % 4
                            if k == 0:
                                met(pe, gl_ok, q + 3)
                            elif n == 0:
                                met(pe, z_ok, q - 1)
                            for f in range(FC):
                                i = pe.matmul(bank(7)[:, (k % 2 if k < 2 else 0) * C:(k % 2 if k < 2 else 0) * C + C],
                                              gl[:, f, k * P:(k + 1) * P], f2T[:, f, :], start=(f == 0), stop=(f == FC - 1))
                            i.then_inc(m_ps.sem, 1)
                        scores(s + 1)
                        hidden(s, 1)
                        if s.real():
                            met(pe, prT_a, s)
                            met(pe, prT_v, s)
                            met(pe, on_ok, s - 1)
                            for k in range(8):
                                j, t = k // 2, k % 2
                                for w in range(2):
                                    o = bank(4)[64 * w:64 * w + 64, 0:NH * (HD + 1)]\
                                        .rearrange("q (t k j d) -> q t k j d", t=2, k=2, j=4)
                                    v = vd[:, s.p % 2, w].rearrange("q (t k j) d -> q t k j d", t=2, k=2)
                                    i = pe.matmul(o[:, t, :, j, :], prT[:, s.p % 2, k, 64 * w:64 * w + 64], v[:, t, :, j, :],
                                                  start=True, stop=True)
                            i.then_inc(o_ps.sem, 1)
                        hidden(s, 2)
                        q = s - 1
                        if q.real():
                            met(pe, on_ok, q)
                            met(pe, y_ok, q - 1)
                            met(pe, qk_ok, q + 3)
                            met(pe, mT_ok, q + 1)
                            pe.transpose(bank(5)[:, 384:512], on[:, q.p % 2, :], ident[:]).then_inc(onT_ps.sem, 1)
                        q = s - 2
                        if q.real():
                            met(pe, x1_ok, q)
                            met(pe, x1T_ok, q - 1)
                            met(pe, qkT_ok, q + 3)
                            pe.transpose(bank(6)[:, 0:P], x1[:, q.p, :], ident[:]).then_inc(x1T_ps.sem, 1)
                        hidden(s, 3)
                        q = s - 1
                        if q.real():
                            met(pe, onT_ok, q)
                            pe.matmul(bank(5)[:, P:2 * P], onT[:, q.p % 2, :], projT[:], start=True, stop=True)\
                                .then_inc(pj_ps.sem, 1)

                    slots(pe, slot)

        def phase_landmarks(lnT, klA, xA, xTA, yA, stR, stC):
            with ExitStack() as c1:
                def sb(name, shape, dt=F32):
                    return c1.enter_context(nc.sbuf_tensor(name, shape, dt))

                t_in = sb("l_t", [P, NP, C])
                st = sb("l_st", [P, NP, 6])
                mv = sb("l_mv", [P, NP, 2])
                rstd = sb("l_rstd", [P, NP])
                lt = sb("l_lt", [P, T])
                lbar = sb("l_bar", [P, LM])
                kl = sb("l_kl", [P, LM])
                qlm = sb("l_qlm", [P, AH, LM])
                kT = sb("l_kT", [P, T])
                v = sb("l_v", [P, NP, C])
                e2 = sb("l_e2", [P, 4, LM])
                m2 = sb("l_m2", [P, 4])
                r2 = sb("l_r2", [P, 4])
                xTs = sb("l_xTs", [LM, 4 * P])
                m3 = sb("l_m3", [P, 4])
                n3 = sb("l_n3", [P, 4])
                sum3 = sb("l_sum3", [P, 4])
                r3 = sb("l_r3", [P, 4])
                p3 = sb("l_p3", [P, 2, T])
                p3T = lt[:].rearrange("p (t l) -> p t l", t=NP)

                t_land = signal("l_t_land", 1, 16)
                st_ok = signal("l_st_ok", NP)
                mv_ok = signal("l_mv_ok", NP)
                var_ok = signal("l_var_ok", 1)
                rstd_ok = signal("l_rstd_ok", 1)
                xn_ok = signal("l_xn_ok", NP)
                lt_ps = signal("l_lt_ps", 2)
                lt_ok = signal("l_lt_ok", 2)
                lnT_ok = signal("l_lnT_ok", 1)
                bar_ok = signal("l_bar_ok", 2)
                kl_ps = signal("l_kl_ps", 1)
                kl_ok = signal("l_kl_ok", 3)
                kT_ps = signal("l_kT_ps", 2)
                kT_ok = signal("l_kT_ok", 2)
                v_ps = signal("l_v_ps", 2)
                v_ok = signal("l_v_ok", 2)
                s2_ps = signal("l_s2_ps", 1)
                m2_ok = signal("l_m2_ok", 1)
                d2_ok = signal("l_d2_ok", 1)
                e2_ok = signal("l_e2_ok", 1)
                r2_ok = signal("l_r2_ok", 2)
                x_ok = signal("l_x_ok", 1)
                xT_ps = signal("l_xT_ps", 1)
                xT_ok = signal("l_xT_ok", 1)
                keep_ok = signal("l_keep_ok", 2)
                s3_ps = signal("l_s3_ps", 4)
                n3_ok = signal("l_n3_ok", 8)
                p3_ok = signal("l_p3_ok", 4)
                p3T_ps = signal("l_p3T_ps", 8)
                p3T_a = signal("l_p3T_a", 4)
                p3T_v = signal("l_p3T_v", 4)
                y_ps = signal("l_y_ps", 4)
                r3_ok = signal("l_r3_ok", 4)
                y_ok = signal("l_y_ok", 8)
                turn_done = sem("l_turn_done")

                with nc.Block() as block:
                    @block.sync
                    def _(sp):
                        with sp.Fori(0, NB) as b:
                            sp.wait_ge(lt_ps.sem, lt_ps.at(b, 0))
                            apart(sp)
                            sp.dma_start(t_in[:], mid[b].rearrange("(t p) c -> p t c", p=P)).then_inc(t_land.sem, 16)

                    @block.gpsimd
                    def _(gp):
                        with gp.Fori(0, NB) as b:
                            gp.wait_ge(var_ok.sem, var_ok.at(b, 1))
                            gp.tensor_tensor(rstd[:], rstd[:], nhalf[:, 0:NP], ALU.pow).then_inc(rstd_ok.sem, 1)
                            gp.wait_ge(lt_ok.sem, lt_ok.at(b, 2))
                            gp.tensor_copy(lnT[:, b, :], lt[:]).then_inc(lnT_ok.sem, 1)
                            gp.wait_ge(x_ok.sem, x_ok.at(b, 1))
                            gp.tensor_copy(xA[:, b, :], e2[:].rearrange("p h j -> p (h j)")).then_inc(keep_ok.sem, 1)
                            gp.wait_ge(keep_ok.sem, keep_ok.at(b, 1))
                            gp.wait_ge(xT_ok.sem, xT_ok.at(b, 1))
                            gp.tensor_copy(xTA[:, b, :], xTs[:]).then_inc(keep_ok.sem, 1)

                    @block.scalar
                    def _(ac):
                        with ac.Fori(0, NB) as b:
                            ac.wait_ge(turn_done, b * 3)
                            for u in range(2):
                                ac.wait_ge(lt_ps.sem, lt_ps.at(b, u + 1))
                                if u == 0:
                                    ac.wait_ge(lnT_ok.sem, lnT_ok.at(b, 0))
                                ac.activation(lt[:, 512 * u:512 * u + 512], bank(u), ACT.Copy).then_inc(lt_ok.sem, 1)
                            for u in range(2):
                                ac.wait_ge(kT_ps.sem, kT_ps.at(b, u + 1))
                                ac.activation(kT[:, 512 * u:512 * u + 512], bank(3 + u), ACT.Copy).then_inc(kT_ok.sem, 1)
                            ac.wait_ge(d2_ok.sem, d2_ok.at(b, 1))
                            ac.activation(e2[:], e2[:], ACT.Exp).then_inc(e2_ok.sem, 1)
                            ac.wait_ge(xT_ps.sem, xT_ps.at(b, 1))
                            ac.wait_ge(keep_ok.sem, keep_ok.at(b, 0))
                            ac.activation(xTs[:], bank(7)[0:LM, :], ACT.Copy).then_inc(xT_ok.sem, 1)
                            for h in range(4):
                                ac.wait_ge(n3_ok.sem, n3_ok.at(b, 2 * h + 2))
                                if h >= 2:
                                    ac.wait_ge(p3T_ps.sem, p3T_ps.at(b, 2 * h - 2))
                                ac.activation(p3[:, h % 2, :], banks(2 * (h % 2), 2), ACT.Exp, bias=n3[:, h:h + 1],
                                              accum_out=sum3[:, h:h + 1]).then_inc(p3_ok.sem, 1)
                                ac.wait_ge(p3T_ps.sem, p3T_ps.at(b, 2 * h + 1))
                                if h == 0:
                                    ac.wait_ge(lnT_ok.sem, lnT_ok.at(b, 1))
                                else:
                                    ac.wait_ge(y_ps.sem, y_ps.at(b, h))
                                ac.activation(p3T[:, 0:4, :].rearrange("p a c -> p (a c)"), bank(4), ACT.Copy)\
                                    .then_inc(p3T_a.sem, 1)
                            ac.wait_ge(p3T_a.sem, p3T_a.at(b, 4))
                            ac.sem_inc(turn_done, 1)

                    @block.vector
                    def _(ve):
                        with ve.Fori(0, NB) as b:
                            ve.wait_ge(turn_done, b * 3)
                            ve.wait_ge(t_land.sem, t_land.at(b, 1))
                            for t in range(NP):
                                ve.bn_stats(st[:, t, :], t_in[:, t, :]).then_inc(st_ok.sem, 1)
                            for t in range(NP):
                                ve.wait_ge(st_ok.sem, st_ok.at(b, t + 1))
                                apart(ve)
                                ve.bn_aggr(mv[:, t, :], st[:, t, :]).then_inc(mv_ok.sem, 1)
                            ve.wait_ge(mv_ok.sem, mv_ok.at(b, NP))
                            ve.tensor_scalar(rstd[:], mv[:, :, 1], 1e-5, None, ALU.add).then_inc(var_ok.sem, 1)
                            ve.wait_ge(rstd_ok.sem, rstd_ok.at(b, 1))
                            for t in range(NP):
                                ve.tensor_scalar(t_in[:, t, :], t_in[:, t, :], mv[:, t, 0:1], rstd[:, t:t + 1],
                                                 ALU.subtract, ALU.mult).then_inc(xn_ok.sem, 1)
                            ve.wait_ge(lt_ok.sem, lt_ok.at(b, 2))
                            ve.tensor_reduce(lbar[:], lt[:].rearrange("p (l s) -> p l s", s=SEG), X, ALU.add)\
                                .then_inc(bar_ok.sem, 1)
                            ve.wait_ge(bar_ok.sem, bar_ok.at(b, 1))
                            ve.tensor_scalar(lbar[:], lbar[:], 1.0 / SEG, None, ALU.mult).then_inc(bar_ok.sem, 1)
                            ve.wait_ge(kl_ps.sem, kl_ps.at(b, 1))
                            ve.tensor_copy(kl[:], bank(2)[:, 0:LM]).then_inc(kl_ok.sem, 1)
                            ve.tensor_copy(klA[:, b, :], bank(2)[:, 0:LM]).then_inc(kl_ok.sem, 1)
                            ve.tensor_tensor(qlm[:], bank(2)[:, LM:2 * LM].unsqueeze(1).to_broadcast([P, AH, LM]),
                                             headmask[:].unsqueeze(2).to_broadcast([P, AH, LM]), ALU.mult)\
                                .then_inc(kl_ok.sem, 1)
                            for u in range(2):
                                ve.wait_ge(v_ps.sem, v_ps.at(b, u + 1))
                                ve.tensor_copy(v[:, 4 * u:4 * u + 4, :].rearrange("p t c -> p (t c)"), bank(5 + u))\
                                    .then_inc(v_ok.sem, 1)
                            ve.wait_ge(s2_ps.sem, s2_ps.at(b, 1))
                            ve.wait_ge(keep_ok.sem, keep_ok.at(b, 0))
                            s2 = bank(7)[:, 0:4 * LM].rearrange("p (h j) -> p h j", h=4)
                            ve.tensor_reduce(m2[:], s2, X, ALU.max).then_inc(m2_ok.sem, 1)
                            ve.wait_ge(m2_ok.sem, m2_ok.at(b, 1))
                            ve.tensor_tensor(e2[:], s2, m2[:].unsqueeze(2).to_broadcast([P, 4, LM]), ALU.subtract)\
                                .then_inc(d2_ok.sem, 1)
                            ve.wait_ge(e2_ok.sem, e2_ok.at(b, 1))
                            ve.tensor_reduce(r2[:], e2[:], X, ALU.add).then_inc(r2_ok.sem, 1)
                            ve.wait_ge(r2_ok.sem, r2_ok.at(b, 1))
                            ve.reciprocal(r2[:], r2[:]).then_inc(r2_ok.sem, 1)
                            ve.wait_ge(r2_ok.sem, r2_ok.at(b, 2))
                            ve.tensor_tensor(e2[:], e2[:], r2[:].unsqueeze(2).to_broadcast([P, 4, LM]), ALU.mult)\
                                .then_inc(x_ok.sem, 1)
                            ve.wait_ge(x_ok.sem, x_ok.at(b, 1))
                            ve.tensor_reduce(stR[:, b, :], e2[:], X, ALU.add)
                            ve.wait_ge(xT_ok.sem, xT_ok.at(b, 1))
                            ve.tensor_reduce(stC[:, b, :], xTs[:].rearrange("p (h i) -> p h i", h=AH), X, ALU.add)
                            for h in range(4):
                                ve.wait_ge(s3_ps.sem, s3_ps.at(b, h + 1))
                                ve.tensor_reduce(m3[:, h:h + 1], banks(2 * (h % 2), 2), X, ALU.max).then_inc(n3_ok.sem, 1)
                                ve.wait_ge(n3_ok.sem, n3_ok.at(b, 2 * h + 1))
                                ve.tensor_scalar(n3[:, h:h + 1], m3[:, h:h + 1], -1.0, None, ALU.mult)\
                                    .then_inc(n3_ok.sem, 1)
                                ve.wait_ge(p3T_ps.sem, p3T_ps.at(b, 2 * h + 2))
                                if h == 0:
                                    ve.wait_ge(lnT_ok.sem, lnT_ok.at(b, 1))
                                else:
                                    ve.wait_ge(y_ps.sem, y_ps.at(b, h))
                                ve.tensor_copy(p3T[:, 4:8, :].rearrange("p a c -> p (a c)"), bank(5))\
                                    .then_inc(p3T_v.sem, 1)
                                ve.wait_ge(p3_ok.sem, p3_ok.at(b, h + 1))
                                ve.reciprocal(r3[:, h:h + 1], sum3[:, h:h + 1]).then_inc(r3_ok.sem, 1)
                                ve.wait_ge(r3_ok.sem, r3_ok.at(b, h + 1))
                                ve.wait_ge(y_ps.sem, y_ps.at(b, h + 1))
                                for k in range(2):
                                    q = slice(64 * k, 64 * k + 64)
                                    ve.tensor_scalar(yA[q, b, AD * h:AD * h + AD], bank(6)[q, 32 * h + AD * k:32 * h + AD * k + AD],
                                                     r3[q, h:h + 1], None, ALU.mult).then_inc(y_ok.sem, 1)
                            ve.wait_ge(y_ok.sem, y_ok.at(b, 8))
                            ve.sem_inc(turn_done, 1)

                    @block.tensor
                    def _(pe):
                        with pe.Fori(0, NB) as b:
                            pe.wait_ge(turn_done, b * 3)
                            for t in range(NP):
                                pe.wait_ge(xn_ok.sem, xn_ok.at(b, t + 1))
                                i = pe.transpose(bank(t // 4)[:, (t % 4) * P:(t % 4 + 1) * P], t_in[:, t, :], ident[:])
                                if t % 4 == 3:
                                    i.then_inc(lt_ps.sem, 1)
                            pe.wait_ge(lt_ok.sem, lt_ok.at(b, 2))
                            for u in range(2):
                                pe.matmul(bank(3 + u), wqkv2[:, C:2 * C], lt[:, 512 * u:512 * u + 512], start=True, stop=True)\
                                    .then_inc(kT_ps.sem, 1)
                            for t in range(NP):
                                i = pe.matmul(bank(5 + t // 4)[:, (t % 4) * C:(t % 4 + 1) * C], lt[:, t * P:(t + 1) * P],
                                              wqkv2[:, 2 * C:3 * C], start=True, stop=True)
                                if t % 4 == 3:
                                    i.then_inc(v_ps.sem, 1)
                            pe.wait_ge(bar_ok.sem, bar_ok.at(b, 2))
                            pe.matmul(bank(2)[:, 0:LM], wqkv2[:, C:2 * C], lbar[:], start=True, stop=True)
                            pe.matmul(bank(2)[:, LM:2 * LM], wqkv2[:, 0:C], lbar[:], start=True, stop=True)\
                                .then_inc(kl_ps.sem, 1)
                            pe.wait_ge(kl_ok.sem, kl_ok.at(b, 3))
                            for h in range(4):
                                i = pe.matmul(bank(7)[:, h * LM:(h + 1) * LM], qlm[:, 2 * h:2 * h + 2, :]
                                              .rearrange("p a l -> p (a l)"), kl[:], start=True, stop=True)
                            i.then_inc(s2_ps.sem, 1)

                            def scores(h):
                                if h == 0:
                                    pe.wait_ge(kT_ok.sem, kT_ok.at(b, 2))
                                if h >= 2:
                                    pe.wait_ge(p3_ok.sem, p3_ok.at(b, h - 1))
                                for u in range(2):
                                    i = pe.matmul(bank(2 * (h % 2) + u), qlm[:, 2 * h:2 * h + 2, :].rearrange("p a l -> p (a l)"),
                                                  kT[:, 512 * u:512 * u + 512], start=True, stop=True)
                                i.then_inc(s3_ps.sem, 1)

                            scores(0)
                            scores(1)
                            pe.wait_ge(x_ok.sem, x_ok.at(b, 1))
                            apart(pe)
                            for h in range(4):
                                i = pe.transpose(bank(7)[0:LM, h * P:(h + 1) * P], e2[:, h, :], ident[:])
                            i.then_inc(xT_ps.sem, 1)
                            for h in range(4):
                                pe.wait_ge(p3_ok.sem, p3_ok.at(b, h + 1))
                                if h == 0:
                                    pe.wait_ge(v_ok.sem, v_ok.at(b, 2))
                                else:
                                    pe.wait_ge(p3T_a.sem, p3T_a.at(b, h))
                                    pe.wait_ge(p3T_v.sem, p3T_v.at(b, h))
                                for t in range(NP):
                                    i = pe.transpose(bank(4 + t // 4)[:, (t % 4) * P:(t % 4 + 1) * P],
                                                     p3[:, h % 2, t * P:(t + 1) * P], ident[:])
                                    if t % 4 == 3:
                                        i.then_inc(p3T_ps.sem, 1)
                                if h + 2 < 4:
                                    scores(h + 2)
                                pe.wait_ge(p3T_a.sem, p3T_a.at(b, h + 1))
                                pe.wait_ge(p3T_v.sem, p3T_v.at(b, h + 1))
                                if h:
                                    pe.wait_ge(y_ok.sem, y_ok.at(b, 2 * h))
                                for t in range(NP):
                                    i = pe.matmul(bank(6)[:, 32 * h:32 * h + 32], p3T[:, t, :], v[:, t, 32 * h:32 * h + 32],
                                                  start=(t == 0), stop=(t == NP - 1))
                                i.then_inc(y_ps.sem, 1)
                            pe.sem_inc(turn_done, 1)

        def phase_pinv(xA, xTA, yA, zA, stR, stC):
            G = min(4, NB)
            with ExitStack() as c1:
                def sb(name, shape, dt=F32):
                    return c1.enter_context(nc.sbuf_tensor(name, shape, dt))

                i64 = sb("p_i64", [P, 3, LM])
                mxs = sb("p_mx", [P, 2])
                mrow = sb("p_mrow", [1, 4])
                cc = sb("p_c", [P, 1])
                xts = sb("p_xts", [LM, G, 4 * P])
                xs = sb("p_xs", [P, G, 4 * LM])
                ay = sb("p_ay", [P, G, 4, LM + AD])
                tm = sb("p_t", [P, G, 4, LM])

                s_i = sem("p_s_i")
                s_ik = sem("p_s_ik")
                s_m = sem("p_s_m")
                s_mt = sem("p_s_mt")
                s_row = sem("p_s_row")
                s_cb = sem("p_s_cb")
                s_c = sem("p_s_c")
                got = signal("p_got", 3 * G)
                prod = signal("p_prod", G * (3 * ITERS + 2))
                a_ok = signal("p_a_ok", G * (ITERS + 1))
                t_ok = signal("p_t_ok", G * 3 * ITERS)
                z_ok = signal("p_z_ok", G)

                def slot(n, i):
                    return (n % 2) * 4 + i

                with nc.Block() as block:
                    @block.sync
                    def _(sp):
                        sp.dma_start(i64[:, 0, :], A["i64"]).then_inc(s_i, 16)

                    @block.gpsimd
                    def _(gp):
                        with gp.Fori(0, NB // G) as g:
                            gp.wait_ge(prod.sem, prod.at(g, 0))
                            gp.wait_ge(z_ok.sem, z_ok.at(g, 0))
                            for i in range(G):
                                if i:
                                    gp.wait_ge(got.sem, got.at(g, 3 * i))
                                gp.tensor_copy(xts[:, i, :], xTA[:, g * G + i, :]).then_inc(got.sem, 1)
                                gp.wait_ge(got.sem, got.at(g, 3 * i + 1))
                                gp.tensor_copy(xs[:, i, :], xA[:, g * G + i, :]).then_inc(got.sem, 1)
                                gp.tensor_copy(ay[:, i, :, LM:LM + AD],
                                               yA[:, g * G + i, :].rearrange("p (h d) -> p h d", h=4)).then_inc(got.sem, 1)

                    @block.vector
                    def _(ve):
                        ve.wait_ge(s_i, 16)
                        ve.tensor_scalar(i64[:, 1, :], i64[:, 0, :], 15.0, None, ALU.mult).then_inc(s_ik, 1)
                        ve.tensor_scalar(i64[:, 2, :], i64[:, 0, :], 3.25, None, ALU.mult).then_inc(s_ik, 1)
                        ve.wait_ge(s_ik, 2)
                        ve.tensor_scalar(i64[:, 0, :], i64[:, 0, :], 7.0, None, ALU.mult).then_inc(s_ik, 1)
                        ve.tensor_reduce(mxs[:, 0:1], stR[:].rearrange("p b h -> p (b h)"), X, ALU.max).then_inc(s_m, 1)
                        ve.tensor_reduce(mxs[0:LM, 1:2], stC[:].rearrange("p b h -> p (b h)"), X, ALU.max).then_inc(s_m, 1)
                        ve.wait_ge(s_mt, 1)
                        ve.tensor_reduce(mrow[:, 0:1], bank(0)[0:1, 0:P], X, ALU.max).then_inc(s_row, 1)
                        ve.tensor_reduce(mrow[:, 1:2], bank(0)[0:1, P:P + LM], X, ALU.max).then_inc(s_row, 1)
                        ve.wait_ge(s_row, 2)
                        ve.tensor_tensor(mrow[:, 2:3], mrow[:, 0:1], mrow[:, 1:2], ALU.mult).then_inc(s_row, 1)
                        ve.wait_ge(s_row, 3)
                        ve.reciprocal(mrow[:, 3:4], mrow[:, 2:3]).then_inc(s_row, 1)
                        ve.wait_ge(s_cb, 1)
                        ve.tensor_copy(cc[:], bank(1)[:, 0:1]).then_inc(s_c, 1)
                        ve.wait_ge(s_c, 1)
                        ve.wait_ge(s_ik, 3)
                        with ve.Fori(0, NB // G) as g:
                            def ident_minus(i, k, n):
                                ps = bank(slot(n, i))[:, 0:4 * (LM + AD)].rearrange("p (h j) -> p h j", h=4)[:, :, 0:LM]
                                eye = i64[:, k, :].unsqueeze(1).to_broadcast([P, 4, LM])
                                if k == 2:
                                    ve.scalar_tensor_tensor(out=tm[:, i], in0=ps, scalar=-0.25, in1=eye, op0=ALU.mult,
                                                            op1=ALU.add).then_inc(t_ok.sem, 1)
                                else:
                                    ve.tensor_tensor(tm[:, i], eye, ps, ALU.subtract).then_inc(t_ok.sem, 1)

                            for i in range(G):
                                ve.wait_ge(prod.sem, prod.at(g, i + 1))
                                ps = bank(slot(0, i))[:, 0:4 * (LM + AD)].rearrange("p (h j) -> p h j", h=4)[:, :, 0:LM]
                                ve.tensor_scalar(ay[:, i, :, 0:LM], ps, cc[:, 0:1], None, ALU.mult).then_inc(a_ok.sem, 1)
                            for i in range(G):
                                ve.wait_ge(a_ok.sem, a_ok.at(g, i + 1))
                                ve.tensor_tensor(tm[:, i], i64[:, 0, :].unsqueeze(1).to_broadcast([P, 4, LM]),
                                                 ay[:, i, :, 0:LM], ALU.subtract).then_inc(t_ok.sem, 1)
                            n = 1
                            for it in range(ITERS):
                                for k in (1, 2, 0):
                                    for i in range(G):
                                        ve.wait_ge(prod.sem, prod.at(g, G * n + i + 1))
                                        if k:
                                            ident_minus(i, k, n)
                                        else:
                                            ve.tensor_copy(ay[:, i], bank(slot(n, i))[:, 0:4 * (LM + AD)]
                                                           .rearrange("p (h j) -> p h j", h=4)).then_inc(a_ok.sem, 1)
                                            if it < ITERS - 1:
                                                ident_minus(i, 0, n)
                                    n += 1
                            for i in range(G):
                                ve.wait_ge(prod.sem, prod.at(g, G * n + i + 1))
                                ve.tensor_scalar(zA[:, g * G + i, :], bank(slot(n, i))[:, 0:4 * AD], cc[:, 0:1], None,
                                                 ALU.mult).then_inc(z_ok.sem, 1)

                    @block.tensor
                    def _(pe):
                        pe.wait_ge(s_m, 2)
                        pe.transpose(bank(0)[0:1, 0:P], mxs[:, 0:1], ident[:])
                        pe.transpose(bank(0)[0:1, P:P + LM], mxs[0:LM, 1:2], ident[0:LM, 0:LM]).then_inc(s_mt, 1)
                        pe.wait_ge(s_row, 4)
                        pe.matmul(bank(1)[:, 0:1], ones1[:], mrow[:, 3:4], start=True, stop=True).then_inc(s_cb, 1)
                        pe.wait_ge(s_c, 1)
                        with pe.Fori(0, NB // G) as g:
                            def each(n, i, width, left, right, stride=LM + AD):
                                for h in range(4):
                                    for k in range(2):
                                        j = pe.matmul(bank(slot(n, i))[64 * k:64 * k + 64, stride * h:stride * h + width],
                                                      left(h, k), right(h, k), start=True, stop=True)
                                j.then_inc(prod.sem, 1)

                            half = lambda k: slice(64 * k, 64 * k + 64)
                            pe.wait_ge(z_ok.sem, z_ok.at(g, 0))
                            for i in range(G):
                                pe.wait_ge(got.sem, got.at(g, 3 * i + 3))
                                apart(pe)
                                xt = lambda h, k: xts[:, i, P * h + 64 * k:P * h + 64 * k + 64]
                                each(0, i, LM, xt, xt)
                            n = 1
                            for it in range(ITERS):
                                for k in range(3):
                                    for i in range(G):
                                        if it == 0 and k == 0:
                                            pe.wait_ge(a_ok.sem, a_ok.at(g, i + 1))
                                        pe.wait_ge(t_ok.sem, t_ok.at(g, G * (n - 1) + i + 1))
                                        apart(pe)
                                        a = lambda h, q: ay[half(q), i, h, 0:LM]
                                        t = lambda h, q: tm[half(q), i, h, :]
                                        if k < 2:
                                            each(n, i, LM, a, t)
                                        else:
                                            each(n, i, LM + AD, t, lambda h, q: ay[half(q), i, h, :])
                                    n += 1
                            for i in range(G):
                                pe.wait_ge(a_ok.sem, a_ok.at(g, G * ITERS + i + 1))
                                apart(pe)
                                each(n, i, AD, lambda h, q: xs[half(q), i, LM * h:LM * h + LM],
                                     lambda h, q: ay[half(q), i, h, LM:LM + AD], stride=AD)

        def phase_mix(lnT, klA, zA):
            with ExitStack() as c1:
                def sb(name, shape, dt=F32):
                    return c1.enter_context(nc.sbuf_tensor(name, shape, dt))

                t_in = sb("m_t", [P, NP, C])
                lt = sb("m_lt", [P, T])
                kl = sb("m_kl", [P, LM])
                klm = sb("m_klm", [P, AH, LM])
                zd = sb("m_zd", [P, 4, 2, AD + 1])
                qT = sb("m_qT", [P, T])
                m1 = sb("m_m1", [P, 2, AH])
                e1 = sb("m_e1", [P, 2, AH, LM])
                p1T = sb("m_p1T", [P, 2, 4, P])
                r1 = sb("m_r1", [P, 2, AH])
                on = sb("m_on", [P, 2, C])
                onT = sb("m_onT", [P, 2, P])
                t2 = sb("m_t2", [P, NP, C])
                xn = sb("m_xn", [P, NP, C])
                st = sb("m_st", [P, NP, 6])
                mv = sb("m_mv", [P, NP, 2])
                rstd = sb("m_rstd", [P, NP])
                xf = sb("m_xf", [P, T])
                xh = sb("m_xh", [P, T], F16)
                lg = sb("m_lg", [P, NP, NE])
                lm = sb("m_lm", [P, NP])
                gt = sb("m_gt", [P, NP, NE, NE])
                eq = sb("m_eq", [P, NP, NE, NE])
                tri = sb("m_tri", [P, NE, NE])
                rank = sb("m_rank", [P, NP, NE])
                cwl = sb("m_cwl", [P, NP, NE])
                cwT = sb("m_cwT", [NE, T])
                x16 = lnT[:].bitcast(F16)

                tri_in = sem("m_tri_in")
                zd_set = sem("m_zd_set")
                t_land = signal("m_t_land", 1, 16)
                lt_in = signal("m_lt_in", 1)
                klz_in = signal("m_klz_in", 3)
                klm_ok = signal("m_klm_ok", 1)
                tb_ok = signal("m_tb_ok", 1)
                qT_ps = signal("m_qT_ps", 2)
                qT_ok = signal("m_qT_ok", 2)
                s_ps = signal("m_s_ps", NP)
                mx_ok = signal("m_mx_ok", NP)
                d_ok = signal("m_d_ok", NP)
                e_ok = signal("m_e_ok", NP)
                eT_ps = signal("m_eT_ps", NP)
                eT_ok = signal("m_eT_ok", NP)
                o_ps = signal("m_o_ps", NP)
                r_ok = signal("m_r_ok", NP)
                on_ok = signal("m_on_ok", NP)
                onT_ps = signal("m_onT_ps", NP)
                onT_ok = signal("m_onT_ok", NP)
                w_ps = signal("m_w_ps", NP)
                t2_ok = signal("m_t2_ok", NP)
                st_ok = signal("m_st_ok", NP)
                mv_ok = signal("m_mv_ok", NP)
                var_ok = signal("m_var_ok", 1)
                rstd_ok = signal("m_rstd_ok", 1)
                xn_ok = signal("m_xn_ok", NP)
                xf_ps = signal("m_xf_ps", 2)
                xf_ok = signal("m_xf_ok", 2)
                hi_ok = signal("m_hi_ok", 2)
                keep_ok = signal("m_keep_ok", 1)
                lo_ok = signal("m_lo_ok", 1)
                lg_ps = signal("m_lg_ps", 1)
                gate = signal("m_gate", 13)
                ex_ok = signal("m_ex_ok", 1)
                cwT_ps = signal("m_cwT_ps", 1)
                cwT_ok = signal("m_cwT_ok", 1)
                b_ps = signal("m_b_ps", 1)
                b_ok = signal("m_b_ok", 1)
                r_out = signal("m_r_out", 1)
                stored = signal("m_stored", 1, 16)
                turn_done = sem("m_turn_done")

                def onT_copy(ac, b, t):
                    ac.wait_ge(onT_ps.sem, onT_ps.at(b, t + 1))
                    if t >= 2:
                        ac.wait_ge(w_ps.sem, w_ps.at(b, t - 1))
                    ac.activation(onT[:, t % 2, :], bank(t % 2)[:, 0:P], ACT.Copy).then_inc(onT_ok.sem, 1)

                with nc.Block() as block:
                    @block.sync
                    def _(sp):
                        sp.dma_start(tri[:], A["tri"]).then_inc(tri_in, 16)
                        with sp.Fori(0, NB) as b:
                            sp.wait_ge(r_out.sem, r_out.at(b, 0))
                            apart(sp)
                            sp.dma_start(t_in[:], mid[b].rearrange("(t p) c -> p t c", p=P)).then_inc(t_land.sem, 16)
                            sp.wait_ge(r_out.sem, r_out.at(b, 1))
                            apart(sp)
                            sp.dma_start(res[b].rearrange("(t p) c -> p t c", p=P), xn[:]).then_inc(stored.sem, 16)
                            sp.wait_ge(stored.sem, stored.at(b, 1))
                            apart(sp)

                    @block.gpsimd
                    def _(gp):
                        gp.memset(zd[:], 0.0).then_inc(zd_set, 1)
                        for k in range(2):
                            gp.wait_ge(zd_set, k + 1)
                            gp.memset(zd[64 * k:64 * k + 64, :, k, AD:AD + 1], 1.0).then_inc(zd_set, 1)
                        gp.wait_ge(zd_set, 3)
                        with gp.Fori(0, NB) as b:
                            gp.wait_ge(turn_done, b * 4)
                            gp.tensor_copy(lt[:], lnT[:, b, :]).then_inc(lt_in.sem, 1)
                            gp.tensor_copy(kl[:], klA[:, b, :]).then_inc(klz_in.sem, 1)
                            for k in range(2):
                                q = slice(64 * k, 64 * k + 64)
                                gp.wait_ge(klz_in.sem, klz_in.at(b, k + 1))
                                gp.tensor_copy(zd[q, :, k, 0:AD], zA[q, b, :].rearrange("p (h d) -> p h d", h=4))\
                                    .then_inc(klz_in.sem, 1)
                            gp.wait_ge(klz_in.sem, klz_in.at(b, 3))
                            gp.wait_ge(t_land.sem, t_land.at(b, 1))
                            gp.tensor_tensor(t_in[:], t_in[:], bout[:].unsqueeze(1).to_broadcast([P, NP, C]), ALU.add)\
                                .then_inc(tb_ok.sem, 1)
                            gp.wait_ge(var_ok.sem, var_ok.at(b, 1))
                            gp.tensor_tensor(rstd[:], rstd[:], nhalf[:, 0:NP], ALU.pow).then_inc(rstd_ok.sem, 1)
                            gp.wait_ge(hi_ok.sem, hi_ok.at(b, 2))
                            gp.tensor_copy(x16[:, b, 0:T], xh[:]).then_inc(keep_ok.sem, 1)
                            gp.wait_ge(b_ok.sem, b_ok.at(b, 1))
                            gp.tensor_tensor(xn[:], xn[:], b2s[:, 0, :].unsqueeze(1).to_broadcast([P, NP, C]), ALU.add)\
                                .then_inc(r_out.sem, 1)
                            gp.wait_ge(r_out.sem, r_out.at(b, 1))
                            gp.wait_ge(keep_ok.sem, keep_ok.at(b, 1))
                            gp.sem_inc(turn_done, 1)

                    @block.scalar
                    def _(ac):
                        with ac.Fori(0, NB) as b:
                            ac.wait_ge(turn_done, b * 4)
                            for u in range(2):
                                ac.wait_ge(qT_ps.sem, qT_ps.at(b, u + 1))
                                ac.activation(qT[:, 512 * u:512 * u + 512], bank(u), ACT.Copy).then_inc(qT_ok.sem, 1)
                            for t in range(NP):
                                ac.wait_ge(d_ok.sem, d_ok.at(b, t + 1))
                                ac.activation(e1[:, t % 2], e1[:, t % 2], ACT.Exp).then_inc(e_ok.sem, 1)
                                ac.wait_ge(eT_ps.sem, eT_ps.at(b, t + 1))
                                if t >= 2:
                                    ac.wait_ge(o_ps.sem, o_ps.at(b, t - 1))
                                ac.activation(p1T[:, t % 2].rearrange("p a c -> p (a c)"), bank(4 + t % 2), ACT.Copy)\
                                    .then_inc(eT_ok.sem, 1)
                                if t >= 1:
                                    onT_copy(ac, b, t - 1)
                            onT_copy(ac, b, NP - 1)
                            for u in range(2):
                                ac.wait_ge(xf_ps.sem, xf_ps.at(b, u + 1))
                                s = slice(512 * u, 512 * u + 512)
                                ac.activation(xf[:, s], bank(2 + u), ACT.Copy).then_inc(xf_ok.sem, 1)
                                ac.activation(xh[:, s], bank(2 + u), ACT.Copy).then_inc(hi_ok.sem, 1)
                            ac.wait_ge(gate.sem, gate.at(b, 3))
                            ac.activation(lg[:], lg[:], ACT.Exp).then_inc(ex_ok.sem, 1)
                            ac.wait_ge(cwT_ps.sem, cwT_ps.at(b, 1))
                            ac.activation(cwT[:], banks(5, 2)[0:NE, :], ACT.Copy).then_inc(cwT_ok.sem, 1)
                            ac.wait_ge(cwT_ok.sem, cwT_ok.at(b, 1))
                            ac.sem_inc(turn_done, 1)

                    @block.vector
                    def _(ve):
                        ve.wait_ge(tri_in, 16)
                        with ve.Fori(0, NB) as b:
                            ve.wait_ge(turn_done, b * 4)
                            ve.wait_ge(klz_in.sem, klz_in.at(b, 1))
                            ve.tensor_tensor(klm[:], kl[:].unsqueeze(1).to_broadcast([P, AH, LM]),
                                             headmask[:].unsqueeze(2).to_broadcast([P, AH, LM]), ALU.mult)\
                                .then_inc(klm_ok.sem, 1)

                            def soft(t):
                                ve.wait_ge(s_ps.sem, s_ps.at(b, t + 1))
                                if t >= 2:
                                    ve.wait_ge(eT_ps.sem, eT_ps.at(b, t - 1))
                                s = bank(2 + t % 2).rearrange("p (h l) -> p h l", h=AH)
                                ve.tensor_reduce(m1[:, t % 2, :], s, X, ALU.max).then_inc(mx_ok.sem, 1)
                                ve.wait_ge(mx_ok.sem, mx_ok.at(b, t + 1))
                                ve.tensor_tensor(e1[:, t % 2], s, m1[:, t % 2, :].unsqueeze(2).to_broadcast([P, AH, LM]),
                                                 ALU.subtract).then_inc(d_ok.sem, 1)

                            def normed(t):
                                ve.wait_ge(o_ps.sem, o_ps.at(b, t + 1))
                                if t >= 2:
                                    ve.wait_ge(onT_ps.sem, onT_ps.at(b, t - 1))
                                o = bank(6 + t % 2)[:, 0:AH * (AD + 1)].rearrange("p (h d) -> p h d", h=AH)
                                ve.reciprocal(r1[:, t % 2, :], o[:, :, AD]).then_inc(r_ok.sem, 1)
                                ve.wait_ge(r_ok.sem, r_ok.at(b, t + 1))
                                ve.tensor_tensor(on[:, t % 2, :].rearrange("p (h d) -> p h d", h=AH), o[:, :, 0:AD],
                                                 r1[:, t % 2, :].unsqueeze(2).to_broadcast([P, AH, AD]), ALU.mult)\
                                    .then_inc(on_ok.sem, 1)

                            def add_out(t):
                                ve.wait_ge(w_ps.sem, w_ps.at(b, t + 1))
                                if t == 0:
                                    ve.wait_ge(tb_ok.sem, tb_ok.at(b, 1))
                                ve.tensor_tensor(t2[:, t, :], bank(t % 2)[:, C:2 * C], t_in[:, t, :], ALU.add)\
                                    .then_inc(t2_ok.sem, 1)
                                ve.wait_ge(t2_ok.sem, t2_ok.at(b, t + 1))
                                ve.bn_stats(st[:, t, :], t2[:, t, :]).then_inc(st_ok.sem, 1)

                            soft(0)
                            for t in range(NP):
                                if t + 1 < NP:
                                    soft(t + 1)
                                normed(t)
                                if t >= 1:
                                    add_out(t - 1)
                            add_out(NP - 1)
                            for t in range(NP):
                                ve.wait_ge(st_ok.sem, st_ok.at(b, t + 1))
                                apart(ve)
                                ve.bn_aggr(mv[:, t, :], st[:, t, :]).then_inc(mv_ok.sem, 1)
                            ve.wait_ge(mv_ok.sem, mv_ok.at(b, NP))
                            ve.tensor_scalar(rstd[:], mv[:, :, 1], 1e-5, None, ALU.add).then_inc(var_ok.sem, 1)
                            ve.wait_ge(rstd_ok.sem, rstd_ok.at(b, 1))
                            ve.wait_ge(stored.sem, stored.at(b, 0))
                            for t in range(NP):
                                ve.tensor_scalar(xn[:, t, :], t2[:, t, :], mv[:, t, 0:1], rstd[:, t:t + 1],
                                                 ALU.subtract, ALU.mult).then_inc(xn_ok.sem, 1)
                            g = lambda n: gate.at(b, n)
                            ve.wait_ge(lg_ps.sem, lg_ps.at(b, 1))
                            ve.tensor_tensor(lg[:], bank(4)[:, 0:NP * NE].rearrange("p (t e) -> p t e", e=NE),
                                             gb[:].unsqueeze(1).to_broadcast([P, NP, NE]), ALU.add).then_inc(gate.sem, 1)
                            ve.wait_ge(gate.sem, g(1))
                            ve.tensor_reduce(lm[:], lg[:], X, ALU.max).then_inc(gate.sem, 1)
                            ve.wait_ge(gate.sem, g(2))
                            ve.tensor_tensor(lg[:], lg[:], lm[:].unsqueeze(2).to_broadcast([P, NP, NE]), ALU.subtract)\
                                .then_inc(gate.sem, 1)
                            ve.wait_ge(ex_ok.sem, ex_ok.at(b, 1))
                            ve.tensor_reduce(lm[:], lg[:], X, ALU.add).then_inc(gate.sem, 1)
                            ve.wait_ge(gate.sem, g(4))
                            ve.reciprocal(lm[:], lm[:]).then_inc(gate.sem, 1)
                            ve.wait_ge(gate.sem, g(5))
                            ve.tensor_tensor(lg[:], lg[:], lm[:].unsqueeze(2).to_broadcast([P, NP, NE]), ALU.mult)\
                                .then_inc(gate.sem, 1)
                            ve.wait_ge(gate.sem, g(6))
                            for t in range(NP):
                                other = lg[:, t, :].unsqueeze(1).to_broadcast([P, NE, NE])
                                own = lg[:, t, :].unsqueeze(2).to_broadcast([P, NE, NE])
                                i1 = ve.tensor_tensor(eq[:, t], other, own, ALU.is_equal)
                                i2 = ve.tensor_tensor(gt[:, t], other, own, ALU.is_gt)
                            i1.then_inc(gate.sem, 1)
                            i2.then_inc(gate.sem, 1)
                            ve.wait_ge(gate.sem, g(8))
                            ve.tensor_tensor(eq[:].rearrange("p t a b -> p t (a b)"), eq[:].rearrange("p t a b -> p t (a b)"),
                                             tri[:].rearrange("p a b -> p (a b)").unsqueeze(1).to_broadcast([P, NP, NE * NE]),
                                             ALU.mult).then_inc(gate.sem, 1)
                            ve.wait_ge(gate.sem, g(9))
                            flat = lambda a: a[:].rearrange("p t a b -> p (t a b)")
                            ve.tensor_tensor(flat(gt), flat(gt), flat(eq), ALU.add).then_inc(gate.sem, 1)
                            ve.wait_ge(gate.sem, g(10))
                            ve.tensor_reduce(rank[:].rearrange("p t e -> p (t e)"), gt[:].rearrange("p t a b -> p (t a) b"),
                                             X, ALU.add).then_inc(gate.sem, 1)
                            ve.wait_ge(gate.sem, g(11))
                            ve.tensor_scalar(rank[:], rank[:], 2.0, None, ALU.is_lt).then_inc(gate.sem, 1)
                            ve.wait_ge(gate.sem, g(12))
                            ve.tensor_tensor(cwl[:], rank[:], lg[:], ALU.mult).then_inc(gate.sem, 1)
                            ve.wait_ge(gate.sem, g(13))
                            ve.tensor_scalar(cw[:, b, :], cwl[:].rearrange("p t e -> p (t e)"), 1.0 / WSCALE, None, ALU.mult)
                            ve.wait_ge(xf_ok.sem, xf_ok.at(b, 2))
                            ve.wait_ge(hi_ok.sem, hi_ok.at(b, 2))
                            ve.tensor_tensor(x16[:, b, T:2 * T], xf[:], xh[:], ALU.subtract).then_inc(lo_ok.sem, 1)
                            ve.wait_ge(b_ps.sem, b_ps.at(b, 1))
                            ve.tensor_tensor(xn[:].rearrange("p t c -> p (t c)"), banks(0, 2),
                                             t2[:].rearrange("p t c -> p (t c)"), ALU.add).then_inc(b_ok.sem, 1)
                            ve.wait_ge(b_ok.sem, b_ok.at(b, 1))
                            ve.wait_ge(lo_ok.sem, lo_ok.at(b, 1))
                            ve.sem_inc(turn_done, 1)

                    @block.tensor
                    def _(pe):
                        with pe.Fori(0, NB) as b:
                            pe.wait_ge(turn_done, b * 4)
                            pe.wait_ge(lt_in.sem, lt_in.at(b, 1))
                            for u in range(2):
                                pe.matmul(bank(u), wqkv2[:, 0:C], lt[:, 512 * u:512 * u + 512], start=True, stop=True)\
                                    .then_inc(qT_ps.sem, 1)
                            pe.wait_ge(klm_ok.sem, klm_ok.at(b, 1))
                            pe.wait_ge(klz_in.sem, klz_in.at(b, 3))

                            def scores(t):
                                if t % 4 == 0:
                                    pe.wait_ge(qT_ok.sem, qT_ok.at(b, t // 4 + 1))
                                if t >= 2:
                                    pe.wait_ge(d_ok.sem, d_ok.at(b, t - 1))
                                pe.matmul(bank(2 + t % 2), qT[:, t * P:(t + 1) * P], klm[:].rearrange("p h l -> p (h l)"),
                                          start=True, stop=True).then_inc(s_ps.sem, 1)

                            def turned(t):
                                pe.wait_ge(e_ok.sem, e_ok.at(b, t + 1))
                                if t >= 2:
                                    pe.wait_ge(eT_ok.sem, eT_ok.at(b, t - 1))
                                for h in range(4):
                                    i = pe.transpose(bank(4 + t % 2)[:, h * P:(h + 1) * P],
                                                     e1[:, t % 2, 2 * h:2 * h + 2, :].rearrange("p a l -> p (a l)"), ident[:])
                                i.then_inc(eT_ps.sem, 1)

                            def values(t):
                                pe.wait_ge(eT_ok.sem, eT_ok.at(b, t + 1))
                                if t >= 2:
                                    pe.wait_ge(on_ok.sem, on_ok.at(b, t - 1))
                                for h in range(4):
                                    w = 2 * (AD + 1)
                                    i = pe.matmul(bank(6 + t % 2)[:, w * h:w * h + w], p1T[:, t % 2, h, :],
                                                  zd[:, h].rearrange("p a d -> p (a d)"), start=True, stop=True)
                                i.then_inc(o_ps.sem, 1)

                            def merge(t):
                                pe.wait_ge(on_ok.sem, on_ok.at(b, t + 1))
                                if t == 0:
                                    pe.wait_ge(qT_ok.sem, qT_ok.at(b, 2))
                                if t >= 2:
                                    pe.wait_ge(t2_ok.sem, t2_ok.at(b, t - 1))
                                pe.transpose(bank(t % 2)[:, 0:P], on[:, t % 2, :], ident[:]).then_inc(onT_ps.sem, 1)

                            def project(t):
                                pe.wait_ge(onT_ok.sem, onT_ok.at(b, t + 1))
                                pe.matmul(bank(t % 2)[:, C:2 * C], onT[:, t % 2, :], wout[:], start=True, stop=False)
                                pe.matmul(bank(t % 2)[:, C:2 * C], lt[:, t * P:(t + 1) * P], wvc[:], start=False, stop=True)\
                                    .then_inc(w_ps.sem, 1)

                            scores(0)
                            scores(1)
                            for t in range(NP):
                                turned(t)
                                if t + 2 < NP:
                                    scores(t + 2)
                                if t >= 1:
                                    merge(t - 1)
                                values(t)
                                if t >= 1:
                                    project(t - 1)
                            merge(NP - 1)
                            project(NP - 1)
                            pe.wait_ge(d_ok.sem, d_ok.at(b, NP))
                            for t in range(NP):
                                pe.wait_ge(xn_ok.sem, xn_ok.at(b, t + 1))
                                i = pe.transpose(bank(2 + t // 4)[:, (t % 4) * P:(t % 4 + 1) * P], xn[:, t, :], ident[:])
                                if t % 4 == 3:
                                    i.then_inc(xf_ps.sem, 1)
                            for t in range(NP):
                                pe.wait_ge(xf_ok.sem, xf_ok.at(b, t // 4 + 1))
                                i = pe.matmul(bank(4)[:, NE * t:NE * t + NE], xf[:, t * P:(t + 1) * P], gw[:],
                                              start=True, stop=True)
                            i.then_inc(lg_ps.sem, 1)
                            pe.wait_ge(gate.sem, gate.at(b, 13))
                            for t in range(NP):
                                i = pe.transpose(bank(5 + t // 4)[0:NE, (t % 4) * P:(t % 4 + 1) * P], cwl[:, t, :], ident[:])
                            i.then_inc(cwT_ps.sem, 1)
                            pe.wait_ge(cwT_ok.sem, cwT_ok.at(b, 1))
                            pe.wait_ge(t2_ok.sem, t2_ok.at(b, NP))
                            for t in range(NP):
                                i = pe.matmul(bank(t // 4)[:, (t % 4) * C:(t % 4 + 1) * C], cwT[:, t * P:(t + 1) * P], b2r[:],
                                              start=True, stop=True)
                            i.then_inc(b_ps.sem, 1)
                            pe.sem_inc(turn_done, 1)

        def phase_experts(lnT):
            NC = 2 * NX * FC
            with ExitStack() as c1:
                def sb(name, shape, dt=F32):
                    return c1.enter_context(nc.sbuf_tensor(name, shape, dt))

                acc = sb("e_acc", [P, NP, C])
                g32 = sb("e_g32", [P, 4, 512])
                ghi = sb("e_ghi", [P, 4, 512], F16)
                glo = sb("e_glo", [P, 4, 512], F16)
                x16 = lnT[:].bitcast(F16)
                NG = 2 * (NE + 1)

                r_in = signal("e_r_in", 1, 16)
                h_ps = signal("e_h_ps", NC)
                g_ok = signal("e_g_ok", NC)
                ghi_a = signal("e_ghi_a", NC // 2)
                ghi_v = signal("e_ghi_v", NC // 2)
                glo_ok = signal("e_glo_ok", NC)
                y_ps = signal("e_y_ps", NC)
                acc_ok = signal("e_acc_ok", NG)
                out_ok = signal("e_out_ok", 2, 16)

                def group(c):
                    u, e = c // (NX * FC), c // FC % NX
                    return u * (NE + 1) + max(e - 1, 0)

                with nc.Block() as block:
                    @block.sync
                    def _(sp):
                        with sp.Fori(0, NB) as b:
                            sp.wait_ge(out_ok.sem, out_ok.at(b, 0))
                            apart(sp)
                            sp.dma_start(acc[:], res[b].rearrange("(t p) c -> p t c", p=P)).then_inc(r_in.sem, 16)
                            for u in range(2):
                                sp.wait_ge(acc_ok.sem, acc_ok.at(b, (u + 1) * (NE + 1)))
                                apart(sp)
                                sp.dma_start(out[b].rearrange("(t p) c -> p t c", p=P)[:, 4 * u:4 * u + 4, :],
                                             acc[:, 4 * u:4 * u + 4, :]).then_inc(out_ok.sem, 16)
                        sp.wait_ge(out_ok.sem, out_ok.at(NB, 0))

                    @block.scalar
                    def _(ac):
                        with ac.Fori(0, NB) as b:
                            for c in range(NC):
                                e, f = c // FC % NX, c % FC
                                ac.wait_ge(h_ps.sem, h_ps.at(b, c + 1))
                                ac.wait_ge(glo_ok.sem, glo_ok.at(b, c - 3) if c >= 4 else glo_ok.at(b, 0))
                                ac.activation(g32[:, c % 4, :], bank(c % 3), ACT.Gelu, bias=b1[:, e, f:f + 1],
                                              scale=1.0 / WSCALE).then_inc(g_ok.sem, 1)
                                if f < 2:
                                    ac.wait_ge(y_ps.sem, y_ps.at(b, c - 3) if c >= 4 else y_ps.at(b, 0))
                                    ac.activation(ghi[:, c % 4, :], bank(c % 3), ACT.Gelu, bias=b1[:, e, f:f + 1],
                                                  scale=1.0 / WSCALE).then_inc(ghi_a.sem, 1)

                    @block.vector
                    def _(ve):
                        with ve.Fori(0, NB) as b:
                            def add_up(n):
                                u, e = n // (NE + 1), n % (NE + 1)
                                last = (u * NX + e + 1) * FC + FC
                                ve.wait_ge(y_ps.sem, y_ps.at(b, last))
                                bk = bank(4 + n % 2)
                                if e == 0:
                                    if u == 0:
                                        ve.wait_ge(r_in.sem, r_in.at(b, 1))
                                    a = acc[:, 4 * u:4 * u + 4, :].rearrange("p t c -> p (t c)")
                                    ve.scalar_tensor_tensor(out=a, in0=bk, scalar=1.0 / WSCALE, in1=a, op0=ALU.mult,
                                                            op1=ALU.add).then_inc(acc_ok.sem, 1)
                                    return
                                ve.wait_ge(acc_ok.sem, acc_ok.at(b, n))
                                for t in range(4):
                                    tt = 4 * u + t
                                    i = ve.scalar_tensor_tensor(out=acc[:, tt, :], in0=bk[:, C * t:C * t + C],
                                                                scalar=cw[:, b, tt * NE + e - 1:tt * NE + e],
                                                                in1=acc[:, tt, :], op0=ALU.mult, op1=ALU.add)
                                i.then_inc(acc_ok.sem, 1)

                            for c in range(NC):
                                f = c % FC
                                ve.wait_ge(g_ok.sem, g_ok.at(b, c + 1))
                                ve.wait_ge(y_ps.sem, y_ps.at(b, c - 3) if c >= 4 else y_ps.at(b, 0))
                                if f >= 2:
                                    ve.tensor_copy(ghi[:, c % 4, :], g32[:, c % 4, :]).then_inc(ghi_v.sem, 1)
                                    ve.wait_ge(ghi_v.sem, ghi_v.at(b, 2 * (c // FC) + f - 1))
                                else:
                                    ve.wait_ge(ghi_a.sem, ghi_a.at(b, 2 * (c // FC) + f + 1))
                                ve.tensor_tensor(glo[:, c % 4, :], g32[:, c % 4, :], ghi[:, c % 4, :], ALU.subtract)\
                                    .then_inc(glo_ok.sem, 1)
                                if f == 3 and c // FC >= 1:
                                    done = c // FC - 1
                                    if done % NX != 0:
                                        add_up(done // NX * (NE + 1) + done % NX - 1)
                            add_up(NG - 1)

                    @block.tensor
                    def _(pe):
                        with pe.Fori(0, NB) as b:
                            def hidden(c):
                                u, e, f = c // (NX * FC), c // FC % NX, c % FC
                                if c >= 3:
                                    pe.wait_ge(g_ok.sem, g_ok.at(b, c - 2))
                                    k = c - 3
                                    if k % FC < 2:
                                        pe.wait_ge(ghi_a.sem, ghi_a.at(b, 2 * (k // FC) + k % FC + 1))
                                else:
                                    pe.wait_ge(g_ok.sem, g_ok.at(b, 0))
                                    pe.wait_ge(ghi_a.sem, ghi_a.at(b, 0))
                                w = slice(f * P, f * P + P)
                                xhi = x16[:, b, 512 * u:512 * u + 512]
                                xlo = x16[:, b, T + 512 * u:T + 512 * u + 512]
                                pe.matmul(bank(c % 3), w1hi[:, e, w], xhi, start=True, stop=False)
                                pe.matmul(bank(c % 3), w1hi[:, e, w], xlo, start=False, stop=False)
                                pe.matmul(bank(c % 3), w1lo[:, e, w], xhi, start=False, stop=True).then_inc(h_ps.sem, 1)

                            def output(c):
                                e, f = c // FC % NX, c % FC
                                n = group(c)
                                first = f == 0 and e != 1
                                if first:
                                    pe.wait_ge(acc_ok.sem, acc_ok.at(b, n - 1) if n >= 2 else acc_ok.at(b, 0))
                                pe.wait_ge(glo_ok.sem, glo_ok.at(b, c + 1))
                                for t in range(4):
                                    o = bank(4 + n % 2)[:, C * t:C * t + C]
                                    s = slice(t * P, t * P + P)
                                    pe.matmul(o, ghi[:, c % 4, s], w2hi[:, e, f, :], start=first and t == 0, stop=False,
                                              skip_group_check=True)
                                    pe.matmul(o, ghi[:, c % 4, s], w2lo[:, e, f, :], start=False, stop=False,
                                              skip_group_check=True)
                                    i = pe.matmul(o, glo[:, c % 4, s], w2hi[:, e, f, :], start=False,
                                                  stop=True, skip_group_check=True)
                                i.then_inc(y_ps.sem, 1)

                            hidden(0)
                            hidden(1)
                            for c in range(NC):
                                if c + 2 < NC:
                                    hidden(c + 2)
                                output(c)

        with ExitStack() as first:
            W = {}
            phase_setup(first, W)
            phase_ends()
            phase_windows(first, W)
            phase_ends()
        lnT = sb("lnT", [P, NB, T])
        with ExitStack() as c2:
            def sb2(name, shape):
                return c2.enter_context(nc.sbuf_tensor(name, shape, F32))

            klA = sb2("klA", [P, NB, LM])
            zA = sb2("zA", [P, NB, 4 * AD])
            with ExitStack() as c3:
                def sb3(name, shape):
                    return c3.enter_context(nc.sbuf_tensor(name, shape, F32))

                xA = sb3("xA", [P, NB, 4 * LM])
                xTA = sb3("xTA", [LM, NB, 4 * P])
                yA = sb3("yA", [P, NB, 4 * AD])
                stR = sb3("stR", [P, NB, 4])
                stC = sb3("stC", [LM, NB, AH])
                phase_landmarks(lnT, klA, xA, xTA, yA, stR, stC)
                phase_pinv(xA, xTA, yA, zA, stR, stC)
            phase_mix(lnT, klA, zA)
        phase_experts(lnT)


def host_arrays(inp):
    rel, mask, sel, _, _ = window_constants()
    f = lambda a: np.ascontiguousarray(a)
    rows = lambda a, *s: f(np.broadcast_to(np.reshape(a, (1, *s)), (P, *s)))
    I = {k: np.asarray(v) for k, v in inp.items()}
    L0 = lambda k: I["L0_conv_" + k]
    w1 = np.concatenate([I["L1_ffn_sw1"], I["L1_ffn_rw1"]])
    w2 = np.concatenate([I["L1_ffn_sw2"], I["L1_ffn_rw2"]])
    bb = np.concatenate([I["L1_ffn_sb1"], I["L1_ffn_rb1"]])
    kernel_w = I["L1_attn_conv_w"][:, 0]
    hh, cc = np.meshgrid(np.arange(AH), np.arange(AD), indexing="ij")
    hh, cc = hh.reshape(-1), cc.reshape(-1)
    convT = kernel_w[hh[None, :] - hh[:, None] + 16, cc[None, :] % 2, cc[:, None]]
    convmask = (cc[None, :] // 2 == cc[:, None] // 2).astype(np.float32)
    headmask = np.zeros((P, AH), np.float32)
    headmask[np.arange(P), hh] = 0.25
    i64 = np.concatenate([np.eye(LM, dtype=np.float32)] * 2)
    wqkv2 = I["L1_attn_Wqkv"]
    return {
        "x": f(I["x"]).reshape(-1, T, C),
        "ident": np.eye(P, dtype=np.float32), "ident16": np.eye(P, dtype=np.float16),
        "i64": i64, "tri": rows(np.tril(np.ones((NE, NE), np.float32), -1), NE, NE), "wqkv2": f(wqkv2), "wvT": f(wqkv2[:, 2 * C:].T), "wout": f(I["L1_attn_Wout"]),
        "bout": rows(I["L1_attn_bout"], C), "gw": f(I["L1_ffn_gate_w"].T), "gb": rows(I["L1_ffn_gate_b"], NE),
        "b2r": f(I["L1_ffn_rb2"]), "b2s": rows(I["L1_ffn_sb2"], 2, C), "headmask": headmask,
        "b1": f(bb.reshape(NX, FC, P).transpose(2, 0, 1)), "convT": f(convT), "convmask": convmask,
        "w1": f(w1.transpose(2, 0, 1)).reshape(P, NX * F),
        "w2": f(w2.reshape(NX, C, FC, P).transpose(3, 0, 2, 1)).reshape(P, NX * F),
        "wqkT": f(L0("qkv_w").T), "qb": rows(np.concatenate([L0("q_bias"), np.zeros_like(L0("q_bias"))]), 2 * C),
        "projT": f(L0("proj_w").T), "projb": rows(L0("proj_b"), C),
        "vbcol": f(np.broadcast_to(L0("v_bias")[:, None], (C, P))),
        "g1": rows(L0("norm1_g"), C), "be1": rows(L0("norm1_b"), C),
        "g2": rows(L0("norm2_g"), C), "be2": rows(L0("norm2_b"), C),
        "f1T": f(L0("fc1_w").T), "f1b": f(L0("fc1_b").reshape(FC, P).T),
        "f2T": f(L0("fc2_w").T.reshape(FC, P, C).transpose(1, 0, 2)), "f2b": rows(L0("fc2_b"), C),
        "ls": rows(L0("logit_scale").reshape(NH), NH), "cpw1": f(L0("cpb_w1").T), "cpb1": f(L0("cpb_b1")[:, None]),
        "cpw2": f(L0("cpb_w2").T), "rel": rel, "mask": mask, "sel": sel,
    }


def kernel(**inputs):
    import concourse.bacc as bacc
    from concourse.bass_utils import run_bass_kernel_spmd

    nc = bacc.Bacc("TRN2", target_bir_lowering=False, num_devices=1)
    arrays = {f"in_{k}": a for k, a in host_arrays(inputs).items()}
    A = {k[3:]: nc.dram_tensor(k, a.shape, mybir.dt.from_np(a.dtype), kind="ExternalInput").ap()
         for k, a in arrays.items()}
    NB = arrays["in_x"].shape[0]
    out = nc.dram_tensor("out_dram", (NB, T, C), F32, kind="ExternalOutput").ap()
    build(nc, NB, A, out)
    r = run_bass_kernel_spmd(nc, [arrays], core_ids=[0])
    return r.results[0]["out_dram"].reshape(NB, HW, HW, C)
```

```python
from contextlib import ExitStack
import math

import numpy as np

import concourse.bass as bass
from concourse import mybir

F32 = mybir.dt.float32
F16 = mybir.dt.float16
ALU = mybir.AluOpType
ACT = mybir.ActivationFunctionType
X = mybir.AxisListType.X

C = 128
P = 128
HW = 32
WS, SS = 8, 4
N = WS * WS
T = HW * HW
NP = T // P
NH, HD = 16, 8
AH, AD = 8, 16
LM = 64
SEG = T // LM
F = 512
NE = 8
NX = 10
FC = F // P
WSCALE = 64.0
ITERS = 6
LOADED = 16 * 31


class Signal:

    def __init__(self, sem, per, by=1):
        self.sem, self.per, self.by = sem, per, by

    def at(self, turn, n):
        return turn * (self.per * self.by) + n * self.by


def window_constants():
    r = np.arange(-(WS - 1), WS, dtype=np.float32)
    tab = np.stack(np.meshgrid(r, r, indexing="ij"), axis=-1) / (WS - 1) * 8.0
    tab = (np.sign(tab) * np.log2(np.abs(tab) + 1.0) / np.log2(8.0)).astype(np.float32)
    rel = np.ascontiguousarray(tab.reshape(-1, 2).T)
    ch, rr, cc = np.meshgrid(np.arange(2), np.arange(WS), np.arange(4), indexing="ij")
    y, x = rr.reshape(-1), (4 * ch + cc).reshape(-1)
    img = np.zeros((HW, HW), np.float32)
    cnt = 0
    for hs in (slice(0, -WS), slice(-WS, -SS), slice(-SS, None)):
        for ws in (slice(0, -WS), slice(-WS, -SS), slice(-SS, None)):
            img[hs, ws] = cnt
            cnt += 1
    mask = np.zeros((P, 4, N), np.float32)
    for kind in range(4):
        wy, half = (3 if kind >= 2 else 0), kind % 2
        for w in range(2):
            m = img[8 * wy + y, 8 * (2 * half + w) + x]
            mask[64 * w:64 * w + 64, kind] = np.where(m[None, :] != m[:, None], -100.0, 0.0)
    sel = np.zeros((NH, NH, N), np.float16)
    for i in range(NH):
        sel[i, i] = 1.0
    return rel, mask, sel.reshape(NH, NH * N), y, x


def build(nc, NB, A, out):
    _, _, _, KY, KX = window_constants()
    with ExitStack() as ctx:
        def sb(name, shape, dt=F32):
            return ctx.enter_context(nc.sbuf_tensor(name, shape, dt))

        phase_sems = []

        def sem(name):
            phase_sems.append(nc.alloc_semaphore(name))
            return phase_sems[-1]

        def phase_ends():
            nc.clear_and_free_semaphores(phase_sems)
            phase_sems.clear()
            nc.all_engine_barrier()

        def signal(name, per, by=1):
            return Signal(sem(name), per, by)

        mid = nc.dram_tensor("mid_dram", [NB, T, C], F32).ap()
        res = nc.dram_tensor("res_dram", [NB, T, C], F32).ap()
        psum = ctx.enter_context(nc.psum_tensor("psum", [P, 8 * 512], F32))

        def apart(eng):
            eng.sem_inc(s_apart, 1)

        def banks(i, n):
            return psum[:, 512 * i:512 * (i + n)]

        def bank(i):
            return banks(i, 1)

        ident = sb("ident", [P, P])
        ident16 = sb("ident16", [P, P], F16)
        w1hi = sb("w1hi", [P, NX, F], F16)
        w1lo = sb("w1lo", [P, NX, F], F16)
        w2hi = sb("w2hi", [P, NX, FC, C], F16)
        w2lo = sb("w2lo", [P, NX, FC, C], F16)
        b1 = sb("b1", [P, NX, FC])
        wqkv2 = sb("wqkv2", [P, 3 * C])
        wvc = sb("wvc", [P, C])
        wout = sb("wout", [P, C])
        gw = sb("gw", [P, NE])
        gb = sb("gb", [P, NE])
        headmask = sb("headmask", [P, AH])
        nhalf = sb("nhalf", [P, NP])
        ones1 = sb("ones1", [1, P])

        s_load = sem("s_load")
        s_apart = sem("s_apart")
        phase_sems.clear()

        def phase_setup(c1, W):
            with ExitStack() as c2:
                def sb(name, shape, dt=F32):
                    return c2.enter_context(nc.sbuf_tensor(name, shape, dt))

                def keep(name, shape, dt=F32):
                    W[name] = c1.enter_context(nc.sbuf_tensor(name, shape, dt))
                    return W[name]

                wqkT = keep("wqkT", [P, 3 * C])
                qb = keep("qb", [P, 2 * C])
                projT = keep("projT", [P, C])
                projb = keep("projb", [P, C])
                g1, be1, g2, be2 = (keep(n, [P, C]) for n in ("g1", "be1", "g2", "be2"))
                f1T = keep("f1T", [P, F])
                f1b = keep("f1b", [P, FC])
                f2T = keep("f2T", [P, FC, C])
                f2b = keep("f2b", [P, C])
                sc = keep("sc", [P, NH])
                sel = keep("sel", [NH, NH * N], F16)
                bth = keep("bth", [P, 4, 4, 4, N], F16)
                btl = keep("btl", [P, 4, 4, 4, N], F16)
                vbcol = sb("vbcol", [P, P])
                cpw1 = sb("cpw1", [2, P])
                cpb1 = sb("cpb1", [P, 1])
                cpw2 = sb("cpw2", [P, NH])
                rel = sb("rel", [2, 225])
                relh = sb("relh", [P, 15, 15])
                relx = sb("relx", [P, 12, 15, 4])
                sig = sb("sig", [P, N, NH])
                mask = sb("mask", [P, 4, N])
                btmp = sb("btmp", [P, 2, 4, N])
                cm = sb("cm", [P, 4, C])

                loads = [(ident, "ident"), (ident16, "ident16"), (wqkv2, "wqkv2"), (wout, "wout"), (gw, "gw"), (gb, "gb"),
                         (headmask, "headmask"), (b1, "b1"),
                         (wqkT, "wqkT"), (qb, "qb"), (projT, "projT"), (projb, "projb"), (vbcol, "vbcol"),
                         (g1, "g1"), (be1, "be1"), (g2, "g2"), (be2, "be2"), (f1T, "f1T"), (f1b, "f1b"),
                         (f2T, "f2T"), (f2b, "f2b"), (sc, "ls"), (cpw1, "cpw1"), (cpb1, "cpb1"), (cpw2, "cpw2"),
                         (rel, "rel"), (mask, "mask"), (sel, "sel")]
                stage = sb("stage", [P, NX * F])
                assert LOADED == 16 * (len(loads) + 3)

                s_w = sem("s_w")
                s_wdone = sem("s_wdone")
                s_pe = sem("s_pe")
                s_ac = sem("s_ac")
                s_ve = sem("s_ve")
                s_po = sem("s_po")
                s_rel = sem("s_rel")
                with nc.Block() as block:
                    @block.sync
                    def _(sp):
                        for dst, name in loads:
                            sp.dma_start(dst[:], A[name]).then_inc(s_load, 16)
                        sp.dma_start(cm[:, 0, :], A["convT"]).then_inc(s_load, 16)
                        sp.dma_start(cm[:, 1, :], A["convmask"]).then_inc(s_load, 16)
                        sp.dma_start(cm[:, 2, :], A["wvT"]).then_inc(s_load, 16)
                        sp.dma_start(stage[:], A["w1"]).then_inc(s_w, 16)
                        sp.wait_ge(s_wdone, 2)
                        sp.dma_start(stage[:], A["w2"]).then_inc(s_w, 16)

                    @block.gpsimd
                    def _(gp):
                        gp.memset(nhalf[:], -0.5).then_inc(s_po, 1)
                        gp.memset(ones1[:], 1.0).then_inc(s_po, 1)
                        gp.wait_ge(s_ac, 2)
                        for i in range(12):
                            gp.tensor_copy(relx[:, i], relh[:, :, i:i + 4]).then_inc(s_rel, 1)

                    @block.scalar
                    def _(ac):
                        ac.wait_ge(s_ve, 1)
                        ac.activation(sc[:], sc[:], ACT.Exp).then_inc(s_ac, 1)
                        ac.wait_ge(s_pe, 1)
                        ac.activation(relh[:].rearrange("q a b -> q (a b)"), bank(0)[:, 0:225], ACT.Relu,
                                      bias=cpb1[:, 0:1]).then_inc(s_ac, 1)
                        ac.wait_ge(s_pe, 2)
                        for i in range(2):
                            ac.activation(sig[:, 32 * i:32 * i + 32, :].rearrange("q m h -> q (m h)"), bank(1 + i)[:, :],
                                          ACT.Sigmoid).then_inc(s_ac, 1)
                        ac.wait_ge(s_pe, 5)
                        ac.activation(wvc[:], bank(3)[:, 0:C], ACT.Copy).then_inc(s_ac, 1)

                    @block.vector
                    def _(ve):
                        ve.wait_ge(s_load, LOADED)
                        ve.tensor_scalar(sc[:], sc[:], math.log(100.0), None, ALU.min).then_inc(s_ve, 1)
                        ve.tensor_tensor(cm[:, 0, :], cm[:, 0, :], cm[:, 1, :], ALU.mult).then_inc(s_ve, 1)
                        ve.wait_ge(s_pe, 4)
                        ve.tensor_copy(cm[:, 3, :], bank(4)[:, 0:C]).then_inc(s_ve, 1)
                        ve.tensor_tensor(projb[:], projb[:], bank(5)[:, 0:C], ALU.add).then_inc(s_ve, 1)
                        n = 4
                        ve.wait_ge(s_ac, 4)
                        k = 0
                        for kind in range(4):
                            for j in range(4):
                                t = btmp[:, k % 2]
                                src = sig[:].rearrange("q m (g j) -> q g m j", j=4)[:, :, :, j]
                                ve.scalar_tensor_tensor(out=t, in0=src, scalar=16.0,
                                                        in1=mask[:, kind, :].unsqueeze(1).to_broadcast([P, 4, N]),
                                                        op0=ALU.mult, op1=ALU.add).then_inc(s_ve, 1)
                                n += 1
                                ve.wait_ge(s_ve, n)
                                ve.tensor_copy(bth[:, kind, j], t).then_inc(s_ve, 1)
                                n += 1
                                ve.wait_ge(s_ve, n)
                                ve.tensor_tensor(btl[:, kind, j], t, bth[:, kind, j], ALU.subtract).then_inc(s_ve, 1)
                                n += 1
                                k += 1
                                ve.wait_ge(s_ve, n)
                        wd = 0
                        for which, (hi, lo) in enumerate(((w1hi, w1lo), (w2hi, w2lo))):
                            ve.wait_ge(s_w, 16 * which + 16)
                            src = stage[:]
                            hi2 = hi[:].rearrange("p a b -> p (a b)") if not which else hi[:].rearrange("p a b c -> p (a b c)")
                            lo2 = lo[:].rearrange("p a b -> p (a b)") if not which else lo[:].rearrange("p a b c -> p (a b c)")
                            ve.tensor_scalar(hi2, src, WSCALE, None, ALU.mult).then_inc(s_wdone, 1)
                            wd += 1
                            ve.wait_ge(s_wdone, wd)
                            ve.scalar_tensor_tensor(out=lo2, in0=src, scalar=WSCALE, in1=hi2, op0=ALU.mult,
                                                    op1=ALU.subtract).then_inc(s_wdone, 1)
                            wd += 1

                    @block.tensor
                    def _(pe):
                        pe.wait_ge(s_load, LOADED)
                        pe.matmul(bank(0)[:, 0:225], cpw1[:], rel[:], start=True, stop=True).then_inc(s_pe, 1)
                        pe.wait_ge(s_rel, 12)
                        for m in range(N):
                            ky, kx = int(KY[m]), int(KX[m])
                            for half in range(2):
                                for c in range(2):
                                    w = relx[:, 7 - kx + 4 * c, 7 - ky:15 - ky, :].rearrange("q a b -> q (a b)")
                                    i = pe.matmul(bank(1 + m // 32)[64 * half + 32 * c:64 * half + 32 * c + 32,
                                                                    (m % 32) * NH:(m % 32 + 1) * NH],
                                                  w, cpw2[:], start=True, stop=True)
                        i.then_inc(s_pe, 1)
                        pe.wait_ge(s_ve, 2)
                        pe.matmul(bank(4)[:, 0:C], cm[:, 0, :], wout[:], start=True, stop=True)
                        pe.matmul(bank(5)[:, 0:C], vbcol[:], projT[:], start=True, stop=True).then_inc(s_pe, 2)
                        pe.wait_ge(s_ve, 4)
                        pe.matmul(bank(3)[:, 0:C], cm[:, 2, :], cm[:, 3, :], start=True, stop=True).then_inc(s_pe, 1)

        def phase_windows(c1, W):
            I32 = mybir.dt.int32

            def sb(name, shape, dt=F32):
                return c1.enter_context(nc.sbuf_tensor(name, shape, dt))

            wqkT, qb, projT, projb, g1, be1, g2, be2, f1T, f1b, f2T, f2b, sel, bth, btl, sc = (
                W[k] for k in "wqkT qb projT projb g1 be1 g2 be2 f1T f1b f2T f2b sel bth btl sc".split())
            xw = sb("xw", [P, NP, C])
            xT = sb("xT", [P, 2, 2 * P])
            qk = sb("qk", [P, 2, 2, NH, HD])
            sq = sb("sq", [P, 2, 2 * C])
            nrm = sb("nrm", [P, 2, 2, NH])
            rsq = sb("rsq", [P, 2, 2 * NH])
            split = sb("split", [P, 2, 2, NH, 4, HD], F16)
            qkT = sb("qkT", [P, 2, 2, 4, P], F16)
            vd = sb("vd", [P, 2, 2, NH, HD + 1])
            mx = sb("mx", [P, NH])
            mT = sb("mT", [NH, P], F16)
            pr = sb("pr", [P, 2, 16, N])
            prT = sb("prT", [P, 2, 8, P])
            rs = sb("rs", [P, NH])
            on = sb("on", [P, 2, C])
            onT = sb("onT", [P, 2, P])
            y = sb("y", [P, 4, C])
            st = sb("st", [P, 4, 6])
            mv = sb("mv", [P, 4, 2])
            rstd = sb("rstd", [P, 4])
            x1 = sb("x1", [P, NP, C])
            x1T = sb("x1T", [P, 2, 4 * P])
            gl = sb("gl", [P, FC, 4 * P])
            z = sb("z", [P, 4, C])
            zt = sb("zt", [P, 4, 6])
            zv = sb("zv", [P, 4, 2])
            zr = sb("zr", [P, 4])
            xo = sb("xo", [P, 4, C])

            beside = psum[:, 0:4 * 512].rearrange("q (j c) -> q j c", j=4)
            heads, turned = beside[:, :, 0:256], beside[:, :, 256:512]
            psig = lambda name, per=1, by=1: signal("w_" + name, per, by)
            x_in = [psig(f"x_in{p}", 1, 16) for p in range(NP)]
            stored = [psig(f"stored{p}", 1, 16) for p in range(4)]
            ready = sem("w_ready")
            (xT_ps, xT_ok, qk_ps, qk_ok, sq_ok, ss_ok, rsq_ok, v_ps, v_ok, qn_ok, qkT_ps, qkT_ok, s_ps, mx_ok,
             mT_ps, mT_ok, sm_ps, pr_ok, prT_ps, prT_a, prT_v, o_ps, rs_ok, on_ok, onT_ps, onT_ok, pj_ps, y_ok, st_ok,
             mv_ok, ve_ok, rstd_ok, yn_ok, yg_ok, x1_ok, x1T_ps, x1T_ok, m_ps, z_ok, zt_ok, zv_ok, ze_ok,
             zr_ok, zn_ok, zg_ok, xo_ok) = (psig(k) for k in (
                 "xT_ps xT_ok qk_ps qk_ok sq_ok ss_ok rsq_ok v_ps v_ok qn_ok qkT_ps qkT_ok s_ps mx_ok "
                 "mT_ps mT_ok sm_ps pr_ok prT_ps prT_a prT_v o_ps rs_ok on_ok onT_ps onT_ok pj_ps y_ok st_ok "
                 "mv_ok ve_ok rstd_ok yn_ok yg_ok x1_ok x1T_ps x1T_ok m_ps z_ok zt_ok zv_ok ze_ok "
                 "zr_ok zn_ok zg_ok xo_ok").split())
            hi_ok, lo_ok = psig("hi_ok", 2), psig("lo_ok", 2)
            newton = psig("newton", 11)
            be_ok, bf_ok = psig("be_ok"), psig("bf_ok")
            h_ps, gl_ok = psig("h_ps"), psig("gl_ok")

            class Pair:

                def __init__(self, b, p):
                    if isinstance(b, int):
                        b, p = b + p // NP, p % NP
                    else:
                        b, p = (b + p // NP if p // NP else b), p % NP
                    self.b, self.p = b, p

                def real(self):
                    return not isinstance(self.b, int) or 0 <= self.b < NB

                def __add__(self, d):
                    return Pair(self.b, self.p + d)

                def __sub__(self, d):
                    return self + -d

            def met(eng, s, q, n=1):
                if q.real():
                    eng.wait_ge(s.sem, (s.per * s.by) * NP * q.b + s.by * (s.per * q.p + n))

            def landed(eng, q):
                eng.wait_ge(x_in[q.p].sem, 16 * PIECES[q.p] * (q.b + 1))

            def written(eng, q):
                if q.real():
                    k = q.p % 4
                    eng.wait_ge(stored[k].sem, 16 * (PIECES[k] + PIECES[k + 4]) * q.b
                                + 16 * (PIECES[k] + (PIECES[k + 4] if q.p >= 4 else 0)))

            PIECES = [4] * 6 + [8] * 2

            def pieces(q, dram):
                img = dram[q.b].rearrange("(y x) c -> y x c", y=HW)
                wy = q.p // 2
                for w in range(2):
                    for ch in range(2):
                        x0 = (WS * (2 * (q.p % 2) + w) + 4 * ch + SS) % HW
                        q0 = 64 * w + 32 * ch
                        if wy < 3:
                            yield q0, 32, img[8 * wy + SS:8 * wy + SS + 8, x0:x0 + 4, :]
                        else:
                            yield q0, 16, img[28:32, x0:x0 + 4, :]
                            yield q0 + 16, 16, img[0:4, x0:x0 + 4, :]

            def outputs_of(s):
                g = {3: (s - 7, (0, 1)), 0: (s - 8, (2,)), 1: (s - 9, (3,))}.get(s.p % 4)
                return [g[0] + r for r in g[1]] if g else []

            def hidden_of(s):
                return s - 6 if s.p % 4 == 2 else None

            def slots(eng, body):
                for s in range(-2, NP * min(2, NB - 1)):
                    body(Pair(0, s))
                if NB > 3:
                    with eng.Fori(2, NB - 1) as b:
                        for s in range(NP):
                            body(Pair(b, s))
                for s in range(NP):
                    body(Pair(NB - 1, s))
                for s in range(NP + 3):
                    body(Pair(NB, s))

            with nc.Block() as block:
                @block.sync
                def _(sp):
                    def load(q):
                        if q.real():
                            met(sp, x1_ok, q - 8)
                            apart(sp)
                            for q0, n, src in pieces(q, A["x"]):
                                sp.dma_start(xw[q0:q0 + n, q.p, :], src).then_inc(x_in[q.p].sem, 16)

                    for p in range(3):
                        load(Pair(0, p))

                    def slot(s):
                        load(s + 5)
                        for q in outputs_of(s - 1):
                            if q.real():
                                met(sp, xo_ok, q)
                                apart(sp)
                                for q0, n, dst in pieces(q, mid):
                                    sp.dma_start(dst, xo[q0:q0 + n, q.p % 4, :]).then_inc(stored[q.p % 4].sem, 16)

                    slots(sp, slot)
                    for p in range(4, NP):
                        written(sp, Pair(NB - 1, p))

                @block.gpsimd
                def _(gp):
                    k = 2
                    gp.memset(vd[:], 0.0).then_inc(ready, 1)
                    gp.memset(split[:], 0.0).then_inc(ready, 1)
                    for p in range(2):
                        for w in range(2):
                            v = vd[:, p, w].rearrange("q (t k j) d -> q t k j d", t=2, k=2)
                            for t in range(2):
                                for half in range(2):
                                    gp.wait_ge(ready, k)
                                    gp.memset(v[64 * half:64 * half + 64, t, half, :, HD:HD + 1], 1.0).then_inc(ready, 1)
                                    k += 1
                    gp.wait_ge(ready, k)

                    def slot(s):
                        q = s - 2
                        if q.real():
                            met(gp, ve_ok, q)
                            r = rstd[:, q.p % 4:q.p % 4 + 1]
                            gp.tensor_tensor(r, r, nhalf[:, 0:1], ALU.pow).then_inc(rstd_ok.sem, 1)
                        q = s - 2
                        if q.real():
                            met(gp, rstd_ok, q)
                            met(gp, yn_ok, q)
                            yp = y[:, q.p % 4, :]
                            gp.tensor_tensor(yp, yp, g1[:], ALU.mult).then_inc(yg_ok.sem, 1)
                            met(gp, yg_ok, q)
                            gp.tensor_tensor(yp, yp, be1[:], ALU.add).then_inc(be_ok.sem, 1)
                        q = s + 2
                        if q.real():
                            met(gp, qk_ok, q)
                            met(gp, ss_ok, q - 2)
                            q2 = qk[:, q.p % 2].rearrange("q a h d -> q (a h d)")
                            gp.tensor_tensor(sq[:, q.p % 2, :], q2, q2, ALU.mult).then_inc(sq_ok.sem, 1)
                        for q in outputs_of(s - 1):
                            if q.real():
                                met(gp, zn_ok, q)
                                zp = z[:, q.p % 4, :]
                                gp.tensor_tensor(zp, zp, g2[:], ALU.mult).then_inc(zg_ok.sem, 1)
                                met(gp, zg_ok, q)
                                gp.tensor_tensor(zp, zp, be2[:], ALU.add).then_inc(bf_ok.sem, 1)
                        for q in outputs_of(s):
                            if q.real():
                                met(gp, ze_ok, q)
                                r = zr[:, q.p % 4:q.p % 4 + 1]
                                gp.tensor_tensor(r, r, nhalf[:, 0:1], ALU.pow).then_inc(zr_ok.sem, 1)

                    slots(gp, slot)

                @block.scalar
                def _(ac):
                    ac.wait_ge(ready, 18)

                    def hidden(s, f):
                        q0 = hidden_of(s)
                        if q0 is not None and q0.real():
                            if f == 0:
                                met(ac, m_ps, q0 - 1)
                            met(ac, h_ps, q0 + f)
                            ac.activation(gl[:, f, :], bank(7), ACT.Gelu, bias=f1b[:, f:f + 1]).then_inc(gl_ok.sem, 1)

                    def slot(s):
                        if s.real():
                            met(ac, mT_ps, s)
                            ac.activation(mT[:], bank(5)[0:NH, 384:512], ACT.Copy, scale=-1.0).then_inc(mT_ok.sem, 1)
                        q = s + 2
                        if q.real():
                            met(ac, xT_ps, q)
                            met(ac, v_ps, q - 2)
                            ac.activation(xT[:, q.p % 2, :].rearrange("q (w r t) -> q w r t", w=2, r=2),
                                          bank(5)[:, 0:P].rearrange("q (w t) -> q w t", w=2).unsqueeze(2)
                                          .to_broadcast([P, 2, 2, N]), ACT.Copy).then_inc(xT_ok.sem, 1)
                        if s.real():
                            met(ac, sm_ps, s)
                            met(ac, prT_ps, s - 2)
                            ac.activation(pr[:, s.p % 2].rearrange("q (j g) m -> q j (g m)", j=4), heads, ACT.Exp)\
                                .then_inc(pr_ok.sem, 1)
                        q = s + 1
                        if q.real():
                            met(ac, qn_ok, q)
                            met(ac, qkT_ps, q - 2)
                            for a in range(2):
                                dst = split[:, q.p % 2, a, :, 0:2 + a:1 + a, :]
                                ac.activation(dst, qk[:, q.p % 2, a].unsqueeze(2).to_broadcast([P, NH, 2, HD]), ACT.Copy)\
                                    .then_inc(hi_ok.sem, 1)
                            met(ac, v_ps, q)
                            met(ac, o_ps, q - 2)
                            for k in range(2):
                                src = bank(6)[64 * k:64 * k + 64, 0:2 * C].rearrange("q (u k j d) -> q u k j d", u=4, k=2, j=4)
                                dst = vd[64 * k:64 * k + 64, q.p % 2].rearrange("q w (t k j) d -> q (w t) k j d", t=2, k=2)
                                i = ac.activation(dst[:, :, k, :, 0:HD], src[:, :, k], ACT.Copy)
                            i.then_inc(v_ok.sem, 1)
                        if s.real():
                            met(ac, prT_ps, s)
                            met(ac, o_ps, s - 2)
                            ac.activation(prT[:, s.p % 2, 0:4, :].rearrange("q (j k) t -> q j (k t)", j=2), turned[:, 0:2, :],
                                          ACT.Copy).then_inc(prT_a.sem, 1)
                        if q.real():
                            met(ac, qkT_ps, q)
                            met(ac, s_ps, q - 2)
                            ac.activation(qkT[:, q.p % 2].rearrange("q a g t -> q (a g t)"), bank(6).bitcast(F16), ACT.Copy)\
                                .then_inc(qkT_ok.sem, 1)
                        q = s - 1
                        if q.real():
                            met(ac, onT_ps, q)
                            met(ac, pj_ps, q - 2)
                            ac.activation(onT[:, q.p % 2, :], bank(5)[:, 384:512], ACT.Copy).then_inc(onT_ok.sem, 1)
                        hidden(s, 0)
                        hidden(s, 1)
                        q = s - 2
                        if q.real():
                            met(ac, x1T_ps, q)
                            if q.p % 4 == 0:
                                met(ac, h_ps, q - 5)
                            ac.activation(x1T[:, q.p // 4, (q.p % 4) * P:(q.p % 4 + 1) * P], bank(6)[:, 0:P], ACT.Copy)\
                                .then_inc(x1T_ok.sem, 1)
                        hidden(s, 2)
                        hidden(s, 3)

                    slots(ac, slot)

                @block.vector
                def _(ve):
                    def rsqrt(q):
                        k = [0]

                        def done(i):
                            i.then_inc(newton.sem, 1)
                            k[0] += 1
                            met(ve, newton, q, k[0])

                        v = nrm[:, q.p % 2].rearrange("q a h -> q (a h)")
                        g, t = rsq[:, 0, :], rsq[:, 1, :]
                        done(ve.tensor_scalar(v, v, 1e-24, None, ALU.max))
                        done(ve.tensor_scalar(g.bitcast(I32), v.bitcast(I32), -0.5, float(0x5F3759DF), ALU.mult, ALU.add))
                        for it in range(3):
                            done(ve.tensor_tensor(t, g, g, ALU.mult))
                            done(ve.scalar_tensor_tensor(out=t, in0=t, scalar=-0.5, in1=v, op0=ALU.mult, op1=ALU.mult))
                            i = ve.scalar_tensor_tensor(out=(g, g, v)[it], in0=t, scalar=1.5, in1=g, op0=ALU.add, op1=ALU.mult)
                            if it < 2:
                                done(i)
                        i.then_inc(rsq_ok.sem, 1)

                    def slot(s):
                        q = s - 2
                        if q.real():
                            k = q.p % 4
                            met(ve, y_ok, q)
                            ve.bn_stats(st[:, k, :], y[:, k, :]).then_inc(st_ok.sem, 1)
                            met(ve, st_ok, q)
                            apart(ve)
                            ve.bn_aggr(mv[:, k, :], st[:, k, :]).then_inc(mv_ok.sem, 1)
                            met(ve, mv_ok, q)
                            ve.tensor_scalar(rstd[:, k:k + 1], mv[:, k, 1:2], 1e-5, None, ALU.add).then_inc(ve_ok.sem, 1)
                        q = s + 1
                        if q.real():
                            met(ve, ss_ok, q)
                            rsqrt(q)
                            met(ve, rsq_ok, q)
                            nq = nrm[:, q.p % 2]
                            ve.tensor_tensor(nq[:, 0, :], nq[:, 0, :], sc[:], ALU.mult).then_inc(newton.sem, 1)
                            met(ve, newton, q, 11)
                            q3 = qk[:, q.p % 2].rearrange("q a h d -> q (a h) d")
                            ve.tensor_tensor(q3, q3, nq.rearrange("q a h -> q (a h)").unsqueeze(2)
                                             .to_broadcast([P, 2 * NH, HD]), ALU.mult).then_inc(qn_ok.sem, 1)
                        q = s - 2
                        if q.real():
                            met(ve, rstd_ok, q)
                            k = q.p % 4
                            ve.tensor_scalar(y[:, k, :], y[:, k, :], mv[:, k, 0:1], rstd[:, k:k + 1],
                                             ALU.subtract, ALU.mult).then_inc(yn_ok.sem, 1)
                        for q in outputs_of(s):
                            if q.real():
                                k = q.p % 4
                                met(ve, m_ps, outputs_of(s)[-1])
                                c = 0 if k in (0, 2, 3) else C
                                ve.tensor_tensor(z[:, k, :], bank(7)[:, c:c + C], f2b[:], ALU.add).then_inc(z_ok.sem, 1)
                                met(ve, z_ok, q)
                                ve.bn_stats(zt[:, k, :], z[:, k, :]).then_inc(zt_ok.sem, 1)
                                met(ve, zt_ok, q)
                                apart(ve)
                                ve.bn_aggr(zv[:, k, :], zt[:, k, :]).then_inc(zv_ok.sem, 1)
                                met(ve, zv_ok, q)
                                ve.tensor_scalar(zr[:, k:k + 1], zv[:, k, 1:2], 1e-5, None, ALU.add).then_inc(ze_ok.sem, 1)
                        q = s + 2
                        if q.real():
                            met(ve, qk_ps, q)
                            q2 = qk[:, q.p % 2].rearrange("q a h d -> q (a h d)")
                            met(ve, lo_ok, q - 2, 2)
                            ve.tensor_tensor(q2, bank(5)[:, P:P + 2 * C], qb[:], ALU.add).then_inc(qk_ok.sem, 1)
                        q = s + 1
                        if q.real():
                            met(ve, hi_ok, q, 2)
                            for a in range(2):
                                ve.tensor_tensor(split[:, q.p % 2, a, :, 2 - a, :], qk[:, q.p % 2, a],
                                                 split[:, q.p % 2, a, :, 0, :], ALU.subtract).then_inc(lo_ok.sem, 1)
                        if s.real():
                            met(ve, prT_ps, s)
                            met(ve, o_ps, s - 2)
                            ve.tensor_copy(prT[:, s.p % 2, 4:8, :].rearrange("q (j k) t -> q j (k t)", j=2),
                                           turned[:, 2:4, :]).then_inc(prT_v.sem, 1)
                        q = s - 2
                        if q.real():
                            met(ve, be_ok, q)
                            ve.tensor_tensor(x1[:, q.p, :], y[:, q.p % 4, :], xw[:, q.p, :], ALU.add).then_inc(x1_ok.sem, 1)
                        q = s + 2
                        if q.real():
                            met(ve, sq_ok, q)
                            ve.tensor_reduce(nrm[:, q.p % 2].rearrange("q a h -> q (a h)"),
                                             sq[:, q.p % 2].rearrange("q (h d) -> q h d", d=HD), X, ALU.add)\
                                .then_inc(ss_ok.sem, 1)
                        for q in outputs_of(s - 1):
                            if q.real():
                                k = q.p % 4
                                met(ve, zr_ok, q)
                                ve.tensor_scalar(z[:, k, :], z[:, k, :], zv[:, k, 0:1], zr[:, k:k + 1],
                                                 ALU.subtract, ALU.mult).then_inc(zn_ok.sem, 1)
                        for q in outputs_of(s - 1):
                            if q.real():
                                k = q.p % 4
                                met(ve, bf_ok, q)
                                written(ve, q - 4)
                                ve.tensor_tensor(xo[:, k, :], z[:, k, :], x1[:, q.p, :], ALU.add).then_inc(xo_ok.sem, 1)
                        if s.real():
                            met(ve, o_ps, s)
                            met(ve, onT_ps, s - 2)
                            o = bank(4)[:, 0:NH * (HD + 1)].rearrange("q (h d) -> q h d", d=HD + 1)
                            ve.reciprocal(rs[:], o[:, :, HD]).then_inc(rs_ok.sem, 1)
                            met(ve, rs_ok, s)
                            ve.tensor_tensor(on[:, s.p % 2, :].rearrange("q (h d) -> q h d", d=HD), o[:, :, 0:HD],
                                             rs[:].unsqueeze(2).to_broadcast([P, NH, HD]), ALU.mult).then_inc(on_ok.sem, 1)
                        q = s - 1
                        if q.real():
                            k = q.p % 4
                            met(ve, pj_ps, q)
                            ve.tensor_tensor(y[:, k, :], bank(5)[:, P:2 * P], projb[:], ALU.add).then_inc(y_ok.sem, 1)
                        q = s + 1
                        if q.real():
                            met(ve, s_ps, q)
                            met(ve, mT_ps, q - 1)
                            ve.tensor_reduce(mx[:].rearrange("q (j g) -> q j g", j=4),
                                             heads.rearrange("q j (g m) -> q j g m", g=4), X, ALU.max).then_inc(mx_ok.sem, 1)

                    slots(ve, slot)

                @block.tensor
                def _(pe):
                    def scores(q):
                        if not q.real():
                            return
                        kind = (2 if q.p >= 6 else 0) + q.p % 2
                        met(pe, pr_ok, q - 1)
                        met(pe, prT_a, q - 1)
                        met(pe, prT_v, q - 1)
                        met(pe, qkT_ok, q)
                        for j in range(4):
                            for k, bt in enumerate((bth, btl)):
                                pe.matmul(bank(j)[:, 0:256], ident16[:], bt[:, kind, j].rearrange("q g m -> q (g m)"),
                                          start=(k == 0), stop=False, skip_group_check=True)
                        for g in range(4):
                            for w in range(2):
                                for j in range(4):
                                    i = pe.matmul(bank(j)[64 * w:64 * w + 64, 64 * g:64 * g + 64],
                                                  qkT[32 * j:32 * j + 32, q.p % 2, 0, g, 64 * w:64 * w + 64],
                                                  qkT[32 * j:32 * j + 32, q.p % 2, 1, g, 64 * w:64 * w + 64],
                                                  start=False, stop=False, skip_group_check=True)
                        i.then_inc(s_ps.sem, 1)

                    def hidden(s, f):
                        q0 = hidden_of(s)
                        if q0 is None or not q0.real():
                            return
                        if f == 0:
                            met(pe, x1T_ok, q0 + 3)
                            met(pe, z_ok, q0 - 1)
                        met(pe, gl_ok, q0 + (f - 1))
                        pe.matmul(bank(7), f1T[:, f * P:(f + 1) * P], x1T[:, q0.p // 4, :], start=True, stop=True)\
                            .then_inc(h_ps.sem, 1)

                    def slot(s):
                        if s.real():
                            met(pe, mx_ok, s)
                            met(pe, qk_ok, s + 1)
                            met(pe, y_ok, s - 2)
                            pe.transpose(bank(5)[0:NH, 384:512], mx[:], ident[:]).then_inc(mT_ps.sem, 1)
                        todo = [q for q in outputs_of(s) if q.real()]
                        for n, q in enumerate(todo):
                            k = q.p % 4
                            if k == 0:
                                met(pe, gl_ok, q + 3)
                            elif n == 0:
                                met(pe, z_ok, q - 1)
                            for f in range(FC):
                                i = pe.matmul(bank(7)[:, (k % 2 if k < 2 else 0) * C:(k % 2 if k < 2 else 0) * C + C],
                                              gl[:, f, k * P:(k + 1) * P], f2T[:, f, :], start=(f == 0), stop=(f == FC - 1))
                            i.then_inc(m_ps.sem, 1)
                        if s.real():
                            met(pe, mT_ok, s)
                            for j in range(4):
                                i = pe.matmul(bank(j)[:, 0:256], mT[:], sel[:, 256 * j:256 * j + 256],
                                              start=False, stop=True, skip_group_check=True)
                            i.then_inc(sm_ps.sem, 1)
                        q = s + 2
                        if q.real():
                            landed(pe, q)
                            met(pe, qk_ok, q - 1)
                            met(pe, y_ok, q - 4)
                            pe.transpose(bank(5)[:, 0:P], xw[:, q.p, :], ident[:]).then_inc(xT_ps.sem, 1)
                        q = s + 1
                        if q.real():
                            met(pe, x1T_ok, q - 4)
                            met(pe, qkT_ok, q - 1)
                            for w in range(2):
                                i = pe.matmul(bank(6)[:, C * w:C * w + C], xT[:, q.p % 2, P * w:P * w + P], wqkT[:, 2 * C:3 * C],
                                              start=True, stop=True)
                            i.then_inc(v_ps.sem, 1)
                        q = s + 2
                        if q.real():
                            met(pe, xT_ok, q)
                            pe.matmul(bank(5)[:, P:P + 2 * C], xT[:, q.p % 2, 64:64 + P], wqkT[:, 0:2 * C], start=True, stop=True)\
                                .then_inc(qk_ps.sem, 1)
                        if s.real():
                            met(pe, pr_ok, s)
                            for k in range(8):
                                i = pe.transpose(bank(k // 2)[:, 256 + (k % 2) * P:256 + (k % 2 + 1) * P],
                                                 pr[:, s.p % 2, 2 * k:2 * k + 2, :].rearrange("q h m -> q (h m)"), ident[:])
                            i.then_inc(prT_ps.sem, 1)
                        q = s + 1
                        if q.real():
                            met(pe, hi_ok, q, 2)
                            met(pe, lo_ok, q, 2)
                            met(pe, v_ok, q)
                            dst = bank(6).bitcast(F16)
                            for a in range(2):
                                for g in range(4):
                                    i = pe.transpose(dst[:, (4 * a + g) * P:(4 * a + g + 1) * P],
                                                     split[:, q.p % 2, a, 4 * g:4 * g + 4].rearrange("q h s d -> q (h s d)"),
                                                     ident16[:])
                            i.then_inc(qkT_ps.sem, 1)
                        q = s - 1
                        if q.real():
                            met(pe, on_ok, q)
                            met(pe, y_ok, q - 1)
                            met(pe, qk_ok, q + 3)
                            met(pe, mT_ok, q + 1)
                            pe.transpose(bank(5)[:, 384:512], on[:, q.p % 2, :], ident[:]).then_inc(onT_ps.sem, 1)
                        hidden(s, 0)
                        if s.real():
                            met(pe, prT_a, s)
                            met(pe, prT_v, s)
                            met(pe, on_ok, s - 1)
                            for k in range(8):
                                j, t = k // 2, k % 2
                                for w in range(2):
                                    o = bank(4)[64 * w:64 * w + 64, 0:NH * (HD + 1)]\
                                        .rearrange("q (t k j d) -> q t k j d", t=2, k=2, j=4)
                                    v = vd[:, s.p % 2, w].rearrange("q (t k j) d -> q t k j d", t=2, k=2)
                                    i = pe.matmul(o[:, t, :, j, :], prT[:, s.p % 2, k, 64 * w:64 * w + 64], v[:, t, :, j, :],
                                                  start=True, stop=True)
                            i.then_inc(o_ps.sem, 1)
                        q = s - 1
                        if q.real():
                            met(pe, onT_ok, q)
                            pe.matmul(bank(5)[:, P:2 * P], onT[:, q.p % 2, :], projT[:], start=True, stop=True)\
                                .then_inc(pj_ps.sem, 1)
                        hidden(s, 1)
                        scores(s + 1)
                        q = s - 2
                        if q.real():
                            met(pe, x1_ok, q)
                            met(pe, x1T_ok, q - 1)
                            met(pe, qkT_ok, q + 3)
                            pe.transpose(bank(6)[:, 0:P], x1[:, q.p, :], ident[:]).then_inc(x1T_ps.sem, 1)
                        hidden(s, 2)
                        hidden(s, 3)

                    slots(pe, slot)

        def phase_landmarks(lnT, klA, xA, xTA, yA, stR, stC):
            assert NB % 2 == 0
            TURNS = NB // 2
            with ExitStack() as c1:
                def sb(name, shape, dt=F32):
                    return c1.enter_context(nc.sbuf_tensor(name, shape, dt))

                t_in = sb("l_t", [P, NP, C])
                st = sb("l_st", [P, NP, 6])
                mv = sb("l_mv", [P, NP, 2])
                rstd = sb("l_rstd", [P, NP])
                lt = sb("l_lt", [P, T])
                lbar = sb("l_bar", [P, LM])
                kl = sb("l_kl", [P, LM])
                qlm = [sb(f"l_qlm{k}", [P, AH, LM]) for k in range(2)]
                kT = [sb(f"l_kT{k}", [P, T]) for k in range(2)]
                v = [sb(f"l_v{k}", [P, NP, C]) for k in range(2)]
                e2 = sb("l_e2", [P, 4, LM])
                m2 = sb("l_m2", [P, 4])
                r2 = sb("l_r2", [P, 4])
                m3 = sb("l_m3", [P, 4])
                n3 = sb("l_n3", [P, 4])
                sum3 = sb("l_sum3", [P, 4])
                r3 = sb("l_r3", [P, 4])
                p3 = sb("l_p3", [P, 2, T])
                p3T = sb("l_p3T", [P, NP, P])

                t_land = signal("l_t_land", 1, 16)
                st_ok, mv_ok, xn_ok = (signal("l_" + k, NP) for k in ("st_ok", "mv_ok", "xn_ok"))
                var_ok, rstd_ok, lnT_ok, kl_ps, s2_ps, d2_ok, e2_ok, m2_ok, x_ok, xT_ps, xT_ok, xkeep_ok = (
                    signal("l_" + k, 1) for k in ("var_ok rstd_ok lnT_ok kl_ps s2_ps d2_ok e2_ok m2_ok x_ok xT_ps xT_ok "
                                                  "xkeep_ok").split())
                lt_ps, lt_ok, kT_ps, kT_ok, v_ps, v_ok, bar_ok, r2_ok = (
                    signal("l_" + k, 2) for k in "lt_ps lt_ok kT_ps kT_ok v_ps v_ok bar_ok r2_ok".split())
                kl_ok = signal("l_kl_ok", 3)
                s3_ps, m3_ok, n3_ok, p3_ok, p3T_a, p3T_v, y_ps, r3_ok = (
                    signal("l_" + k, 1) for k in "s3_ps m3_ok n3_ok p3_ok p3T_a p3T_v y_ps r3_ok".split())
                p3T_ps, y_ok = signal("l_p3T_ps", 2), signal("l_y_ok", 2)

                class Step:

                    def __init__(self, g, k):
                        self.g, self.k = (g + k // 8 if k // 8 or isinstance(g, int) else g), k % 8
                        self.h = self.k % 4
                        self.odd = self.k // 4

                    def real(self):
                        return not isinstance(self.g, int) or 0 <= self.g < TURNS

                    def __add__(self, d):
                        return Step(self.g, self.k + d)

                    def __sub__(self, d):
                        return self + -d

                    def image(self):
                        return self.g * 2 + self.odd

                def met(eng, s, q, n=1):
                    if q.real():
                        eng.wait_ge(s.sem, (s.per * s.by * 8) * q.g + s.by * (s.per * q.k + n))

                def known(eng, s, q, n=1):
                    if q.real():
                        eng.wait_ge(s.sem, (s.per * s.by * 2) * q.g + s.by * (s.per * q.odd + n))

                def steps(eng, body):
                    for k in range(-8, 8):
                        body(Step(0, k))
                    if TURNS > 2:
                        with eng.Fori(1, TURNS - 1) as g:
                            for k in range(8):
                                body(Step(g, k))
                    for k in range(8 if TURNS > 1 else 0):
                        body(Step(TURNS - 1, k))

                def stages(j):
                    x = j + 6
                    return x, x - 4, x + 4, x.h

                with nc.Block() as block:
                    @block.sync
                    def _(sp):
                        sp.dma_start(t_in[:], mid[0].rearrange("(t p) c -> p t c", p=P)).then_inc(t_land.sem, 16)
                        with sp.Fori(1, NB) as b:
                            sp.wait_ge(lt_ps.sem, lt_ps.at(b, 0))
                            apart(sp)
                            sp.dma_start(t_in[:], mid[b].rearrange("(t p) c -> p t c", p=P)).then_inc(t_land.sem, 16)

                    @block.gpsimd
                    def _(gp):
                        def step(j):
                            x, y, z, stage = stages(j)
                            if stage == 0 and y.real():
                                known(gp, x_ok, y)
                                gp.tensor_copy(xA[:, y.image(), :], e2[:].rearrange("p h j -> p (h j)"))\
                                    .then_inc(xkeep_ok.sem, 1)
                            if stage == 1 and x.real():
                                known(gp, lt_ok, x, 2)
                                gp.tensor_copy(lnT[:, x.image(), :], lt[:]).then_inc(lnT_ok.sem, 1)
                            if stage == 2 and z.real():
                                known(gp, var_ok, z)
                                gp.tensor_tensor(rstd[:], rstd[:], nhalf[:, 0:NP], ALU.pow).then_inc(rstd_ok.sem, 1)

                        steps(gp, step)

                    @block.scalar
                    def _(ac):
                        def step(j):
                            x, y, z, stage = stages(j)
                            if j.real():
                                met(ac, p3T_ps, j, 1)
                                met(ac, y_ps, j - 1)
                                ac.activation(p3T[:, 0:4, :].rearrange("p a c -> p (a c)"), bank(4), ACT.Copy)\
                                    .then_inc(p3T_a.sem, 1)
                            q = j + 1
                            if q.real():
                                met(ac, n3_ok, q)
                                met(ac, p3T_ps, q - 2, 2)
                                ac.activation(p3[:, q.k % 2, :], banks(2 * (q.k % 2), 2), ACT.Exp, bias=n3[:, q.h:q.h + 1],
                                              accum_out=sum3[:, q.h:q.h + 1]).then_inc(p3_ok.sem, 1)
                            if stage == 0 and y.real():
                                known(ac, d2_ok, y)
                                ac.activation(e2[:], e2[:], ACT.Exp).then_inc(e2_ok.sem, 1)
                            if stage == 0 and x.real():
                                known(ac, lnT_ok, x - 4)
                                known(ac, v_ps, x - 4, 2)
                                for u in range(2):
                                    known(ac, lt_ps, x, u + 1)
                                    ac.activation(lt[:, 512 * u:512 * u + 512], bank(7), ACT.Copy).then_inc(lt_ok.sem, 1)
                            if stage in (1, 2) and x.real():
                                u = stage - 1
                                known(ac, kT_ps, x, u + 1)
                                met(ac, s3_ps, j)
                                ac.activation(kT[x.odd][:, 512 * u:512 * u + 512], bank(7), ACT.Copy).then_inc(kT_ok.sem, 1)
                            if stage == 1 and y.real():
                                known(ac, xT_ps, y)
                                ac.activation(xTA[:, y.image(), :], bank(7)[0:LM, :], ACT.Copy).then_inc(xT_ok.sem, 1)

                        steps(ac, step)

                    @block.vector
                    def _(ve):
                        def step(j):
                            x, y, z, stage = stages(j)
                            if j.real():
                                met(ve, p3T_ps, j, 2)
                                met(ve, y_ps, j - 1)
                                ve.tensor_copy(p3T[:, 4:8, :].rearrange("p a c -> p (a c)"), bank(5)).then_inc(p3T_v.sem, 1)
                            if stage == 2 and x.real():
                                known(ve, kl_ps, x)
                                ve.tensor_copy(kl[:], bank(7)[:, 0:LM]).then_inc(kl_ok.sem, 1)
                                ve.tensor_copy(klA[:, x.image(), :], bank(7)[:, 0:LM]).then_inc(kl_ok.sem, 1)
                                ve.tensor_tensor(qlm[x.odd][:], bank(7)[:, LM:2 * LM].unsqueeze(1).to_broadcast([P, AH, LM]),
                                                 headmask[:].unsqueeze(2).to_broadcast([P, AH, LM]), ALU.mult)\
                                    .then_inc(kl_ok.sem, 1)
                            if stage == 3 and x.real():
                                known(ve, s2_ps, x)
                                known(ve, xkeep_ok, x - 4)
                                s2 = bank(7)[:, 0:4 * LM].rearrange("p (h j) -> p h j", h=4)
                                ve.tensor_reduce(m2[:], s2, X, ALU.max).then_inc(m2_ok.sem, 1)
                                known(ve, m2_ok, x)
                                ve.tensor_tensor(e2[:], s2, m2[:].unsqueeze(2).to_broadcast([P, 4, LM]), ALU.subtract)\
                                    .then_inc(d2_ok.sem, 1)
                            q = j + 2
                            if q.real():
                                met(ve, s3_ps, q)
                                ve.tensor_reduce(m3[:, q.h:q.h + 1], banks(2 * (q.k % 2), 2), X, ALU.max).then_inc(m3_ok.sem, 1)
                                met(ve, m3_ok, q)
                                ve.tensor_scalar(n3[:, q.h:q.h + 1], m3[:, q.h:q.h + 1], -1.0, None, ALU.mult)\
                                    .then_inc(n3_ok.sem, 1)

                            def value_rows(u):
                                known(ve, v_ps, x, u + 1)
                                ve.tensor_copy(v[x.odd][:, 4 * u:4 * u + 4, :].rearrange("p t c -> p (t c)"), bank(7))\
                                    .then_inc(v_ok.sem, 1)

                            if stage == 3 and x.real():
                                value_rows(0)
                            if stage == 3 and z.real():
                                known(ve, rstd_ok, z)
                                for t in range(NP):
                                    ve.tensor_scalar(t_in[:, t, :], t_in[:, t, :], mv[:, t, 0:1], rstd[:, t:t + 1],
                                                     ALU.subtract, ALU.mult).then_inc(xn_ok.sem, 1)
                            if stage == 0 and y.real():
                                known(ve, e2_ok, y)
                                ve.tensor_reduce(r2[:], e2[:], X, ALU.add).then_inc(r2_ok.sem, 1)
                                known(ve, r2_ok, y, 1)
                                ve.reciprocal(r2[:], r2[:]).then_inc(r2_ok.sem, 1)
                                known(ve, r2_ok, y, 2)
                                ve.tensor_tensor(e2[:], e2[:], r2[:].unsqueeze(2).to_broadcast([P, 4, LM]), ALU.mult)\
                                    .then_inc(x_ok.sem, 1)
                                known(ve, x_ok, y)
                                ve.tensor_reduce(stR[:, y.image(), :], e2[:], X, ALU.add)
                            if stage == 1 and x.real():
                                known(ve, lt_ok, x, 2)
                                ve.tensor_reduce(lbar[:], lt[:].rearrange("p (l s) -> p l s", s=SEG), X, ALU.add)\
                                    .then_inc(bar_ok.sem, 1)
                                known(ve, bar_ok, x, 1)
                                ve.tensor_scalar(lbar[:], lbar[:], 1.0 / SEG, None, ALU.mult).then_inc(bar_ok.sem, 1)
                            if stage == 2 and y.real():
                                known(ve, xT_ok, y)
                                ve.tensor_reduce(stC[:, y.image(), :], xTA[:, y.image(), :].rearrange("p (h i) -> p h i", h=AH), X, ALU.add)
                            if stage == 2 and z.real():
                                known(ve, t_land, z)
                                for t in range(NP):
                                    ve.bn_stats(st[:, t, :], t_in[:, t, :]).then_inc(st_ok.sem, 1)
                                for t in range(NP):
                                    known(ve, st_ok, z, t + 1)
                                    apart(ve)
                                    ve.bn_aggr(mv[:, t, :], st[:, t, :]).then_inc(mv_ok.sem, 1)
                                known(ve, mv_ok, z, NP)
                                ve.tensor_scalar(rstd[:], mv[:, :, 1], 1e-5, None, ALU.add).then_inc(var_ok.sem, 1)
                            if j.real():
                                met(ve, p3_ok, j)
                                ve.reciprocal(r3[:, j.h:j.h + 1], sum3[:, j.h:j.h + 1]).then_inc(r3_ok.sem, 1)
                                met(ve, r3_ok, j)
                                met(ve, y_ps, j)
                                for k in range(2):
                                    q = slice(64 * k, 64 * k + 64)
                                    ve.tensor_scalar(yA[q, j.image(), AD * j.h:AD * j.h + AD],
                                                     bank(6)[q, 32 * j.h + AD * k:32 * j.h + AD * k + AD],
                                                     r3[q, j.h:j.h + 1], None, ALU.mult).then_inc(y_ok.sem, 1)
                            if stage == 3 and x.real():
                                value_rows(1)

                        steps(ve, step)

                    @block.tensor
                    def _(pe):
                        def step(j):
                            x, y, z, stage = stages(j)

                            def channels_first(u):
                                for t in range(4 * u, 4 * u + 4):
                                    known(pe, xn_ok, x, t + 1)
                                    i = pe.transpose(bank(7)[:, (t % 4) * P:(t % 4 + 1) * P], t_in[:, t, :], ident[:])
                                i.then_inc(lt_ps.sem, 1)

                            def keys(u):
                                pe.matmul(bank(7), wqkv2[:, C:2 * C], lt[:, 512 * u:512 * u + 512], start=True, stop=True)\
                                    .then_inc(kT_ps.sem, 1)

                            def values(u):
                                for t in range(4 * u, 4 * u + 4):
                                    i = pe.matmul(bank(7)[:, (t % 4) * C:(t % 4 + 1) * C], lt[:, t * P:(t + 1) * P],
                                                  wqkv2[:, 2 * C:3 * C], start=True, stop=True)
                                i.then_inc(v_ps.sem, 1)

                            if j.real():
                                met(pe, p3_ok, j)
                                met(pe, p3T_a, j - 1)
                                met(pe, p3T_v, j - 1)
                                for t in range(NP):
                                    i = pe.transpose(bank(4 + t // 4)[:, (t % 4) * P:(t % 4 + 1) * P],
                                                     p3[:, j.k % 2, t * P:(t + 1) * P], ident[:])
                                    if t % 4 == 3:
                                        i.then_inc(p3T_ps.sem, 1)
                            if stage == 0 and x.real():
                                known(pe, v_ok, x - 4, 2)
                                channels_first(0)
                            if stage == 1 and x.real():
                                known(pe, lt_ok, x, 2)
                                keys(0)
                            if stage == 2 and x.real():
                                known(pe, bar_ok, x, 2)
                                known(pe, kT_ok, x, 1)
                                known(pe, xT_ok, y)
                                pe.matmul(bank(7)[:, 0:LM], wqkv2[:, C:2 * C], lbar[:], start=True, stop=True)
                                pe.matmul(bank(7)[:, LM:2 * LM], wqkv2[:, 0:C], lbar[:], start=True, stop=True)\
                                    .then_inc(kl_ps.sem, 1)
                            if stage == 3 and x.real():
                                known(pe, kT_ok, x, 2)
                                for h in range(4):
                                    i = pe.matmul(bank(7)[:, h * LM:(h + 1) * LM], qlm[x.odd][:, 2 * h:2 * h + 2, :]
                                                  .rearrange("p a l -> p (a l)"), kl[:], start=True, stop=True)
                                i.then_inc(s2_ps.sem, 1)
                            q = j + 2
                            if q.real():
                                if q.h == 0:
                                    known(pe, kT_ok, q, 2)
                                    known(pe, kl_ok, q, 3)
                                met(pe, p3_ok, j)
                                for u in range(2):
                                    i = pe.matmul(bank(2 * (q.k % 2) + u), qlm[q.odd][:, 2 * q.h:2 * q.h + 2, :]
                                                  .rearrange("p a l -> p (a l)"),
                                                  kT[q.odd][:, 512 * u:512 * u + 512], start=True, stop=True)
                                i.then_inc(s3_ps.sem, 1)
                            if stage == 0 and x.real():
                                known(pe, lt_ok, x, 1)
                                channels_first(1)
                            if stage == 1 and y.real():
                                known(pe, v_ok, y, 2)
                                known(pe, kT_ok, x, 1)
                                known(pe, x_ok, y)
                                apart(pe)
                                for h in range(4):
                                    i = pe.transpose(bank(7)[0:LM, h * P:(h + 1) * P], e2[:, h, :], ident[:])
                                i.then_inc(xT_ps.sem, 1)
                            if stage == 2 and x.real():
                                known(pe, kl_ok, x, 3)
                                keys(1)
                            if stage == 3 and x.real():
                                known(pe, d2_ok, x)
                                values(0)
                            if j.real():
                                met(pe, p3T_a, j)
                                met(pe, p3T_v, j)
                                met(pe, y_ok, j - 1, 2)
                                for t in range(NP):
                                    i = pe.matmul(bank(6)[:, 32 * j.h:32 * j.h + 32], p3T[:, t, :],
                                                  v[j.odd][:, t, 32 * j.h:32 * j.h + 32], start=(t == 0), stop=(t == NP - 1))
                                i.then_inc(y_ps.sem, 1)
                            if stage == 3 and x.real():
                                known(pe, v_ok, x, 1)
                                values(1)

                        steps(pe, step)

        def phase_pinv(xA, xTA, yA, zA, stR, stC):
            G = min(4, NB)
            with ExitStack() as c1:
                def sb(name, shape, dt=F32):
                    return c1.enter_context(nc.sbuf_tensor(name, shape, dt))

                i64 = sb("p_i64", [P, 3, LM])
                mxs = sb("p_mx", [P, 2])
                mrow = sb("p_mrow", [1, 4])
                cc = sb("p_c", [P, 1])
                xts = sb("p_xts", [LM, G, 4 * P])
                xs = sb("p_xs", [P, G, 4 * LM])
                ay = sb("p_ay", [P, G, 4, LM + AD])
                tm = sb("p_t", [P, G, 4, LM])

                s_i = sem("p_s_i")
                s_ik = sem("p_s_ik")
                s_m = sem("p_s_m")
                s_mt = sem("p_s_mt")
                s_row = sem("p_s_row")
                s_cb = sem("p_s_cb")
                s_c = sem("p_s_c")
                xt_in, x_in, y_in = signal("p_xt_in", G), signal("p_x_in", G), signal("p_y_in", G)
                prod = signal("p_prod", G * (3 * ITERS + 2))
                a_ok = signal("p_a_ok", G * (ITERS + 1))
                t_ok = signal("p_t_ok", G * 3 * ITERS)
                z_ok = signal("p_z_ok", G)

                GROUPS = NB // G
                first = lambda g: isinstance(g, int) and g == 0
                last = lambda g: isinstance(g, int) and g == GROUPS - 1

                def groups(eng, body):
                    body(0)
                    if GROUPS > 2:
                        with eng.Fori(1, GROUPS - 1) as g:
                            body(g)
                    if GROUPS > 1:
                        body(GROUPS - 1)

                def slot(n, i):
                    return (n % 2) * 4 + i

                with nc.Block() as block:
                    @block.sync
                    def _(sp):
                        sp.dma_start(i64[:, 0, :], A["i64"]).then_inc(s_i, 16)

                    @block.gpsimd
                    def _(gp):
                        def group(g):
                            for i in range(G):
                                if not first(g):
                                    gp.wait_ge(z_ok.sem, z_ok.at(g - 1, i + 1))
                                gp.tensor_copy(ay[:, i, :, LM:LM + AD],
                                               yA[:, g * G + i, :].rearrange("p (h d) -> p h d", h=4)).then_inc(y_in.sem, 1)
                                gp.tensor_copy(xs[:, i, :], xA[:, g * G + i, :]).then_inc(x_in.sem, 1)

                        groups(gp, group)

                    @block.scalar
                    def _(ac):
                        def bring(g):
                            for i in range(G):
                                if not first(g):
                                    ac.wait_ge(prod.sem, prod.at(g - 1, i + 1))
                                ac.activation(xts[:, i, :], xTA[:, g * G + i, :], ACT.Copy).then_inc(xt_in.sem, 1)

                        def group(g):
                            if not last(g):
                                bring(g + 1)

                        bring(0)
                        groups(ac, group)

                    @block.vector
                    def _(ve):
                        ve.wait_ge(s_i, 16)
                        ve.tensor_scalar(i64[:, 1, :], i64[:, 0, :], 15.0, None, ALU.mult).then_inc(s_ik, 1)
                        ve.tensor_scalar(i64[:, 2, :], i64[:, 0, :], 3.25, None, ALU.mult).then_inc(s_ik, 1)
                        ve.wait_ge(s_ik, 2)
                        ve.tensor_scalar(i64[:, 0, :], i64[:, 0, :], 7.0, None, ALU.mult).then_inc(s_ik, 1)
                        ve.tensor_reduce(mxs[:, 0:1], stR[:].rearrange("p b h -> p (b h)"), X, ALU.max).then_inc(s_m, 1)
                        ve.tensor_reduce(mxs[0:LM, 1:2], stC[:].rearrange("p b h -> p (b h)"), X, ALU.max).then_inc(s_m, 1)
                        ve.wait_ge(s_mt, 1)
                        ve.tensor_reduce(mrow[:, 0:1], bank(0)[0:1, 0:P], X, ALU.max).then_inc(s_row, 1)
                        ve.tensor_reduce(mrow[:, 1:2], bank(0)[0:1, P:P + LM], X, ALU.max).then_inc(s_row, 1)
                        ve.wait_ge(s_row, 2)
                        ve.tensor_tensor(mrow[:, 2:3], mrow[:, 0:1], mrow[:, 1:2], ALU.mult).then_inc(s_row, 1)
                        ve.wait_ge(s_row, 3)
                        ve.reciprocal(mrow[:, 3:4], mrow[:, 2:3]).then_inc(s_row, 1)
                        ve.wait_ge(s_cb, 1)
                        ve.tensor_copy(cc[:], bank(1)[:, 0:1]).then_inc(s_c, 1)
                        ve.wait_ge(s_c, 1)
                        ve.wait_ge(s_ik, 3)
                        def group(g):
                            def ident_minus(i, k, n):
                                ps = bank(slot(n, i))[:, 0:4 * (LM + AD)].rearrange("p (h j) -> p h j", h=4)[:, :, 0:LM]
                                eye = i64[:, k, :].unsqueeze(1).to_broadcast([P, 4, LM])
                                if k == 2:
                                    ve.scalar_tensor_tensor(out=tm[:, i], in0=ps, scalar=-0.25, in1=eye, op0=ALU.mult,
                                                            op1=ALU.add).then_inc(t_ok.sem, 1)
                                else:
                                    ve.tensor_tensor(tm[:, i], eye, ps, ALU.subtract).then_inc(t_ok.sem, 1)

                            for i in range(G):
                                ve.wait_ge(prod.sem, prod.at(g, i + 1))
                                ps = bank(slot(0, i))[:, 0:4 * (LM + AD)].rearrange("p (h j) -> p h j", h=4)[:, :, 0:LM]
                                ve.tensor_scalar(ay[:, i, :, 0:LM], ps, cc[:, 0:1], None, ALU.mult).then_inc(a_ok.sem, 1)
                            for i in range(G):
                                ve.wait_ge(a_ok.sem, a_ok.at(g, i + 1))
                                ve.tensor_tensor(tm[:, i], i64[:, 0, :].unsqueeze(1).to_broadcast([P, 4, LM]),
                                                 ay[:, i, :, 0:LM], ALU.subtract).then_inc(t_ok.sem, 1)
                            n = 1
                            for it in range(ITERS):
                                for k in (1, 2, 0):
                                    for i in range(G):
                                        ve.wait_ge(prod.sem, prod.at(g, G * n + i + 1))
                                        if k:
                                            ident_minus(i, k, n)
                                        else:
                                            ve.tensor_copy(ay[:, i], bank(slot(n, i))[:, 0:4 * (LM + AD)]
                                                           .rearrange("p (h j) -> p h j", h=4)).then_inc(a_ok.sem, 1)
                                            if it < ITERS - 1:
                                                ident_minus(i, 0, n)
                                    n += 1
                            for i in range(G):
                                ve.wait_ge(prod.sem, prod.at(g, G * n + i + 1))
                                ve.tensor_scalar(zA[:, g * G + i, :], bank(slot(n, i))[:, 0:4 * AD], cc[:, 0:1], None,
                                                 ALU.mult).then_inc(z_ok.sem, 1)

                        groups(ve, group)

                    @block.tensor
                    def _(pe):
                        pe.wait_ge(s_m, 2)
                        pe.transpose(bank(0)[0:1, 0:P], mxs[:, 0:1], ident[:])
                        pe.transpose(bank(0)[0:1, P:P + LM], mxs[0:LM, 1:2], ident[0:LM, 0:LM]).then_inc(s_mt, 1)
                        pe.wait_ge(s_row, 4)
                        pe.matmul(bank(1)[:, 0:1], ones1[:], mrow[:, 3:4], start=True, stop=True).then_inc(s_cb, 1)
                        pe.wait_ge(s_c, 1)
                        def group(g):
                            def each(n, i, width, left, right, stride=LM + AD):
                                for h in range(4):
                                    for k in range(2):
                                        j = pe.matmul(bank(slot(n, i))[64 * k:64 * k + 64, stride * h:stride * h + width],
                                                      left(h, k), right(h, k), start=True, stop=True)
                                j.then_inc(prod.sem, 1)

                            half = lambda k: slice(64 * k, 64 * k + 64)
                            if not first(g):
                                pe.wait_ge(z_ok.sem, z_ok.at(g, 0))
                            for i in range(G):
                                pe.wait_ge(xt_in.sem, xt_in.at(g, i + 1))
                                apart(pe)
                                xt = lambda h, k: xts[:, i, P * h + 64 * k:P * h + 64 * k + 64]
                                each(0, i, LM, xt, xt)
                            n = 1
                            for it in range(ITERS):
                                for k in range(3):
                                    for i in range(G):
                                        if it == 0 and k == 0:
                                            pe.wait_ge(a_ok.sem, a_ok.at(g, i + 1))
                                        pe.wait_ge(t_ok.sem, t_ok.at(g, G * (n - 1) + i + 1))
                                        apart(pe)
                                        if it == 0 and k == 2:
                                            pe.wait_ge(y_in.sem, y_in.at(g, i + 1))
                                            apart(pe)
                                        a = lambda h, q: ay[half(q), i, h, 0:LM]
                                        t = lambda h, q: tm[half(q), i, h, :]
                                        if k < 2:
                                            each(n, i, LM, a, t)
                                        else:
                                            each(n, i, LM + AD, t, lambda h, q: ay[half(q), i, h, :])
                                    n += 1
                            for i in range(G):
                                pe.wait_ge(a_ok.sem, a_ok.at(g, G * ITERS + i + 1))
                                pe.wait_ge(x_in.sem, x_in.at(g, i + 1))
                                apart(pe)
                                each(n, i, AD, lambda h, q: xs[half(q), i, LM * h:LM * h + LM],
                                     lambda h, q: ay[half(q), i, h, LM:LM + AD], stride=AD)

                        groups(pe, group)

        def phase_mix(lnT, klA, zA, cw):
            assert NB % 2 == 0
            TURNS = NB // 2
            with ExitStack() as c1:
                def sb(name, shape, dt=F32):
                    return c1.enter_context(nc.sbuf_tensor(name, shape, dt))

                def two(name, shape):
                    return [sb(f"{name}{k}", shape) for k in range(2)]

                t_in = two("m_t", [P, NP, C])
                lt = two("m_lt", [P, T])
                klm = two("m_klm", [P, AH, LM])
                zd = two("m_zd", [P, 4, 2, AD + 1])
                qT = two("m_qT", [P, T])
                t2 = two("m_t2", [P, NP, C])
                m1 = sb("m_m1", [P, 2, AH])
                e1 = sb("m_e1", [P, 2, AH, LM])
                p1T = sb("m_p1T", [P, 2, 4, P])
                r1 = sb("m_r1", [P, 2, AH])
                on = sb("m_on", [P, 2, C])
                onT = sb("m_onT", [P, 2, P])
                xn = sb("m_xn", [P, NP, C])
                rest = sb("m_rest", [P, NP, C])
                st = sb("m_st", [P, NP, 6])
                mv = sb("m_mv", [P, NP, 2])
                rstd = sb("m_rstd", [P, NP])
                xf = sb("m_xf", [P, T])
                xh = sb("m_xh", [P, T], F16)
                lg = sb("m_lg", [P, NP, NE])
                lm = sb("m_lm", [P, NP])
                gt = sb("m_gt", [P, NP, NE, NE])
                eq = sb("m_eq", [P, NP, NE, NE])
                tri = sb("m_tri", [P, NE, NE])
                bout = sb("m_bout", [P, C])
                b2r = sb("m_b2r", [NE, C])
                b2s = sb("m_b2s", [P, 2, C])
                rank = sb("m_rank", [P, NP, NE])
                cwl = sb("m_cwl", [P, NP, NE])
                cwT = sb("m_cwT", [NE, T])
                x16 = lnT[:].bitcast(F16)

                m_load = sem("m_load")
                b2s_ok = sem("m_b2s_ok")
                zd_set = sem("m_zd_set")
                t_land = signal("m_t_land", 1, 16)
                stored = signal("m_stored", 1, 16)
                lt_in, klm_ok, tb_ok, var_ok, rstd_ok, keep_ok, lo_ok, lg_ps, ex_ok, cwT_ps, b_ps, r_out = (
                    signal("m_" + k, 1) for k in "lt_in klm_ok tb_ok var_ok rstd_ok keep_ok lo_ok lg_ps ex_ok cwT_ps b_ps "
                                                 "r_out".split())
                zd_in, qT_ps, qT_ok, xf_ps, xf_ok, hi_ok, cwT_ok, b_ok = (
                    signal("m_" + k, 2) for k in "zd_in qT_ps qT_ok xf_ps xf_ok hi_ok cwT_ok b_ok".split())
                mv_ok, xn_ok = signal("m_mv_ok", NP), signal("m_xn_ok", NP)
                gate = signal("m_gate", 13)
                s_ps, mx_ok, d_ok, e_ok, eT_ps, eT_ok, o_ps, r_ok, on_ok, onT_ps, onT_ok, w_ps, t2_ok, st_ok = (
                    signal("m_" + k, 1) for k in "s_ps mx_ok d_ok e_ok eT_ps eT_ok o_ps r_ok on_ok onT_ps onT_ok w_ps t2_ok "
                                                 "st_ok".split())

                class Tile:

                    def __init__(self, g, k):
                        self.g, self.k = (g + k // 16 if k // 16 or isinstance(g, int) else g), k % 16
                        self.t = self.k % NP
                        self.odd = self.k // NP
                        self.r = self.k % 2

                    def real(self):
                        return not isinstance(self.g, int) or 0 <= self.g < TURNS

                    def __add__(self, d):
                        return Tile(self.g, self.k + d)

                    def __sub__(self, d):
                        return self + -d

                    def image(self):
                        return self.g * 2 + self.odd

                def met(eng, s, q):
                    if q.real():
                        eng.wait_ge(s.sem, (s.by * 16) * q.g + s.by * (q.k + 1))

                def known(eng, s, q, n=1):
                    if q.real():
                        eng.wait_ge(s.sem, (s.per * s.by * 2) * q.g + s.by * (s.per * q.odd + n))

                def tiles(eng, body):
                    for k in range(-NP, 16 * min(2, TURNS - 1)):
                        body(Tile(0, k))
                    if TURNS > 3:
                        with eng.Fori(2, TURNS - 1) as g:
                            for k in range(16):
                                body(Tile(g, k))
                    for k in range(16):
                        body(Tile(TURNS - 1, k))
                    for k in range(NP + 3):
                        body(Tile(TURNS, k))

                with nc.Block() as block:
                    @block.sync
                    def _(sp):
                        for dst, name in ((tri, "tri"), (bout, "bout"), (b2r, "b2r"), (b2s, "b2s")):
                            sp.dma_start(dst[:], A[name]).then_inc(m_load, 16)

                        def step(j):
                            x, w = j + NP, j - 2 * NP
                            if j.t == 1 and x.real():
                                met(sp, t2_ok, j - 2)
                                apart(sp)
                                known(sp, tb_ok, x - NP)
                                apart(sp)
                                sp.dma_start(t_in[x.odd][:], mid[x.image()].rearrange("(t p) c -> p t c", p=P))\
                                    .then_inc(t_land.sem, 16)
                            if j.t == 2 and w.real():
                                known(sp, r_out, w)
                                apart(sp)
                                sp.dma_start(res[w.image()].rearrange("(t p) c -> p t c", p=P), rest[:])\
                                    .then_inc(stored.sem, 16)

                        tiles(sp, step)
                        sp.wait_ge(stored.sem, stored.at(NB, 0))

                    @block.gpsimd
                    def _(gp):
                        n = 0
                        for k in range(2):
                            gp.memset(zd[k][:], 0.0).then_inc(zd_set, 1)
                            n += 1
                        for k in range(2):
                            for half in range(2):
                                gp.wait_ge(zd_set, n)
                                gp.memset(zd[k][64 * half:64 * half + 64, :, half, AD:AD + 1], 1.0).then_inc(zd_set, 1)
                                n += 1
                        gp.wait_ge(zd_set, n)
                        gp.wait_ge(m_load, 64)
                        gp.wait_ge(b2s_ok, 1)

                        def step(j):
                            x, y, w = j + NP, j - NP, j - 2 * NP
                            if j.t == 0 and y.real():
                                known(gp, var_ok, y)
                                gp.tensor_tensor(rstd[:], rstd[:], nhalf[:, 0:NP], ALU.pow).then_inc(rstd_ok.sem, 1)
                            if j.t == 1 and x.real():
                                met(gp, w_ps, j - 2)
                                for k in range(2):
                                    q = slice(64 * k, 64 * k + 64)
                                    if k:
                                        known(gp, zd_in, x, 1)
                                    gp.tensor_copy(zd[x.odd][q, :, k, 0:AD],
                                                   zA[q, x.image(), :].rearrange("p (h d) -> p h d", h=4)).then_inc(zd_in.sem, 1)
                                known(gp, zd_in, x, 2)
                            if j.t == 2 and w.real():
                                known(gp, b_ok, w, 2)
                                gp.tensor_tensor(rest[:], rest[:], b2s[:, 0, :].unsqueeze(1).to_broadcast([P, NP, C]), ALU.add)\
                                    .then_inc(r_out.sem, 1)
                            if j.t == 3 and x.real():
                                known(gp, t_land, x)
                                gp.tensor_tensor(t_in[x.odd][:], t_in[x.odd][:], bout[:].unsqueeze(1).to_broadcast([P, NP, C]),
                                                 ALU.add).then_inc(tb_ok.sem, 1)
                            if j.t == 5 and y.real():
                                known(gp, hi_ok, y, 2)
                                gp.tensor_copy(x16[:, y.image(), 0:T], xh[:]).then_inc(keep_ok.sem, 1)

                        tiles(gp, step)

                    @block.scalar
                    def _(ac):
                        def step(j):
                            x, y, w = j + NP, j - NP, j - 2 * NP
                            if j.real():
                                met(ac, eT_ps, j)
                                met(ac, o_ps, j - 2)
                                ac.activation(p1T[:, j.r].rearrange("p a c -> p (a c)"), bank(4 + j.r), ACT.Copy)\
                                    .then_inc(eT_ok.sem, 1)
                            q = j - 1
                            if q.real():
                                met(ac, onT_ps, q)
                                met(ac, w_ps, q - 2)
                                ac.activation(onT[:, q.r, :], bank(0)[:, 0:P], ACT.Copy).then_inc(onT_ok.sem, 1)
                            q = j + 1
                            if q.real():
                                met(ac, d_ok, q)
                                ac.activation(e1[:, q.r], e1[:, q.r], ACT.Exp).then_inc(e_ok.sem, 1)
                            if j.t == 0 and w.real():
                                known(ac, cwT_ps, w)
                                for u in range(2):
                                    ac.activation(cwT[:, 512 * u:512 * u + 512], bank((1, 7)[u])[0:NE, :], ACT.Copy)\
                                        .then_inc(cwT_ok.sem, 1)
                            if j.t == 1 and x.real():
                                met(ac, w_ps, j - 2)
                                ac.activation(lt[x.odd][:], lnT[:, x.image(), :], ACT.Copy).then_inc(lt_in.sem, 1)
                            if j.t == 2 and x.real():
                                for u in range(2):
                                    known(ac, qT_ps, x, u + 1)
                                    ac.activation(qT[x.odd][:, 512 * u:512 * u + 512], bank((1, 7)[u]), ACT.Copy)\
                                        .then_inc(qT_ok.sem, 1)
                            if j.t == 3 and y.real():
                                known(ac, lg_ps, y - NP)
                                known(ac, lo_ok, y - NP)
                                known(ac, keep_ok, y - NP)
                                for u in range(2):
                                    known(ac, xf_ps, y, u + 1)
                                    s = slice(512 * u, 512 * u + 512)
                                    ac.activation(xf[:, s], bank((1, 7)[u]), ACT.Copy).then_inc(xf_ok.sem, 1)
                                    ac.activation(xh[:, s], bank((1, 7)[u]), ACT.Copy).then_inc(hi_ok.sem, 1)
                            if j.t == 5 and y.real():
                                known(ac, gate, y, 3)
                                ac.activation(lg[:], lg[:], ACT.Exp).then_inc(ex_ok.sem, 1)

                        tiles(ac, step)

                    @block.vector
                    def _(ve):
                        ve.wait_ge(m_load, 64)
                        ve.tensor_tensor(b2s[:, 0, :], b2s[:, 0, :], b2s[:, 1, :], ALU.add).then_inc(b2s_ok, 1)

                        def soft(q):
                            met(ve, s_ps, q)
                            met(ve, eT_ps, q - 2)
                            s = bank(2 + q.r).rearrange("p (h l) -> p h l", h=AH)
                            ve.tensor_reduce(m1[:, q.r, :], s, X, ALU.max).then_inc(mx_ok.sem, 1)
                            met(ve, mx_ok, q)
                            ve.tensor_tensor(e1[:, q.r], s, m1[:, q.r, :].unsqueeze(2).to_broadcast([P, AH, LM]),
                                             ALU.subtract).then_inc(d_ok.sem, 1)

                        def normed(q):
                            met(ve, o_ps, q)
                            met(ve, onT_ps, q - 2)
                            o = bank(6)[:, 0:AH * (AD + 1)].rearrange("p (h d) -> p h d", h=AH)
                            ve.reciprocal(r1[:, q.r, :], o[:, :, AD]).then_inc(r_ok.sem, 1)
                            met(ve, r_ok, q)
                            ve.tensor_tensor(on[:, q.r, :].rearrange("p (h d) -> p h d", h=AH), o[:, :, 0:AD],
                                             r1[:, q.r, :].unsqueeze(2).to_broadcast([P, AH, AD]), ALU.mult)\
                                .then_inc(on_ok.sem, 1)

                        def add_out(q):
                            met(ve, w_ps, q)
                            known(ve, tb_ok, q)
                            ve.tensor_tensor(t2[q.odd][:, q.t, :], bank(0)[:, C:2 * C], t_in[q.odd][:, q.t, :], ALU.add)\
                                .then_inc(t2_ok.sem, 1)
                            met(ve, t2_ok, q)
                            ve.bn_stats(st[:, q.t, :], t2[q.odd][:, q.t, :]).then_inc(st_ok.sem, 1)

                        def gate_logits(y):
                            known(ve, lg_ps, y)
                            ve.tensor_tensor(lg[:], bank(1)[:, 0:NP * NE].rearrange("p (t e) -> p t e", e=NE),
                                             gb[:].unsqueeze(1).to_broadcast([P, NP, NE]), ALU.add).then_inc(gate.sem, 1)
                            known(ve, gate, y, 1)
                            ve.tensor_reduce(lm[:], lg[:], X, ALU.max).then_inc(gate.sem, 1)
                            known(ve, gate, y, 2)
                            ve.tensor_tensor(lg[:], lg[:], lm[:].unsqueeze(2).to_broadcast([P, NP, NE]), ALU.subtract)\
                                .then_inc(gate.sem, 1)

                        def gate_compare(y):
                            known(ve, ex_ok, y)
                            ve.tensor_reduce(lm[:], lg[:], X, ALU.add).then_inc(gate.sem, 1)
                            known(ve, gate, y, 4)
                            ve.reciprocal(lm[:], lm[:]).then_inc(gate.sem, 1)
                            known(ve, gate, y, 5)
                            ve.tensor_tensor(lg[:], lg[:], lm[:].unsqueeze(2).to_broadcast([P, NP, NE]), ALU.mult)\
                                .then_inc(gate.sem, 1)
                            known(ve, gate, y, 6)
                            for t in range(NP):
                                other = lg[:, t, :].unsqueeze(1).to_broadcast([P, NE, NE])
                                own = lg[:, t, :].unsqueeze(2).to_broadcast([P, NE, NE])
                                i1 = ve.tensor_tensor(eq[:, t], other, own, ALU.is_equal)
                                i2 = ve.tensor_tensor(gt[:, t], other, own, ALU.is_gt)
                            i1.then_inc(gate.sem, 1)
                            i2.then_inc(gate.sem, 1)

                        def gate_choose(y):
                            known(ve, gate, y, 8)
                            ve.tensor_tensor(eq[:].rearrange("p t a b -> p t (a b)"), eq[:].rearrange("p t a b -> p t (a b)"),
                                             tri[:].rearrange("p a b -> p (a b)").unsqueeze(1).to_broadcast([P, NP, NE * NE]),
                                             ALU.mult).then_inc(gate.sem, 1)
                            known(ve, gate, y, 9)
                            flat = lambda a: a[:].rearrange("p t a b -> p (t a b)")
                            ve.tensor_tensor(flat(gt), flat(gt), flat(eq), ALU.add).then_inc(gate.sem, 1)
                            known(ve, gate, y, 10)
                            ve.tensor_reduce(rank[:].rearrange("p t e -> p (t e)"), gt[:].rearrange("p t a b -> p (t a) b"),
                                             X, ALU.add).then_inc(gate.sem, 1)
                            known(ve, gate, y, 11)
                            ve.tensor_scalar(rank[:], rank[:], 2.0, None, ALU.is_lt).then_inc(gate.sem, 1)
                            known(ve, gate, y, 12)
                            known(ve, cwT_ps, y - NP)
                            ve.tensor_tensor(cwl[:], rank[:], lg[:], ALU.mult).then_inc(gate.sem, 1)
                            known(ve, gate, y, 13)
                            ve.tensor_scalar(cw[:, y.image(), :], cwl[:].rearrange("p t e -> p (t e)"), 1.0 / WSCALE, None,
                                             ALU.mult)

                        def step(j):
                            x, y, w = j + NP, j - NP, j - 2 * NP
                            if (j + 1).real():
                                soft(j + 1)
                            if j.t == 1 and w.real():
                                known(ve, b_ps, w)
                                known(ve, stored, w - NP)
                                for u in range(2):
                                    ve.tensor_tensor(rest[:, 4 * u:4 * u + 4, :].rearrange("p t c -> p (t c)"), bank((1, 7)[u]),
                                                     t2[w.odd][:, 4 * u:4 * u + 4, :].rearrange("p t c -> p (t c)"), ALU.add)\
                                        .then_inc(b_ok.sem, 1)
                            if j.real():
                                normed(j)
                            if (j - 1).real():
                                add_out(j - 1)
                            if j.t == 0 and y.real():
                                for t in range(NP):
                                    met(ve, st_ok, y + t)
                                    apart(ve)
                                    ve.bn_aggr(mv[:, t, :], st[:, t, :]).then_inc(mv_ok.sem, 1)
                                known(ve, mv_ok, y, NP)
                                ve.tensor_scalar(rstd[:], mv[:, :, 1], 1e-5, None, ALU.add).then_inc(var_ok.sem, 1)
                            if j.t == 2 and x.real():
                                ve.tensor_tensor(klm[x.odd][:], klA[:, x.image(), :].unsqueeze(1).to_broadcast([P, AH, LM]),
                                                 headmask[:].unsqueeze(2).to_broadcast([P, AH, LM]), ALU.mult)\
                                    .then_inc(klm_ok.sem, 1)
                            if j.t == 2 and y.real():
                                known(ve, rstd_ok, y)
                                for t in range(NP):
                                    ve.tensor_scalar(xn[:, t, :], t2[y.odd][:, t, :], mv[:, t, 0:1], rstd[:, t:t + 1],
                                                     ALU.subtract, ALU.mult).then_inc(xn_ok.sem, 1)
                            if j.t == 5 and y.real():
                                gate_logits(y)
                                known(ve, xf_ok, y, 2)
                                known(ve, hi_ok, y, 2)
                                ve.tensor_tensor(x16[:, y.image(), T:2 * T], xf[:], xh[:], ALU.subtract).then_inc(lo_ok.sem, 1)
                            if j.t == 6 and y.real():
                                gate_compare(y)
                            if j.t == 7 and y.real():
                                gate_choose(y)

                        tiles(ve, step)

                    @block.tensor
                    def _(pe):
                        pe.wait_ge(m_load, 64)

                        def step(j):
                            x, y, w = j + NP, j - NP, j - 2 * NP
                            if j.real():
                                met(pe, e_ok, j)
                                met(pe, eT_ok, j - 2)
                                for h in range(4):
                                    i = pe.transpose(bank(4 + j.r)[:, h * P:(h + 1) * P],
                                                     e1[:, j.r, 2 * h:2 * h + 2, :].rearrange("p a l -> p (a l)"), ident[:])
                                i.then_inc(eT_ps.sem, 1)
                            q = j + 2
                            if q.real():
                                known(pe, qT_ok, q, q.t // 4 + 1)
                                known(pe, klm_ok, q)
                                met(pe, d_ok, j)
                                pe.matmul(bank(2 + q.r), qT[q.odd][:, q.t * P:(q.t + 1) * P],
                                          klm[q.odd][:].rearrange("p h l -> p (h l)"), start=True, stop=True)\
                                    .then_inc(s_ps.sem, 1)
                            q = j - 1
                            if q.real():
                                met(pe, on_ok, q)
                                met(pe, t2_ok, q - 1)
                                pe.transpose(bank(0)[:, 0:P], on[:, q.r, :], ident[:]).then_inc(onT_ps.sem, 1)
                            if j.t == 0 and w.real():
                                known(pe, gate, w, 13)
                                known(pe, hi_ok, w, 2)
                                for t in range(NP):
                                    i = pe.transpose(bank((1, 7)[t // 4])[0:NE, (t % 4) * P:(t % 4 + 1) * P], cwl[:, t, :],
                                                     ident[:])
                                i.then_inc(cwT_ps.sem, 1)

                            def normed_first(u):
                                known(pe, qT_ok, x, u + 1)
                                known(pe, b_ok, w, 2)
                                for t in range(4 * u, 4 * u + 4):
                                    known(pe, xn_ok, y, t + 1)
                                    i = pe.transpose(bank((1, 7)[u])[:, (t % 4) * P:(t % 4 + 1) * P], xn[:, t, :], ident[:])
                                i.then_inc(xf_ps.sem, 1)

                            if j.t == 3 and y.real():
                                normed_first(0)
                            if j.real():
                                met(pe, eT_ok, j)
                                known(pe, zd_in, j, 2)
                                met(pe, on_ok, j - 1)
                                for h in range(4):
                                    n = 2 * (AD + 1)
                                    i = pe.matmul(bank(6)[:, n * h:n * h + n], p1T[:, j.r, h, :],
                                                  zd[j.odd][:, h].rearrange("p a d -> p (a d)"), start=True, stop=True)
                                i.then_inc(o_ps.sem, 1)
                            if q.real():
                                met(pe, onT_ok, q)
                                pe.matmul(bank(0)[:, C:2 * C], onT[:, q.r, :], wout[:], start=True, stop=False)
                                pe.matmul(bank(0)[:, C:2 * C], lt[q.odd][:, q.t * P:(q.t + 1) * P], wvc[:], start=False,
                                          stop=True).then_inc(w_ps.sem, 1)
                            if j.t == 0 and w.real():
                                known(pe, cwT_ok, w, 2)
                                for t in range(NP):
                                    i = pe.matmul(bank((1, 7)[t // 4])[:, (t % 4) * C:(t % 4 + 1) * C], cwT[:, t * P:(t + 1) * P],
                                                  b2r[:], start=True, stop=True)
                                i.then_inc(b_ps.sem, 1)
                            if j.t == 2 and x.real():
                                known(pe, lt_in, x)
                                known(pe, b_ok, w, 2)
                                for u in range(2):
                                    pe.matmul(bank((1, 7)[u]), wqkv2[:, 0:C], lt[x.odd][:, 512 * u:512 * u + 512],
                                              start=True, stop=True).then_inc(qT_ps.sem, 1)
                            if j.t == 3 and y.real():
                                normed_first(1)
                            if j.t == 4 and y.real():
                                known(pe, xf_ok, y, 2)
                                known(pe, hi_ok, y, 1)
                                for t in range(NP):
                                    i = pe.matmul(bank(1)[:, NE * t:NE * t + NE], xf[:, t * P:(t + 1) * P], gw[:],
                                                  start=True, stop=True)
                                i.then_inc(lg_ps.sem, 1)

                        tiles(pe, step)

        def phase_experts(lnT, cw):
            NC = 2 * NX * FC
            with ExitStack() as c1:
                def sb(name, shape, dt=F32):
                    return c1.enter_context(nc.sbuf_tensor(name, shape, dt))

                acc = sb("e_acc", [P, NP, C])
                g32 = sb("e_g32", [P, 4, 512])
                ghi = sb("e_ghi", [P, 4, 512], F16)
                glo = sb("e_glo", [P, 4, 512], F16)
                x16 = lnT[:].bitcast(F16)
                NG = 2 * (NE + 1)

                r_in = signal("e_r_in", 1, 16)
                h_ps = signal("e_h_ps", NC)
                g_ok = signal("e_g_ok", NC)
                ghi_a = signal("e_ghi_a", NC // 2)
                ghi_v = signal("e_ghi_v", NC // 2)
                glo_ok = signal("e_glo_ok", NC)
                y_ps = signal("e_y_ps", NC)
                acc_ok = signal("e_acc_ok", NG)
                out_ok = signal("e_out_ok", 2, 16)

                def images(eng, body):
                    body(0)
                    if NB > 2:
                        with eng.Fori(1, NB - 1) as b:
                            body(b)
                    if NB > 1:
                        body(NB - 1)

                def reached(eng, s, b, n):
                    if not (isinstance(b, int) and s.at(b, n) <= 0):
                        eng.wait_ge(s.sem, s.at(b, n))

                def group(c):
                    u, e = c // (NX * FC), c // FC % NX
                    return u * (NE + 1) + max(e - 1, 0)

                with nc.Block() as block:
                    @block.sync
                    def _(sp):
                        def image(b):
                            reached(sp, out_ok, b, 0)
                            apart(sp)
                            sp.dma_start(acc[:], res[b].rearrange("(t p) c -> p t c", p=P)).then_inc(r_in.sem, 16)
                            for u in range(2):
                                reached(sp, acc_ok, b, (u + 1) * (NE + 1))
                                apart(sp)
                                sp.dma_start(out[b].rearrange("(t p) c -> p t c", p=P)[:, 4 * u:4 * u + 4, :],
                                             acc[:, 4 * u:4 * u + 4, :]).then_inc(out_ok.sem, 16)
                        images(sp, image)
                        sp.wait_ge(out_ok.sem, out_ok.at(NB, 0))

                    @block.scalar
                    def _(ac):
                        def image(b):
                            for c in range(NC):
                                e, f = c // FC % NX, c % FC
                                reached(ac, h_ps, b, c + 1)
                                reached(ac, glo_ok, b, c - 3)
                                ac.activation(g32[:, c % 4, :], bank(c % 4), ACT.Gelu, bias=b1[:, e, f:f + 1],
                                              scale=1.0 / WSCALE).then_inc(g_ok.sem, 1)
                                if f < 2:
                                    reached(ac, y_ps, b, c - 3)
                                    ac.activation(ghi[:, c % 4, :], bank(c % 4), ACT.Gelu, bias=b1[:, e, f:f + 1],
                                                  scale=1.0 / WSCALE).then_inc(ghi_a.sem, 1)

                        images(ac, image)

                    @block.vector
                    def _(ve):
                        def image(b):
                            def add_up(n, b=b):
                                u, e = n // (NE + 1), n % (NE + 1)
                                last = (u * NX + e + 1) * FC + FC
                                reached(ve, y_ps, b, last)
                                bk = bank(4 + n % 2)
                                if e == 0:
                                    if u == 0:
                                        reached(ve, r_in, b, 1)
                                    a = acc[:, 4 * u:4 * u + 4, :].rearrange("p t c -> p (t c)")
                                    ve.scalar_tensor_tensor(out=a, in0=bk, scalar=1.0 / WSCALE, in1=a, op0=ALU.mult,
                                                            op1=ALU.add).then_inc(acc_ok.sem, 1)
                                    return
                                reached(ve, acc_ok, b, n)
                                for t in range(4):
                                    tt = 4 * u + t
                                    i = ve.scalar_tensor_tensor(out=acc[:, tt, :], in0=bk[:, C * t:C * t + C],
                                                                scalar=cw[:, b, tt * NE + e - 1:tt * NE + e],
                                                                in1=acc[:, tt, :], op0=ALU.mult, op1=ALU.add)
                                i.then_inc(acc_ok.sem, 1)

                            for c in range(NC):
                                f = c % FC
                                reached(ve, g_ok, b, c + 1)
                                reached(ve, y_ps, b, c - 3)
                                if f >= 2:
                                    ve.tensor_copy(ghi[:, c % 4, :], g32[:, c % 4, :]).then_inc(ghi_v.sem, 1)
                                    reached(ve, ghi_v, b, 2 * (c // FC) + f - 1)
                                else:
                                    reached(ve, ghi_a, b, 2 * (c // FC) + f + 1)
                                ve.tensor_tensor(glo[:, c % 4, :], g32[:, c % 4, :], ghi[:, c % 4, :], ALU.subtract)\
                                    .then_inc(glo_ok.sem, 1)
                                if f == 3 and c // FC >= 1:
                                    done = c // FC - 1
                                    if done % NX != 0:
                                        add_up(done // NX * (NE + 1) + done % NX - 1)
                                if c == 3 and not (isinstance(b, int) and b == 0):
                                    add_up(NG - 1, b - 1)
                            if isinstance(b, int) and b == NB - 1:
                                add_up(NG - 1)

                        images(ve, image)

                    @block.tensor
                    def _(pe):
                        def image(b):
                            def hidden(c):
                                u, e, f = c // (NX * FC) % 2, c // FC % NX, c % FC
                                reached(pe, g_ok, b, c - 3)
                                if f < 2:
                                    reached(pe, ghi_a, b, 2 * (c // FC - 1) + f + 1)
                                w = slice(f * P, f * P + P)
                                m = b if c < NC else b + 1
                                xhi = x16[:, m, 512 * u:512 * u + 512]
                                xlo = x16[:, m, T + 512 * u:T + 512 * u + 512]
                                pe.matmul(bank(c % 4), w1hi[:, e, w], xhi, start=True, stop=False)
                                pe.matmul(bank(c % 4), w1hi[:, e, w], xlo, start=False, stop=False)
                                pe.matmul(bank(c % 4), w1lo[:, e, w], xhi, start=False, stop=True).then_inc(h_ps.sem, 1)

                            def output(c):
                                e, f = c // FC % NX, c % FC
                                n = group(c)
                                first = f == 0 and e != 1
                                if first:
                                    reached(pe, acc_ok, b, n - 1)
                                reached(pe, glo_ok, b, c + 1)
                                for t in range(4):
                                    o = bank(4 + n % 2)[:, C * t:C * t + C]
                                    s = slice(t * P, t * P + P)
                                    pe.matmul(o, ghi[:, c % 4, s], w2hi[:, e, f, :], start=first and t == 0, stop=False,
                                              skip_group_check=True)
                                    pe.matmul(o, ghi[:, c % 4, s], w2lo[:, e, f, :], start=False, stop=False,
                                              skip_group_check=True)
                                    i = pe.matmul(o, glo[:, c % 4, s], w2hi[:, e, f, :], start=False,
                                                  stop=True, skip_group_check=True)
                                i.then_inc(y_ps.sem, 1)

                            if isinstance(b, int) and b == 0:
                                hidden(0)
                                hidden(1)
                            last = isinstance(b, int) and b == NB - 1
                            for c in range(NC):
                                if c + 2 < NC or not last:
                                    hidden(c + 2)
                                output(c)

                        images(pe, image)

        with ExitStack() as first:
            W = {}
            phase_setup(first, W)
            phase_ends()
            phase_windows(first, W)
            phase_ends()
        lnT = sb("lnT", [P, NB, T])
        klA = sb("klA", [P, NB, LM])
        zA = sb("zA", [P, NB, 4 * AD])
        with ExitStack() as c2:
            def sb2(name, shape):
                return c2.enter_context(nc.sbuf_tensor(name, shape, F32))

            xA = sb2("xA", [P, NB, 4 * LM])
            xTA = sb2("xTA", [LM, NB, 4 * P])
            stR = sb2("stR", [P, NB, 4])
            stC = sb2("stC", [LM, NB, AH])
            phase_landmarks(lnT, klA, xA, xTA, zA, stR, stC)
            phase_ends()
            phase_pinv(xA, xTA, zA, zA, stR, stC)
            phase_ends()
        cw = sb("cw", [P, NB, NP * NE])
        phase_mix(lnT, klA, zA, cw)
        phase_ends()
        phase_experts(lnT, cw)


def host_arrays(inp):
    rel, mask, sel, _, _ = window_constants()
    f = lambda a: np.ascontiguousarray(a)
    rows = lambda a, *s: f(np.broadcast_to(np.reshape(a, (1, *s)), (P, *s)))
    I = {k: np.asarray(v) for k, v in inp.items()}
    L0 = lambda k: I["L0_conv_" + k]
    w1 = np.concatenate([I["L1_ffn_sw1"], I["L1_ffn_rw1"]])
    w2 = np.concatenate([I["L1_ffn_sw2"], I["L1_ffn_rw2"]])
    bb = np.concatenate([I["L1_ffn_sb1"], I["L1_ffn_rb1"]])
    kernel_w = I["L1_attn_conv_w"][:, 0]
    hh, cc = np.meshgrid(np.arange(AH), np.arange(AD), indexing="ij")
    hh, cc = hh.reshape(-1), cc.reshape(-1)
    convT = kernel_w[hh[None, :] - hh[:, None] + 16, cc[None, :] % 2, cc[:, None]]
    convmask = (cc[None, :] // 2 == cc[:, None] // 2).astype(np.float32)
    headmask = np.zeros((P, AH), np.float32)
    headmask[np.arange(P), hh] = 0.25
    i64 = np.concatenate([np.eye(LM, dtype=np.float32)] * 2)
    wqkv2 = I["L1_attn_Wqkv"]
    return {
        "x": f(I["x"]).reshape(-1, T, C),
        "ident": np.eye(P, dtype=np.float32), "ident16": np.eye(P, dtype=np.float16),
        "i64": i64, "tri": rows(np.tril(np.ones((NE, NE), np.float32), -1), NE, NE),
        "wqkv2": f(wqkv2), "wvT": f(wqkv2[:, 2 * C:].T), "wout": f(I["L1_attn_Wout"]),
        "bout": rows(I["L1_attn_bout"], C), "gw": f(I["L1_ffn_gate_w"].T), "gb": rows(I["L1_ffn_gate_b"], NE),
        "b2r": f(I["L1_ffn_rb2"]), "b2s": rows(I["L1_ffn_sb2"], 2, C), "headmask": headmask,
        "b1": f(bb.reshape(NX, FC, P).transpose(2, 0, 1)), "convT": f(convT), "convmask": convmask,
        "w1": f(w1.transpose(2, 0, 1)).reshape(P, NX * F),
        "w2": f(w2.reshape(NX, C, FC, P).transpose(3, 0, 2, 1)).reshape(P, NX * F),
        "wqkT": f(L0("qkv_w").T), "qb": rows(np.concatenate([L0("q_bias"), np.zeros_like(L0("q_bias"))]), 2 * C),
        "projT": f(L0("proj_w").T), "projb": rows(L0("proj_b"), C),
        "vbcol": f(np.broadcast_to(L0("v_bias")[:, None], (C, P))),
        "g1": rows(L0("norm1_g"), C), "be1": rows(L0("norm1_b"), C),
        "g2": rows(L0("norm2_g"), C), "be2": rows(L0("norm2_b"), C),
        "f1T": f(L0("fc1_w").T), "f1b": f(L0("fc1_b").reshape(FC, P).T),
        "f2T": f(L0("fc2_w").T.reshape(FC, P, C).transpose(1, 0, 2)), "f2b": rows(L0("fc2_b"), C),
        "ls": rows(L0("logit_scale").reshape(NH), NH), "cpw1": f(L0("cpb_w1").T), "cpb1": f(L0("cpb_b1")[:, None]),
        "cpw2": f(L0("cpb_w2").T), "rel": rel, "mask": mask, "sel": sel,
    }


def kernel(**inputs):
    import concourse.bacc as bacc
    from concourse.bass_utils import run_bass_kernel_spmd

    nc = bacc.Bacc("TRN2", target_bir_lowering=False, num_devices=1)
    arrays = {f"in_{k}": a for k, a in host_arrays(inputs).items()}
    A = {k[3:]: nc.dram_tensor(k, a.shape, mybir.dt.from_np(a.dtype), kind="ExternalInput").ap()
         for k, a in arrays.items()}
    NB = arrays["in_x"].shape[0]
    out = nc.dram_tensor("out_dram", (NB, T, C), F32, kind="ExternalOutput").ap()
    build(nc, NB, A, out)
    r = run_bass_kernel_spmd(nc, [arrays], core_ids=[0])
    return r.results[0]["out_dram"].reshape(NB, HW, HW, C)
```
